# Optimizing a Trainium2 kernel written in Bass

```python
import numpy as np
import jax
import jax.numpy as jnp

def _softmax(x, axis=-1):
    return jax.nn.softmax(x, axis=axis)

def _gelu(x):
    return jax.nn.gelu(x, approximate=True)

def _silu(x):
    return jax.nn.silu(x)

def _sigmoid(x):
    return jax.nn.sigmoid(x)

def _layernorm(x, axis=-1, eps=1e-05):
    m = jnp.mean(x, axis=axis, keepdims=True)
    v = jnp.var(x, axis=axis, keepdims=True)
    return (x - m) / jnp.sqrt(v + eps)

def _scatter_add(tgt, idx, src, axis=0):
    return tgt.at[idx].add(src)

def _segment_sum(src, seg, n):
    return jax.ops.segment_sum(src, seg, n)
kernel_name = 'mk_seq_preln_d1_jaxref_r4_6bef95'

def setup_inputs(seed: int=0):
    np.random.seed(seed)
    _w = jnp.asarray

    def _L0_attn_setup():
        import jax, jax.numpy as jnp
        import numpy as np
        EMBED_DIM = 256
        NUM_HEADS = 16
        HEAD_DIM = EMBED_DIM // NUM_HEADS
        LAMBDA_ENTANGLE = 0.35
        key = jax.random.key(seed)
        ks = jax.random.split(key, 10)
        B, S, D = (2, 512, EMBED_DIM)
        init = 1.0 / np.sqrt(D)
        x = jax.random.normal(ks[0], (B, S, D), dtype=jnp.float32)
        Wq = jax.random.uniform(ks[1], (D, D), jnp.float32, -init, init)
        bq = jax.random.uniform(ks[2], (D,), jnp.float32, -init, init)
        Wk = jax.random.uniform(ks[3], (D, D), jnp.float32, -init, init)
        bk = jax.random.uniform(ks[4], (D,), jnp.float32, -init, init)
        Wv = jax.random.uniform(ks[5], (D, D), jnp.float32, -init, init)
        bv = jax.random.uniform(ks[6], (D,), jnp.float32, -init, init)
        Wo = jax.random.uniform(ks[7], (D, D), jnp.float32, -init, init)
        bo = jax.random.uniform(ks[8], (D,), jnp.float32, -init, init)
        J_attn = jax.random.normal(ks[9], (NUM_HEADS, HEAD_DIM, HEAD_DIM), dtype=jnp.float32) * 0.02
        lambda_attn = jnp.asarray(LAMBDA_ENTANGLE, dtype=jnp.float32)
        return {'x': x, 'Wq': Wq, 'bq': bq, 'Wk': Wk, 'bk': bk, 'Wv': Wv, 'bv': bv, 'Wo': Wo, 'bo': bo, 'J_attn': J_attn, 'lambda_attn': lambda_attn}
    _L0_attn_in = _L0_attn_setup()

    def _L0_ffn_setup():
        import jax, jax.numpy as jnp
        import numpy as np
        EPS = 1e-05
        LN_EPS = 1e-05
        NUM_EXPERTS = 8
        TOP_K = 2
        HIDDEN = 256
        INTER = 512

        def _swiglu(x, wg, wu, wd):
            return jax.nn.silu(x @ wg) * (x @ wu) @ wd
        key = jax.random.key(seed)
        ks = jax.random.split(key, 10)
        B, S, H, I, E = (8, 1024, HIDDEN, INTER, NUM_EXPERTS)
        std_h = 1.0 / np.sqrt(H)
        std_i = 1.0 / np.sqrt(I)
        return {'x': jax.random.normal(ks[0], (B, S, H), dtype=jnp.float32), 'ln_scale': jnp.ones((H,), dtype=jnp.float32), 'ln_bias': jnp.zeros((H,), dtype=jnp.float32), 'gate_w': jax.random.normal(ks[1], (E, H), dtype=jnp.float32) * 0.01, 'Wg': jax.random.normal(ks[2], (E, H, I), dtype=jnp.float32) * std_h, 'Wu': jax.random.normal(ks[3], (E, H, I), dtype=jnp.float32) * std_h, 'Wd': jax.random.normal(ks[4], (E, I, H), dtype=jnp.float32) * std_i, 'sWg': jax.random.normal(ks[5], (H, I), dtype=jnp.float32) * std_h, 'sWu': jax.random.normal(ks[6], (H, I), dtype=jnp.float32) * std_h, 'sWd': jax.random.normal(ks[7], (I, H), dtype=jnp.float32) * std_i}
    _L0_ffn_in = _L0_ffn_setup()
    _d = {'L0_attn_x': _L0_attn_in['x'], 'L0_attn_Wq': _L0_attn_in['Wq'], 'L0_attn_bq': _L0_attn_in['bq'], 'L0_attn_Wk': _L0_attn_in['Wk'], 'L0_attn_bk': _L0_attn_in['bk'], 'L0_attn_Wv': _L0_attn_in['Wv'], 'L0_attn_bv': _L0_attn_in['bv'], 'L0_attn_Wo': _L0_attn_in['Wo'], 'L0_attn_bo': _L0_attn_in['bo'], 'L0_attn_J_attn': _L0_attn_in['J_attn'], 'L0_attn_lambda_attn': _L0_attn_in['lambda_attn'], 'L0_ffn_ln_scale': _L0_ffn_in['ln_scale'], 'L0_ffn_ln_bias': _L0_ffn_in['ln_bias'], 'L0_ffn_gate_w': _L0_ffn_in['gate_w'], 'L0_ffn_Wg': _L0_ffn_in['Wg'], 'L0_ffn_Wu': _L0_ffn_in['Wu'], 'L0_ffn_Wd': _L0_ffn_in['Wd'], 'L0_ffn_sWg': _L0_ffn_in['sWg'], 'L0_ffn_sWu': _L0_ffn_in['sWu'], 'L0_ffn_sWd': _L0_ffn_in['sWd']}
    _x0 = _d['L0_attn_x']
    _d['L0_attn_x'] = jax.random.normal(jax.random.fold_in(jax.random.key(seed), 1), (16, 512, 256), dtype=_x0.dtype)
    del _x0
    return _d

def reference(L0_attn_x, L0_attn_Wq, L0_attn_bq, L0_attn_Wk, L0_attn_bk, L0_attn_Wv, L0_attn_bv, L0_attn_Wo, L0_attn_bo, L0_attn_J_attn, L0_attn_lambda_attn, L0_ffn_ln_scale, L0_ffn_ln_bias, L0_ffn_gate_w, L0_ffn_Wg, L0_ffn_Wu, L0_ffn_Wd, L0_ffn_sWg, L0_ffn_sWu, L0_ffn_sWd):

    def _L0_attn_ref(x, Wq, bq, Wk, bk, Wv, bv, Wo, bo, J_attn, lambda_attn):
        import jax, jax.numpy as jnp
        import numpy as np
        EMBED_DIM = 256
        NUM_HEADS = 16
        HEAD_DIM = EMBED_DIM // NUM_HEADS
        LAMBDA_ENTANGLE = 0.35
        B, S, D = x.shape
        H, Hd = (NUM_HEADS, HEAD_DIM)
        scale = jnp.sqrt(jnp.asarray(Hd, dtype=x.dtype))

        def heads(W, b):
            y = jnp.einsum('bsd,ed->bse', x, W) + b
            return y.reshape(B, S, H, Hd).transpose(0, 2, 1, 3)
        Q = heads(Wq, bq)
        K = heads(Wk, bk)
        V = heads(Wv, bv)
        scores = jnp.einsum('bhid,bhjd->bhij', Q, K) / scale
        QJ = jnp.einsum('bhid,hde->bhie', jnp.tanh(Q), J_attn)
        delta = jnp.einsum('bhie,bhje->bhij', QJ, jnp.tanh(K))
        scores = scores + lambda_attn * delta
        causal = jnp.triu(jnp.ones((S, S), dtype=bool), k=1)
        scores = jnp.where(causal, -jnp.inf, scores)
        probs = jax.nn.softmax(scores, axis=-1)
        out = jnp.einsum('bhij,bhjd->bhid', probs, V)
        out = out.transpose(0, 2, 1, 3).reshape(B, S, D)
        return jnp.einsum('bsd,ed->bse', out, Wo) + bo

    def _L0_ffn_ref(x, ln_scale, ln_bias, gate_w, Wg, Wu, Wd, sWg, sWu, sWd):
        import jax, jax.numpy as jnp
        import numpy as np
        EPS = 1e-05
        LN_EPS = 1e-05
        NUM_EXPERTS = 8
        TOP_K = 2
        HIDDEN = 256
        INTER = 512

        def _swiglu(x, wg, wu, wd):
            return jax.nn.silu(x @ wg) * (x @ wu) @ wd
        B, S, H = x.shape
        xf = x.reshape(-1, H)
        mu = jnp.mean(xf, axis=-1, keepdims=True)
        var = jnp.var(xf, axis=-1, keepdims=True)
        xn = (xf - mu) * jax.lax.rsqrt(var + LN_EPS) * ln_scale + ln_bias
        logits = xn @ gate_w.T
        probs = jax.nn.softmax(logits, axis=-1)
        tk_probs, tk_idx = jax.lax.top_k(probs, TOP_K)
        tk_probs = tk_probs / (jnp.sum(tk_probs, axis=-1, keepdims=True) + EPS)
        onehot = tk_idx[..., None] == jnp.arange(NUM_EXPERTS)[None, None, :]
        w = jnp.sum(tk_probs[..., None] * onehot.astype(tk_probs.dtype), axis=1)
        out = _swiglu(xf, sWg, sWu, sWd)
        for e in range(NUM_EXPERTS):
            out = out + w[:, e:e + 1] * _swiglu(xf, Wg[e], Wu[e], Wd[e])
        return out.reshape(B, S, H)
    x = L0_attn_x
    x = x + _L0_attn_ref(_layernorm(x, axis=-1), L0_attn_Wq, L0_attn_bq, L0_attn_Wk, L0_attn_bk, L0_attn_Wv, L0_attn_bv, L0_attn_Wo, L0_attn_bo, L0_attn_J_attn, L0_attn_lambda_attn)
    x = x + _L0_ffn_ref(_layernorm(x, axis=-1), L0_ffn_ln_scale, L0_ffn_ln_bias, L0_ffn_gate_w, L0_ffn_Wg, L0_ffn_Wu, L0_ffn_Wd, L0_ffn_sWg, L0_ffn_sWu, L0_ffn_sWd)
    return x

_drawn_inputs = setup_inputs


def setup_inputs(seed=0):
    import zlib

    import numpy as np

    out = dict(_drawn_inputs(seed))
    spreads = {'L0_ffn_ln_scale': (1.0, 0.2), 'L0_ffn_ln_bias': (0.0, 0.1)}
    factors = {'L0_attn_bq': 7.217, 'L0_attn_bk': 200.0, 'L0_attn_J_attn': 21.833}
    for name, (base, spread) in spreads.items():
        noise = np.random.default_rng([zlib.crc32(name.encode()), seed]).standard_normal(out[name].shape)
        drawn = base * np.exp(spread * noise) if base else spread * noise
        out[name] = jnp.asarray(drawn.astype(out[name].dtype))
    for name, factor in factors.items():
        out[name] = (out[name] * factor).astype(out[name].dtype)
    return out
```

```python
import concourse.bass as bass
from concourse import mybir
from contextlib import ExitStack


F32 = mybir.dt.float32
F32R = mybir.dt.float32r
BF16 = mybir.dt.bfloat16
I32 = mybir.dt.int32
ALU = mybir.AluOpType
ACT = mybir.ActivationFunctionType
AX = mybir.AxisListType

P = 128
NB, S, D = 16, 512, 256
H, HD = 16, 16
KT = D // P
TT = S // P
NT = NB * TT
HG = 4
G = H // HG
PG = P // HD
NE, INTER = 8, 512
IT = INTER // P
EPS = 1e-5
MASK = -1e30
NSLOT = 2 * NT + NE - 1
ZR = 3
LEAD = 6
STEPS = G * TT
STACK = 3 * 2 * HD
MROW = STACK
LOADS = 16 * 12
PROLOGUE, TAIL = -1, NB


class Batch:

    def __init__(self, i, off):
        self.i, self.off = i, off
        self.v = off if isinstance(i, int) and i == 0 else i * 2 + off
        self.par = off % 2
        self.fixed = isinstance(i, int)

    def plus(self, k):
        return Batch(self.i, self.off + k)

    def half(self):
        return self.off // 2 if self.fixed else self.i + self.off // 2

    def at_least(self, n):
        return (not self.fixed) or self.off >= n

    def at_most(self, n):
        return (not self.fixed) or self.off <= n


def over_batches(eng, batch):
    batch(Batch(0, PROLOGUE))
    batch(Batch(0, 0))
    with eng.Fori(0, NB // 2 - 1) as i:
        batch(Batch(i, 1))
        batch(Batch(i, 2))
    batch(Batch(0, NB - 1))
    batch(Batch(0, TAIL))


PIECES = [
    (1, 0, "xt", 0, 1), (1, 1, "ot", 3, -1), (1, 1, "xt", 1, 1),
    (2, 0, "mt", 1, 0), (2, 1, "k", 0, 1),
    (3, 0, "k", 1, 1), (3, 1, "q", 0, 1),
    (4, 0, "q", 1, 1), (4, 1, "qj", 0, 1),
    (5, 0, "ot", 0, 0), (5, 1, "qj", 1, 1),
    (6, 0, "mt", 2, 0),
    (7, 0, "v", 0, 1),
    (8, 0, "v", 1, 1),
    (9, 0, "ot", 1, 0), (9, 1, "ont", 0, -1),
    (10, 0, "mt", 3, 0),
    (11, 0, "ont", 1, -1),
    (12, 0, "out", 0, -1),
    (13, 0, "ot", 2, 0), (13, 1, "out", 1, -1),
    (14, 0, "mt", 0, 1),
]
PER_BATCH = {"xt": 2, "k": 2, "q": 2, "qj": 2, "v": 2, "mt": G, "ot": G, "ont": 2, "out": 2}


def piece_exists(b, rel):
    d = b.plus(rel)
    return d.at_least(0) and d.at_most(NB - 1)


def pieces_at(b, n, place):
    found = []
    for at, (step, pl, kind, j, rel) in enumerate(PIECES):
        if step == n and pl == place and piece_exists(b, rel):
            found.append((kind, j, b.plus(rel), piece_before(b, at)))
    return found


def piece_before(b, at):
    for bb, upto in ((b, at), (b.plus(-1), len(PIECES))):
        if bb.fixed and bb.off < PROLOGUE:
            return None
        for _, _, kind, j, rel in reversed(PIECES[:upto]):
            if piece_exists(bb, rel):
                return kind, j, bb.plus(rel)
    return None


def slot(d, g):
    return HG * (2 * d.par + g if g < 2 else 2 + g)


def build(nc, x, wqT, bq, wkT, bk, wvT, bv, woT, bo, J, lam, lns, lnb, gwT, Wg, Wu, Wd, sWg, sWu, sWd, out):
    x_v = x.rearrange("b (t p) d -> b p t d", p=P)
    out_v = out.rearrange("b (t p) d -> b p t d", p=P)
    k_parts = nc.dram_tensor("k_parts", [2, 2, 2, H, HD, S], F32, kind="Internal").ap()
    q_parts = nc.dram_tensor("q_parts", [2, 2, 2, H, HD, S], F32, kind="Internal").ap()
    x1_d = nc.dram_tensor("x1_d", [NB, P, TT, D], F32, kind="Internal").ap()
    ys_d = nc.dram_tensor("ys_d", [NT, P, D], F32, kind="Internal").ap()
    xs_d = nc.dram_tensor("xs_d", [NSLOT * P, D], F32, kind="Internal").ap()
    yo_d = nc.dram_tensor("yo_d", [NSLOT * P, D], F32, kind="Internal").ap()

    top = ExitStack()
    with top:
        def sbt(ctx, name, shape, dt=F32):
            return ctx.enter_context(nc.sbuf_tensor(name, shape, dt))

        ident = sbt(top, "ident", [P, P])
        ones = sbt(top, "ones", [P, P])
        mv2 = sbt(top, "mv2", [P, NT, 2])
        eps = sbt(top, "eps", [P, 1])
        xs_zeroed = top.enter_context(nc.semaphore("xs_zeroed"))

        with ExitStack() as c:
            attention_stage(nc, c, sbt, x_v, wqT, bq, wkT, bk, wvT, bv, woT, bo, J, lam,
                            k_parts, q_parts, x1_d, xs_d, ident, ones, mv2, eps, xs_zeroed)
        with ExitStack() as c:
            moe_stages(nc, c, sbt, lns, lnb, gwT, Wg, Wu, Wd, sWg, sWu, sWd, out_v,
                       x1_d, ys_d, xs_d, yo_d, ident, ones, mv2, eps, xs_zeroed)


def attention_stage(nc, ctx, sbt, x_v, wqT, bq, wkT, bk, wvT, bv, woT, bo, J, lam,
                    k_parts, q_parts, x1_d, xs_d, ident, ones, mv2, eps, xs_zeroed):
    def sb(name, shape, dt=F32):
        return sbt(ctx, name, shape, dt)

    def sem(name):
        return ctx.enter_context(nc.semaphore(name))

    wq = sb("wq", [P, KT, D])
    wk = sb("wk", [P, KT, D])
    wv = sb("wv", [P, KT, D])
    wo = sb("wo", [P, KT, D])
    bq_c = sb("bq_c", [P, 2])
    bk_c = sb("bk_c", [P, 2])
    bv_b = sb("bv_b", [P, D])
    bo_b = sb("bo_b", [P, D])
    lam_b = sb("lam_b", [P, 1])
    jb = sb("jb", [P, 2, P])
    ident_bf = sb("ident_bf", [P, P], BF16)
    mask_bf = sb("mask_bf", [P, P], BF16)
    mv1 = sb("mv1", [P, NT, 2])
    rstd1 = sb("rstd1", [P, NT])
    st1 = sb("st1", [P, 2, TT, 6])
    zrows = sb("zrows", [P, ZR * D])
    pace_v = sb("pace_v", [1, 1])

    with ExitStack() as c1:
        mvt = sbt(c1, "mvt", [P, 2, TT, 2])
        xs1 = sbt(c1, "xs1", [P, 4, TT, D])
        s_w = c1.enter_context(nc.semaphore("s_w"))
        s_j = c1.enter_context(nc.semaphore("s_j"))
        s_x = [c1.enter_context(nc.semaphore(f"s_x{r}")) for r in range(4)]
        s_jz = c1.enter_context(nc.semaphore("s_jz"))
        s_id0 = c1.enter_context(nc.semaphore("s_id0"))
        s_id = c1.enter_context(nc.semaphore("s_id"))
        s_st = c1.enter_context(nc.semaphore("s_st"))
        s_ag = c1.enter_context(nc.semaphore("s_ag"))
        s_cp = c1.enter_context(nc.semaphore("s_cp"))
        s_ep = c1.enter_context(nc.semaphore("s_ep"))
        s_sq = c1.enter_context(nc.semaphore("s_sq"))
        s_zr = c1.enter_context(nc.semaphore("s_zr"))
        block = c1.enter_context(nc.Block())

        @block.sync
        def _(sp):
            for r in range(4):
                sp.dma_start(xs1[:, r], x_v[r]).then_inc(s_x[r], 16)
            with sp.Fori(1, NB // 4) as i:
                for r in range(4):
                    sp.wait_ge(s_st, (i - 1) * 16 + 4 * r + 4)
                    sp.nop(nofuse=True)
                    sp.dma_start(xs1[:, r], x_v[bass.ds(i * 4 + r, 1)].rearrange("o p t d -> (o p) t d")).then_inc(s_x[r], 16)
            sp.wait_ge(s_w, 16 * 11)
            sp.nop(nofuse=True)
            sp.wait_ge(s_j, 16 * H)
            sp.nop(nofuse=True)

        @block.scalar
        def _(act):
            for t, src in ((wq, wqT), (wk, wkT), (wv, wvT), (wo, woT)):
                act.dma_start(t[:], src.rearrange("(k p) n -> p k n", p=P)).then_inc(s_w, 16)
            for g in range(2):
                for t, src in ((bq_c, bq), (bk_c, bk)):
                    act.dma_start(t[:, g:g + 1], src[g * P:(g + 1) * P].rearrange("(p o) -> p o", o=1)).then_inc(s_w, 16)
            act.dma_start(bv_b[:], bv.rearrange("(o n) -> o n", o=1).to_broadcast([P, D])).then_inc(s_w, 16)
            act.dma_start(bo_b[:], bo.rearrange("(o n) -> o n", o=1).to_broadcast([P, D])).then_inc(s_w, 16)
            act.dma_start(lam_b[:], lam.rearrange("(o n) -> o n", o=1).to_broadcast([P, 1])).then_inc(s_w, 16)
            act.wait_ge(s_jz, 1)
            for h in range(H):
                r = (h % PG) * HD
                act.dma_start(jb[r:r + HD, h // PG, r:r + HD], J[h]).then_inc(s_j, 16)
            act.wait_ge(s_ep, 1)
            act.wait_ge(s_cp, NB)
            nc.scalar.activation(rstd1[:], mv1[:, :, 1], ACT.Sqrt, bias=eps[:, 0:1]).then_inc(s_sq, 1)

        @block.gpsimd
        def _(pool):
            nc.gpsimd.memset(jb[:], 0.0).then_inc(s_jz, 1)
            nc.gpsimd.memset(zrows[:], 0.0).then_inc(s_zr, 1)
            nc.gpsimd.memset(ident[:], 0.0).then_inc(s_id0, 1)
            nc.gpsimd.memset(ident_bf[:], 0.0).then_inc(s_id0, 1)
            nc.gpsimd.memset(mask_bf[:], 0.0).then_inc(s_id0, 1)
            nc.gpsimd.memset(ones[:], 1.0).then_inc(s_id0, 1)
            pool.wait_ge(s_id0, 4)
            for t in (ident, ident_bf):
                nc.gpsimd.affine_select(out=t[:], in_=t[:], compare_op=ALU.not_equal, fill=1.0, base=0,
                                        pattern=[[-1, P]], channel_multiplier=1).then_inc(s_id, 1)
            nc.gpsimd.affine_select(out=mask_bf[:], in_=mask_bf[:], compare_op=ALU.is_ge, fill=MASK, base=0,
                                    pattern=[[-1, P]], channel_multiplier=1).then_inc(s_id, 1)
            pool.wait_ge(s_zr, 1)
            xs_z = xs_d.rearrange("(a p s) d -> a p (s d)", p=P, s=ZR)
            with pool.Fori(0, NSLOT // ZR) as a:
                pool.dma_start(xs_z[bass.ds(a, 1)].rearrange("o p n -> (o p) n"), zrows[:]).then_inc(xs_zeroed, 16)
            pool.wait_ge(s_w, 16 * 11)
            pool.wait_ge(s_j, 16 * H)
            nc.gpsimd.tensor_scalar(jb[:], jb[:], lam_b[:, 0:1], None, ALU.mult).then_inc(s_id, 1)

        @block.vector
        def _(dve):
            nc.vector.memset(eps[:], EPS).then_inc(s_ep, 1)

            def stats(i, r, first):
                dve.wait_ge(s_x[r], i * 16 + 16 if not first else 16)
                for t in range(TT):
                    if not (first and r < 2):
                        dve.wait_ge(s_ag, (i * 16 if not first else 0) + 4 * r - 4)
                    nc.vector.bn_stats(st1[:, r % 2, t], xs1[:, r, t]).then_inc(s_st, 1)
                dve.wait_ge(s_st, (i * 16 if not first else 0) + 4 * r + TT)
                nc.vector.tensor_copy(pace_v[:], eps[0:1])
                for t in range(TT):
                    a = nc.vector.bn_aggr(mvt[:, r % 2, t], st1[:, r % 2, t])
                a.then_inc(s_ag, 4)
                dve.wait_ge(s_ag, (i * 16 if not first else 0) + 4 * r + TT)
                nc.vector.tensor_copy(mv1[:, 4 * r:4 * r + TT] if first else mv1[:, bass.ds(i * 16 + 4 * r, TT)], mvt[:, r % 2])\
                    .then_inc(s_cp, 1)

            for r in range(4):
                stats(0, r, True)
            with dve.Fori(1, NB // 4) as i:
                for r in range(4):
                    stats(i, r, False)
            dve.wait_ge(s_sq, 1)
            nc.vector.reciprocal(rstd1[:], rstd1[:])

    qs = sb("qs", [P, 6 * HG, S], F32R)
    ks = sb("ks", [P, 6 * HG, S], F32R)
    xn = sb("xn", [P, TT, D])
    xT = sb("xT", [P, KT, S])
    lin = sb("lin", [P, 2, S])
    th = sb("th", [P, 2, S])
    part = {n: sb("part_" + n, [P, S], F32R) for n in ("kh", "kl", "th", "tl")}
    vt = sb("vt", [P, 2, TT, H, 2 * HD])
    probs = sb("probs", [P, 2, HG, S])
    mx = sb("mx", [P, 2, TT, HG])
    nm = sb("nm", [P, TT, P], F32R)
    mT = sb("mT", [P, S], F32R)
    osb = sb("osb", [P, S])
    rec = sb("rec", [P, TT, HG])
    on = sb("on", [P, 2, TT, D])
    onT = sb("onT", [P, KT, S])
    xres = sb("xres", [P, TT, D])
    st2 = sb("st2", [P, 2, 6])
    mvs = sb("mvs", [P, 2, 2])
    pace = sb("pace", [1, 2])

    ps_rows = [ctx.enter_context(nc.psum_tensor(f"ps_rows{r}", [P, S], F32)) for r in range(2)]
    ps_cols = [ctx.enter_context(nc.psum_tensor(f"ps_cols{r}", [P, 2, S], F32)) for r in range(2)]
    ps_o = ctx.enter_context(nc.psum_tensor("ps_o", [P, S], F32))
    ps_m = ctx.enter_context(nc.psum_tensor("ps_m", [P, S], F32))

    rows_ready = sem("rows_ready")
    max_done = sem("max_done")
    nm_ready = sem("nm_ready")
    nmh_ready = sem("nmh_ready")
    mrow_loaded = sem("mrow_loaded")
    cols_ready = sem("cols_ready")
    exp_done = sem("exp_done")
    sel_done = sem("sel_done")
    pv_done = sem("pv_done")
    o_taken = sem("o_taken")
    ready = {k: sem(k + "_ready") for k in PER_BATCH}
    taken = {k: sem(k + "_taken") for k in PER_BATCH}
    x_loaded = sem("x_loaded")
    xn_ready = sem("xn_ready")
    xres_loaded = sem("xres_loaded")
    xres_ready = sem("xres_ready")
    kth_done = sem("kth_done")
    hi_done = sem("hi_done")
    thi_done = sem("thi_done")
    lo_done = sem("lo_done")
    tlo_done = sem("tlo_done")
    lin_out = sem("lin_out")
    tan_out = sem("tan_out")
    stack01 = [sem(f"stack01_{r}") for r in range(2)]
    stack23 = [sem(f"stack23_{r}") for r in range(2)]
    rec_ready = sem("rec_ready")
    x1_stored = [sem(f"x1_stored{r}") for r in range(2)]
    st2_ready = sem("st2_ready")
    mvs_ready = sem("mvs_ready")
    const_ready = sem("const_ready")

    def count(kind, j, b):
        return b.v * PER_BATCH[kind] + j + 1

    def unit(b, n):
        m = n + LEAD
        return b.plus(m // STEPS), (m % STEPS) // TT, m % TT

    block = ctx.enter_context(nc.Block())

    @block.tensor
    def _(pe):
        def piece(b, n, place):
            for kind, j, d, before in pieces_at(b, n, place):
                if before:
                    pe.wait_ge(taken[before[0]], count(*before))
                if kind == "xt":
                    pe.wait_ge(xn_ready, d.v + 1)
                    for t in range(TT):
                        mm = nc.tensor.transpose(ps_m[:, t * P:(t + 1) * P], xn[:, t, j * P:(j + 1) * P], ident[:])
                elif kind in ("k", "q"):
                    pe.wait_ge(taken["xt"], count("xt", 1, d))
                    w = wk if kind == "k" else wq
                    for k in range(KT):
                        mm = nc.tensor.matmul(ps_m[:], w[:, k, j * P:(j + 1) * P], xT[:, k], start=k == 0, stop=k == KT - 1)
                elif kind == "qj":
                    pe.wait_ge(kth_done, d.v * 4 + 3 + j)
                    mm = nc.tensor.matmul(ps_m[:], jb[:, j], th[:, j], start=True, stop=True)
                elif kind == "v":
                    for tt in range(2):
                        t = 2 * j + tt
                        for k in range(KT):
                            mm = nc.tensor.matmul(ps_m[:, tt * D:(tt + 1) * D], xT[:, k, t * P:(t + 1) * P], wv[:, k],
                                                  start=k == 0, stop=k == KT - 1)
                elif kind == "mt":
                    pe.wait_ge(nm_ready, d.v * G + j + 1)
                    for t in range(TT):
                        mm = nc.tensor.transpose(ps_m[:, t * P:(t + 1) * P], nm[:, t].bitcast(F32), ident[:])
                elif kind == "ot":
                    pe.wait_ge(o_taken, d.v * G + j + 1)
                    for t in range(TT):
                        mm = nc.tensor.transpose(ps_m[:, t * P:(t + 1) * P], osb[:, t * P:(t + 1) * P], ident[:])
                elif kind == "ont":
                    pe.wait_ge(taken["ot"], count("ot", G - 1, d))
                    for t in range(TT):
                        mm = nc.tensor.transpose(ps_m[:, t * P:(t + 1) * P], on[:, d.par, t, j * P:(j + 1) * P], ident[:])
                elif kind == "out":
                    pe.wait_ge(taken["ont"], count("ont", 1, d))
                    for tt in range(2):
                        t = 2 * j + tt
                        for k in range(KT):
                            mm = nc.tensor.matmul(ps_m[:, tt * D:(tt + 1) * D], onT[:, k, t * P:(t + 1) * P], wo[:, k],
                                                  start=k == 0, stop=k == KT - 1)
                mm.then_inc(ready[kind], 1)

        def rows(b, n, h):
            d, g, it = unit(b, n)
            if not (d.at_least(0) and d.at_most(NB - 1)):
                return
            first = d.fixed and d.off == 0 and g == 0 and it == 0 and h < 2
            if g != 1 and it == 0 and h == 0:
                if g == 0:
                    pe.wait_ge(stack01[d.par], (d.half() + 1) * LOADS)
                else:
                    pe.wait_ge(stack23[g - 2], (d.v + 1) * LOADS)
            if not first:
                pe.wait_ge(max_done, d.v * (STEPS * HG) + (g * TT + it) * HG + h - 1)
            hh = slot(d, g) + h
            bank = ps_rows[h % 2]
            nc.tensor.matmul(bank[:, 0:(it + 1) * P], qs[0:STACK, hh, it * P:(it + 1) * P],
                             ks[0:STACK, hh, 0:(it + 1) * P], start=True, stop=False)
            nc.tensor.matmul(bank[:, it * P:(it + 1) * P], ident_bf[:], mask_bf[:], start=False, stop=True)\
                .then_inc(rows_ready, 1)

        def cols(b, n, pair):
            g, jt = n // TT, n % TT
            if pair == 0 and jt == 0:
                pe.wait_ge(mrow_loaded, (b.v * G + g + 1) * 16 * HG)
            if not (b.fixed and b.off == 0 and n == 0):
                pe.wait_ge(exp_done, (b.v * STEPS + n) * 2 + pair - 1)
            for e in range(2):
                hh = slot(b, g) + 2 * pair + e
                mm = nc.tensor.matmul(ps_cols[pair][:, e, jt * P:S], ks[0:MROW + 2, hh, jt * P:(jt + 1) * P],
                                      qs[0:MROW + 2, hh, jt * P:S], start=True, stop=True)
            mm.then_inc(cols_ready, 1)

        def pv(b, n):
            g, jt = n // TT, n % TT
            pe.wait_ge(sel_done, b.v * STEPS + n + 1)
            if n == 0:
                pe.wait_ge(taken["v"], count("v", 1, b))
            if jt == 0 and not (b.fixed and b.off == 0 and g == 0):
                pe.wait_ge(o_taken, b.v * G + g)
            for h in range(HG):
                mm = nc.tensor.matmul(ps_o[2 * HD * h:2 * HD * (h + 1), jt * P:S], vt[:, b.par, jt, g * HG + h],
                                      probs[:, n % 2, h, jt * P:S], start=jt == 0, stop=jt == TT - 1)
            mm.then_inc(pv_done, 1)

        def batch(b):
            att = b.at_least(0) and b.at_most(NB - 1)
            for n in range(STEPS):
                rows(b, n, 0)
                rows(b, n, 1)
                piece(b, n, 0)
                if att:
                    cols(b, n, 0)
                rows(b, n, 2)
                rows(b, n, 3)
                if att:
                    cols(b, n, 1)
                if n > 0 and att:
                    pv(b, n - 1)
                if n == 0 and b.at_least(1):
                    pv(b.plus(-1), STEPS - 1)
                piece(b, n, 1)

        pe.wait_ge(const_ready, 3)
        over_batches(pe, batch)

    @block.scalar
    def _(act):
        def piece(b, n, place):
            for kind, j, d, _ in pieces_at(b, n, place):
                if kind == "xt":
                    act.wait_ge(ready[kind], count(kind, j, d))
                    nc.scalar.activation(xT[:, j], ps_m[:], ACT.Copy).then_inc(taken[kind], 1)
                elif kind in ("k", "q"):
                    c = 0 if kind == "k" else 2
                    act.wait_ge(taken[kind], count(kind, j, d))
                    if kind == "k":
                        if d.at_least(1):
                            act.wait_ge(ready["qj"], d.v * 2 + j - 1)
                    else:
                        act.wait_ge(tlo_done, d.v * 2 + 1 + j)
                    nc.scalar.activation(th[:, j], lin[:, j], ACT.Tanh, scale=1.0 if kind == "k" else 4.0)\
                        .then_inc(kth_done, 1)
                    if j > 0 or kind == "q" or d.at_least(1):
                        act.wait_ge(lin_out, (d.v * 4 + c + j) * 32)
                    nc.scalar.activation(part["kh"][:], lin[:, j], ACT.Copy).then_inc(hi_done, 1)
                    if kind == "k":
                        if j > 0 or d.at_least(1):
                            act.wait_ge(tan_out, (d.v * 4 + j) * 32)
                        act.wait_ge(kth_done, d.v * 4 + j + 1)
                        nc.scalar.activation(part["th"][:], th[:, j], ACT.Copy).then_inc(thi_done, 1)
                elif kind == "qj":
                    act.wait_ge(ready[kind], count(kind, j, d))
                    act.wait_ge(tan_out, (d.v * 4 + 2 + j) * 32)
                    nc.scalar.activation(part["th"][:], ps_m[:], ACT.Copy).then_inc(thi_done, 1)
                elif kind == "mt":
                    act.wait_ge(ready[kind], count(kind, j, d))
                    if j > 0 or d.at_least(1):
                        act.wait_ge(mrow_loaded, (d.v * G + j) * 16 * HG)
                    nc.scalar.activation(mT[0:2 * HG], ps_m[0:2 * HG], ACT.Copy).then_inc(taken[kind], 1)
                elif kind == "ont":
                    act.wait_ge(ready[kind], count(kind, j, d))
                    nc.scalar.activation(onT[:, j], ps_m[:], ACT.Copy).then_inc(taken[kind], 1)

        def exps(b, n, pair):
            g, jt = n // TT, n % TT
            act.wait_ge(cols_ready, (b.v * STEPS + n) * 2 + pair + 1)
            if pair == 0 and not (b.fixed and b.off == 0 and n < 2):
                act.wait_ge(pv_done, b.v * STEPS + n - 1)
            nc.scalar.activation(probs[:, n % 2, 2 * pair:2 * pair + 2, jt * P:S], ps_cols[pair][:, :, jt * P:S],
                                 ACT.Exp).then_inc(exp_done, 1)

        def o_copy(b, g):
            act.wait_ge(pv_done, b.v * STEPS + (g + 1) * TT)
            if g > 0 or b.at_least(1):
                act.wait_ge(ready["ot"], b.v * G + g)
            nc.scalar.activation(osb[:], ps_o[:], ACT.Copy).then_inc(o_taken, 1)

        def batch(b):
            att = b.at_least(0) and b.at_most(NB - 1)
            for n in range(STEPS):
                piece(b, n, 0)
                if att:
                    exps(b, n, 0)
                    exps(b, n, 1)
                if n % TT == 0:
                    if n > 0 and att:
                        o_copy(b, n // TT - 1)
                    if n == 0 and b.at_least(1):
                        o_copy(b.plus(-1), G - 1)
                piece(b, n, 1)

        over_batches(act, batch)

    @block.vector
    def _(dve):
        def layer_norm(d):
            dve.wait_ge(x_loaded, (d.v + 1) * 16)
            for t in range(TT):
                if d.fixed:
                    m, r = mv1[:, d.off * TT + t, 0:1], rstd1[:, d.off * TT + t:d.off * TT + t + 1]
                else:
                    m = mv1[:, bass.ds(d.v * TT + t, 1), 0]
                    r = rstd1[:, bass.ds(d.v * TT + t, 1)]
                ts = nc.vector.tensor_scalar(xn[:, t], xn[:, t], m, r, ALU.subtract, ALU.mult)
            ts.then_inc(xn_ready, 1)

        def maximum(b, n, h):
            d, g, it = unit(b, n)
            if not (d.at_least(0) and d.at_most(NB - 1)):
                return
            gb = g % 2
            dve.wait_ge(rows_ready, d.v * (STEPS * HG) + (g * TT + it) * HG + h + 1)
            nc.vector.tensor_reduce(mx[:, gb, it, h:h + 1], ps_rows[h % 2][:, 0:(it + 1) * P], AX.X, ALU.max)\
                .then_inc(max_done, 1)
            if it == TT - 1 and h == HG - 1:
                dve.wait_ge(max_done, d.v * (STEPS * HG) + (g + 1) * TT * HG)
                if g > 0 or d.at_least(1):
                    dve.wait_ge(ready["mt"], d.v * G + g)
                pair = nm[:, :, 0:2 * HG].rearrange("p t (h two) -> p t h two", two=2)
                nc.vector.tensor_scalar(pair[:, :, :, 0], mx[:, gb], -1.0, None, ALU.mult).then_inc(nmh_ready, 1)
                dve.wait_ge(nmh_ready, d.v * G + g + 1)
                nc.vector.scalar_tensor_tensor(out=pair[:, :, :, 1], in0=mx[:, gb], scalar=-1.0,
                                               in1=pair[:, :, :, 0].bitcast(F32), op0=ALU.mult, op1=ALU.subtract)\
                    .then_inc(nm_ready, 1)

        def piece(b, n, place):
            for kind, j, d, _ in pieces_at(b, n, place):
                if kind in ("xt", "mt", "ont"):
                    continue
                dve.wait_ge(ready[kind], count(kind, j, d))
                if kind == "k":
                    if d.at_least(1):
                        dve.wait_ge(lo_done, d.v * 4 - 1 + j)
                    nc.vector.tensor_scalar(lin[:, j], ps_m[:], bk_c[:, j:j + 1], None, ALU.add).then_inc(taken[kind], 1)
                elif kind == "q":
                    dve.wait_ge(lo_done, d.v * 4 + 1 + j)
                    nc.vector.tensor_scalar(lin[:, j], ps_m[:], bq_c[:, j:j + 1], 0.25, ALU.add, ALU.mult)\
                        .then_inc(taken[kind], 1)
                elif kind == "qj":
                    dve.wait_ge(thi_done, d.v * 4 + 3 + j)
                    dve.wait_ge(tan_out, (d.v * 4 + 2 + j) * 32)
                    nc.vector.tensor_tensor(part["tl"][:], ps_m[:], part["th"][:].bitcast(F32), ALU.subtract)\
                        .then_inc(taken[kind], 1)
                elif kind == "v":
                    for tt in range(2):
                        a = nc.vector.tensor_tensor(
                            vt[:, d.par, 2 * j + tt, :, 0:HD],
                            ps_m[:, tt * D:(tt + 1) * D].rearrange("p (h e) -> p h e", h=H),
                            bv_b[:].rearrange("p (h e) -> p h e", h=H), ALU.add)
                    a.then_inc(taken[kind], 1)
                elif kind == "ot":
                    pso = ps_m[:].rearrange("p (t h e) -> p t h e", t=TT, h=HG)
                    nc.vector.reciprocal(rec[:], pso[:, :, :, HD]).then_inc(rec_ready, 1)
                    dve.wait_ge(rec_ready, d.v * G + j + 1)
                    nc.vector.tensor_tensor(
                        on[:, d.par, :, j * HG * HD:(j + 1) * HG * HD].rearrange("p t (h e) -> p t h e", h=HG),
                        pso[:, :, :, 0:HD], rec[:].unsqueeze(3).to_broadcast([P, TT, HG, HD]), ALU.mult)\
                        .then_inc(taken[kind], 1)
                elif kind == "out":
                    dve.wait_ge(xres_ready, d.v + 1)
                    x1 = xres[:, 2 * j:2 * j + 2]
                    nc.vector.tensor_tensor(x1, ps_m[:].rearrange("p (t e) -> p t e", t=2), x1, ALU.add)\
                        .then_inc(taken[kind], 1)
                    dve.wait_ge(taken[kind], count(kind, j, d))
                    for tt in range(2):
                        s_ = nc.vector.bn_stats(st2[:, tt], xres[:, 2 * j + tt])
                    s_.then_inc(st2_ready, 1)
                    dve.wait_ge(st2_ready, d.v * 2 + j + 1)
                    nc.vector.tensor_copy(pace_v[:], eps[0:1])
                    for tt in range(2):
                        s_ = nc.vector.bn_aggr(mvs[:, tt], st2[:, tt])
                    s_.then_inc(mvs_ready, 1)
                    dve.wait_ge(mvs_ready, d.v * 2 + j + 1)
                    at = d.v * TT + 2 * j
                    nc.vector.tensor_copy(mv2[:, at:at + 2] if d.fixed else mv2[:, bass.ds(at, 2)], mvs[:])

        def batch(b):
            for n in range(STEPS):
                maximum(b, n, 0)
                maximum(b, n, 1)
                piece(b, n, 0)
                maximum(b, n, 2)
                maximum(b, n, 3)
                piece(b, n, 1)
                if n == 0 and b.plus(1).at_most(NB - 1):
                    layer_norm(b.plus(1))

        nc.vector.memset(nm[:].bitcast(F32), 0.0).then_inc(const_ready, 1)
        nc.vector.memset(vt[:, :, :, :, HD:2 * HD], 1.0).then_inc(const_ready, 1)
        over_batches(dve, batch)

    @block.gpsimd
    def _(pool):
        def piece(b, n, place):
            for kind, j, d, _ in pieces_at(b, n, place):
                if kind in ("k", "q"):
                    c = 0 if kind == "k" else 2
                    pool.wait_ge(hi_done, d.v * 4 + c + j + 1)
                    if j > 0 or kind == "q" or d.at_least(1):
                        pool.wait_ge(lin_out, (d.v * 4 + c + j) * 32)
                    nc.gpsimd.tensor_tensor(part["kl"][:], lin[:, j], part["kh"][:].bitcast(F32), ALU.subtract)\
                        .then_inc(lo_done, 1)
                    if kind == "k":
                        pool.wait_ge(thi_done, d.v * 4 + j + 1)
                        if j > 0 or d.at_least(1):
                            pool.wait_ge(tan_out, (d.v * 4 + j) * 32)
                        nc.gpsimd.tensor_tensor(part["tl"][:], th[:, j], part["th"][:].bitcast(F32), ALU.subtract)\
                            .then_inc(tlo_done, 1)

        def select(b, n):
            jt = n % TT
            pool.wait_ge(exp_done, (b.v * STEPS + n) * 2 + 2)
            nc.gpsimd.tensor_tensor(pace[:, n % 2:n % 2 + 1], eps[0:1], eps[0:1], ALU.add)
            blk = probs[:, n % 2, :, jt * P:(jt + 1) * P]
            nc.gpsimd.affine_select(out=blk, in_=blk, compare_op=ALU.is_ge, fill=0.0, base=0,
                                    pattern=[[0, HG], [1, P]], channel_multiplier=-1).then_inc(sel_done, 1)

        def batch(b):
            att = b.at_least(0) and b.at_most(NB - 1)
            for n in range(STEPS):
                piece(b, n, 0)
                if att:
                    select(b, n)
                piece(b, n, 1)
                if n == 6 and piece_exists(b, -1):
                    d = b.plus(-1)
                    pool.wait_ge(xres_loaded, (d.v + 1) * 16)
                    nc.gpsimd.tensor_tensor(xres[:], xres[:], bo_b[:].unsqueeze(1).to_broadcast([P, TT, D]), ALU.add)\
                        .then_inc(xres_ready, 1)

        nc.gpsimd.memset(ks[MROW:P].bitcast(F32), 1.0).then_inc(const_ready, 1)
        over_batches(pool, batch)

    @block.sync
    def _(sp):
        def store(d, kind, j, row, done, tile, out_sem):
            dram = k_parts if kind == "k" else q_parts
            sp.wait_ge(*done)
            sp.nop(nofuse=True)
            sp.dma_start(dram[d.par, row[0], row[1], j * PG:(j + 1) * PG].rearrange("h r t -> (h r) t"), part[tile][:].bitcast(F32))\
                .then_inc(out_sem, 16)

        def store_parts(d, kind, j):
            if kind == "k" and j == 0 and d.at_least(2):
                sp.wait_ge(stack23[1], (d.v - 1) * LOADS)
                sp.nop(nofuse=True)
            if kind in ("k", "q"):
                n = d.v * 4 + (0 if kind == "k" else 2) + j + 1
                store(d, kind, j, (0, 0), (hi_done, n), "kh", lin_out)
                store(d, kind, j, (1, 0), (lo_done, n), "kl", lin_out)
            if kind in ("k", "qj"):
                n = d.v * 4 + (0 if kind == "k" else 2) + j + 1
                store(d, kind, j, (0, 1), (thi_done, n), "th", tan_out)
                store(d, kind, j, (1, 1), (tlo_done, d.v * 2 + j + 1) if kind == "k" else (taken["qj"], count("qj", j, d)),
                      "tl", tan_out)

        def load_stack(d, g, groups, stack, dram, pair, done):
            for a, part_no in enumerate(pair):
                for c in range(2):
                    r = (2 * a + c) * HD
                    sp.dma_start(stack[r:r + HD, slot(d, g):slot(d, g) + HG * groups].bitcast(F32),
                                 dram[d.par, part_no, c, HG * g:HG * (g + groups)].rearrange("h r t -> r h t"))\
                        .then_inc(done, 16)

        KEY_PARTS, QUERY_PARTS = (0, 1, 0), (0, 0, 1)

        def load_keys01(d):
            sp.wait_ge(lin_out, (d.v * 4 + 2) * 32)
            sp.nop(nofuse=True)
            sp.wait_ge(tan_out, (d.v * 4 + 2) * 32)
            sp.nop(nofuse=True)
            if d.at_least(2):
                sp.wait_ge(cols_ready, (d.v - 1) * STEPS * 2)
                sp.nop(nofuse=True)
            load_stack(d, 0, 2, ks, k_parts, KEY_PARTS, stack01[d.par])

        def load_queries01(d):
            sp.wait_ge(lin_out, (d.v + 1) * 4 * 32)
            sp.nop(nofuse=True)
            sp.wait_ge(tan_out, (d.v + 1) * 4 * 32)
            sp.nop(nofuse=True)
            load_stack(d, 0, 2, qs, q_parts, QUERY_PARTS, stack01[d.par])

        def load_group(d, g):
            if d.at_least(1):
                sp.wait_ge(cols_ready, ((d.v - 1) * STEPS + (g + 1) * TT) * 2)
                sp.nop(nofuse=True)
            load_stack(d, g, 1, ks, k_parts, KEY_PARTS, stack23[g - 2])
            load_stack(d, g, 1, qs, q_parts, QUERY_PARTS, stack23[g - 2])

        def max_rows(d, g):
            sp.wait_ge(taken["mt"], d.v * G + g + 1)
            sp.nop(nofuse=True)
            for h in range(HG):
                sp.dma_start(qs[MROW:MROW + 2, slot(d, g) + h].bitcast(F32), mT[2 * h:2 * h + 2, :].bitcast(F32)).then_inc(mrow_loaded, 16)

        def x_of(view, d):
            return view[d.off] if d.fixed else view[bass.ds(d.v, 1)].rearrange("o p t e -> (o p) t e")

        def batch(b):
            if b.plus(1).at_most(NB - 1):
                if b.plus(1).at_least(1):
                    sp.wait_ge(ready["xt"], (b.v + 1) * 2)
                    sp.nop(nofuse=True)
                sp.dma_start(xn[:], x_of(x_v, b.plus(1))).then_inc(x_loaded, 16)
            for n in range(STEPS):
                if n == 0 and b.at_least(0) and b.at_most(NB - 1):
                    load_group(b, 3)
                for place in range(2):
                    for kind, j, d, _ in pieces_at(b, n, place):
                        if kind in ("k", "q", "qj"):
                            store_parts(d, kind, j)
                            if (kind, j) == ("k", 1):
                                load_keys01(d)
                            if (kind, j) == ("qj", 1):
                                load_queries01(d)
                        elif kind == "mt":
                            max_rows(d, j)
                        elif kind == "out":
                            sp.wait_ge(taken["out"], count("out", j, d))
                            sp.nop(nofuse=True)
                            sp.dma_start(x_of(x1_d, d)[:, 2 * j:2 * j + 2], xres[:, 2 * j:2 * j + 2]).then_inc(x1_stored[j], 16)
                if n == 12 and b.plus(1).at_most(NB - 1):
                    load_group(b.plus(1), 2)
                if n == 14 and b.at_least(0) and b.at_most(NB - 1):
                    if b.at_least(1):
                        sp.wait_ge(x1_stored[0], b.v * 16)
                        sp.nop(nofuse=True)
                        sp.wait_ge(x1_stored[1], b.v * 16)
                        sp.nop(nofuse=True)
                        sp.wait_ge(st2_ready, b.v * 2)
                        sp.nop(nofuse=True)
                    sp.dma_start(xres[:], x_of(x_v, b)).then_inc(xres_loaded, 16)

        over_batches(sp, batch)
        for j in range(2):
            sp.wait_ge(x1_stored[j], NB * 16)
            sp.nop(nofuse=True)


def moe_stages(nc, ctx, sbt, lns, lnb, gwT, Wg, Wu, Wd, sWg, sWu, sWd, out_v,
               x1_d, ys_d, xs_d, yo_d, ident, ones, mv2, eps, xs_zeroed):
    pos = [sbt(ctx, f"pos{r}", [P, NT], I32) for r in range(2)]
    wgt = [sbt(ctx, f"wgt{r}", [P, NT]) for r in range(2)]
    slot_e = sbt(ctx, "slot_e", [1, NSLOT], I32)

    with ExitStack() as c:
        x2 = sbt(c, "x2", [P, NT, D])
        rstd3 = sbt(c, "rstd3", [P, NT])
        mv3 = sbt(c, "mv3", [P, NT, 2])
        logits = sbt(c, "logits", [P, NT, NE])
        gws = sbt(c, "gws", [P, KT, NE])
        gwb = sbt(c, "gwb", [P, KT, NE])
        with ExitStack() as c1:
            shared_stage(nc, c1, sbt, lns, lnb, gwT, sWg, sWu, sWd, x1_d, ys_d, ident, mv2, eps,
                         x2, rstd3, mv3, logits, gws, gwb)
        with ExitStack() as c1:
            route_stage(nc, c1, sbt, xs_d, xs_zeroed, ones, x2, rstd3, mv3, logits, gws, gwb, pos, wgt, slot_e)
    with ExitStack() as c:
        expert_stage(nc, c, sbt, Wg, Wu, Wd, xs_d, yo_d, ident, slot_e)
    with ExitStack() as c:
        combine_stage(nc, c, sbt, yo_d, ys_d, out_v, pos, wgt)


def shared_stage(nc, ctx, sbt, lns, lnb, gwT, sWg, sWu, sWd, x1_d, ys_d, ident, mv2, eps,
                 x2, rstd3, mv3, logits, gws, gwb):
    def sb(name, shape, dt=F32):
        return sbt(ctx, name, shape, dt)

    def sem(name):
        return ctx.enter_context(nc.semaphore(name))

    wg = sb("swg", [P, KT, INTER])
    wu = sb("swu", [P, KT, INTER])
    wd = sb("swd", [P, IT, D])
    sc = sb("ln_sc", [P, KT])
    bi = sb("ln_bi", [P, KT])
    gw = sb("gw", [P, KT, NE])
    rstd2 = sb("rstd2", [P, NT])
    x1 = sb("x1s", [P, 2, TT, D])
    x2n = sb("x2n", [P, 2, TT, D])
    x2T = sb("x2T", [P, 2, KT, S])
    st3 = sb("st3", [P, TT, 6])
    mvs = sb("mvs3", [P, TT, 2])
    sg = sb("sg", [P, 2, S])
    hT = sb("hT", [P, 2, IT, S])
    ysb = sb("ysb", [P, 2, 2, D])
    pace_v = sb("pace_v3", [1, 1])
    ps_t = [ctx.enter_context(nc.psum_tensor(f"ps_t{r}", [P, S], F32)) for r in range(2)]
    ps_g = [ctx.enter_context(nc.psum_tensor(f"ps_g{r}", [P, S], F32)) for r in range(2)]
    ps_u = [ctx.enter_context(nc.psum_tensor(f"ps_u{r}", [P, S], F32)) for r in range(2)]
    ps_y = ctx.enter_context(nc.psum_tensor("ps_y", [P, 2, D], F32))
    ps_l = ctx.enter_context(nc.psum_tensor("ps_l", [P, TT, NE], F32))

    w_loaded = sem("w_loaded")
    x1_loaded = [sem(f"x1_loaded{r}") for r in range(2)]
    rs_sqrt = sem("rs_sqrt")
    x2_ready = sem("x2_ready")
    x2_kept = sem("x2_kept")
    st3_ready = sem("st3_ready")
    mvs_ready = sem("mvs3_ready")
    mv3_ready = sem("mv3_ready")
    gw_ready = sem("gw_ready")
    xt_ready = sem("xt_ready")
    xt_taken = sem("xt_taken")
    lg_ready = sem("lg_ready")
    lg_taken = sem("lg_taken")
    g_ready = sem("g_ready")
    u_ready = sem("u_ready")
    sg_ready = sem("sg_ready")
    h_ready = sem("h_ready")
    y_ready = sem("y_ready")
    y_taken = sem("y_taken")
    y_stored = [sem(f"y_stored{r}") for r in range(2)]

    block = ctx.enter_context(nc.Block())
    ys_v = ys_d.rearrange("(c t) p d -> c p t d", t=TT)

    @block.sync
    def _(sp):
        for t, src in ((wg, sWg), (wu, sWu), (wd, sWd), (gw, gwT)):
            sp.dma_start(t[:], src.rearrange("(k p) n -> p k n", p=P)).then_inc(w_loaded, 16)
        for k in range(KT):
            for t, src in ((sc, lns), (bi, lnb)):
                sp.dma_start(t[:, k:k + 1], src[k * P:(k + 1) * P].rearrange("(p o) -> p o", o=1)).then_inc(w_loaded, 16)
        with sp.Fori(0, NB // 2) as i:
            for r in range(2):
                for j in range(2):
                    sp.wait_ge(y_taken, i * 4 + 2 * r + j + 1)
                    sp.nop(nofuse=True)
                    sp.dma_start(ys_v[bass.ds(i * 2 + r, 1)].rearrange("o p t d -> (o p) t d")[:, 2 * j:2 * j + 2],
                                 ysb[:, j]).then_inc(y_stored[j], 16)
        for j in range(2):
            sp.wait_ge(y_stored[j], NB * 16)
            sp.nop(nofuse=True)

    @block.gpsimd
    def _(pool):
        def keep(b, r):
            pool.wait_ge(x2_ready, b + 1)
            nc.gpsimd.tensor_copy(x2[:, b * TT:(b + 1) * TT] if isinstance(b, int) else x2[:, bass.ds(b * TT, TT)], x2n[:, r])\
                .then_inc(x2_kept, 1)

        for c in range(2):
            pool.dma_start(x1[:, c], x1_d[c]).then_inc(x1_loaded[c], 16)
        keep(0, 0)
        keep(1, 1)
        with pool.Fori(0, NB // 2 - 1) as i:
            for r in range(2):
                if r:
                    keep(i * 2 + 2, 0)
                pool.wait_ge(y_taken, i * 4 + 2 * r + 2)
                pool.dma_start(x1[:, r], x1_d[bass.ds(i * 2 + 2 + r, 1)].rearrange("o p t d -> (o p) t d"))\
                    .then_inc(x1_loaded[r], 16)
            keep(i * 2 + 3, 1)

    @block.tensor
    def _(pe):
        pe.wait_ge(gw_ready, 3)

        def transposes(b, r, first):
            pe.wait_ge(x2_ready, b + 1)
            for k in range(KT):
                if not first:
                    pe.wait_ge(xt_taken, b * 2 + k - 1)
                for t in range(TT):
                    mm = nc.tensor.transpose(ps_t[k][:, t * P:(t + 1) * P], x2n[:, r, t, k * P:(k + 1) * P], ident[:])
                mm.then_inc(xt_ready, 1)

        def gate_up(b, r, first):
            pe.wait_ge(xt_taken, b * 2 + 2)
            if not first:
                pe.wait_ge(lg_taken, b)
            for t in range(TT):
                for k in range(KT):
                    mm = nc.tensor.matmul(ps_l[:, t], x2T[:, r, k, t * P:(t + 1) * P], gws[:, k], start=k == 0, stop=k == KT - 1)
            mm.then_inc(lg_ready, 1)
            for i in range(IT):
                for w, bank, freed, done in ((wg, ps_g, sg_ready, g_ready), (wu, ps_u, h_ready, u_ready)):
                    if not (first and i < 2):
                        pe.wait_ge(freed, b * IT + i - 1)
                    for k in range(KT):
                        mm = nc.tensor.matmul(bank[i % 2][:], w[:, k, i * P:(i + 1) * P], x2T[:, r, k],
                                              start=k == 0, stop=k == KT - 1)
                    mm.then_inc(done, 1)

        def down(b, r, first):
            pe.wait_ge(h_ready, b * IT + IT)
            for j in range(2):
                if not (first and j == 0):
                    pe.wait_ge(y_taken, b * 2 + j)
                for tt in range(2):
                    t = 2 * j + tt
                    for i in range(IT):
                        mm = nc.tensor.matmul(ps_y[:, tt], hT[:, r, i, t * P:(t + 1) * P], wd[:, i], start=i == 0, stop=i == IT - 1)
                mm.then_inc(y_ready, 1)

        transposes(0, 0, True)
        gate_up(0, 0, True)
        transposes(1, 1, False)
        down(0, 0, True)
        with pe.Fori(0, NB // 2 - 1) as i:
            for r in (1, 0):
                b = i * 2 + (1 if r else 2)
                gate_up(b, r, False)
                transposes(b + 1, 1 - r, False)
                down(b, r, False)
        gate_up(NB - 1, 1, False)
        down(NB - 1, 1, False)

    @block.scalar
    def _(act):
        nc.scalar.activation(rstd2[:], mv2[:, :, 1], ACT.Sqrt, bias=eps[:, 0:1]).then_inc(rs_sqrt, 1)

        def copies(b, r, first):
            for k in range(KT):
                act.wait_ge(xt_ready, b * 2 + k + 1)
                if not first:
                    act.wait_ge(u_ready, (b - 1) * IT)
                nc.scalar.activation(x2T[:, r, k], ps_t[k][:], ACT.Copy).then_inc(xt_taken, 1)

        def silus(b, r, first):
            for i in range(IT):
                act.wait_ge(g_ready, b * IT + i + 1)
                if not (first and i < 2):
                    act.wait_ge(h_ready, b * IT + i - 1)
                nc.scalar.activation(sg[:, i % 2], ps_g[i % 2][:], ACT.Silu).then_inc(sg_ready, 1)

        copies(0, 0, True)
        silus(0, 0, True)
        copies(1, 1, True)
        with act.Fori(0, NB // 2 - 1) as i:
            for r in (1, 0):
                b = i * 2 + (1 if r else 2)
                silus(b, r, False)
                copies(b + 1, 1 - r, False)
        silus(NB - 1, 1, False)
        act.wait_ge(mv3_ready, NB)
        nc.scalar.activation(rstd3[:], mv3[:, :, 1], ACT.Sqrt, bias=eps[:, 0:1]).then_inc(rs_sqrt, 1)

    @block.vector
    def _(dve):
        dve.wait_ge(rs_sqrt, 1)
        nc.vector.reciprocal(rstd2[:], rstd2[:]).then_inc(gw_ready, 1)
        dve.wait_ge(w_loaded, 16 * 8)
        for k in range(KT):
            nc.vector.tensor_scalar(gws[:, k], gw[:, k], sc[:, k:k + 1], None, ALU.mult)
            nc.vector.tensor_scalar(gwb[:, k], gw[:, k], bi[:, k:k + 1], None, ALU.mult).then_inc(gw_ready, 1)
        dve.wait_ge(gw_ready, 3)

        def norm(b, r, loads):
            dve.wait_ge(x1_loaded[r], loads * 16)
            if not isinstance(b, int):
                dve.wait_ge(xt_ready, b * 2 - 2)
                dve.wait_ge(x2_kept, b - 1)
            for t in range(TT):
                if isinstance(b, int):
                    k = b * TT + t
                    m, rs = mv2[:, k, 0:1], rstd2[:, k:k + 1]
                else:
                    m, rs = mv2[:, bass.ds(b * TT + t, 1), 0], rstd2[:, bass.ds(b * TT + t, 1)]
                a = nc.vector.tensor_scalar(x2n[:, r, t], x1[:, r, t], m, rs, ALU.subtract, ALU.mult)
            a.then_inc(x2_ready, 1)
            dve.wait_ge(x2_ready, b + 1)
            for t in range(TT):
                a = nc.vector.bn_stats(st3[:, t], x2n[:, r, t])
            a.then_inc(st3_ready, 1)
            dve.wait_ge(st3_ready, b + 1)
            nc.vector.tensor_copy(pace_v[:], eps[0:1])
            for t in range(TT):
                a = nc.vector.bn_aggr(mvs[:, t], st3[:, t])
            a.then_inc(mvs_ready, 1)
            dve.wait_ge(mvs_ready, b + 1)
            nc.vector.tensor_copy(mv3[:, b * TT:(b + 1) * TT] if isinstance(b, int) else mv3[:, bass.ds(b * TT, TT)], mvs[:])\
                .then_inc(mv3_ready, 1)

        def products(b, r):
            for i in range(IT):
                dve.wait_ge(u_ready, b * IT + i + 1)
                dve.wait_ge(sg_ready, b * IT + i + 1)
                nc.vector.tensor_tensor(hT[:, r, i], sg[:, i % 2], ps_u[i % 2][:], ALU.mult).then_inc(h_ready, 1)

        def outputs(b, r, first):
            dve.wait_ge(lg_ready, b + 1)
            o = logits[:, b * TT:(b + 1) * TT] if isinstance(b, int) else logits[:, bass.ds(b * TT, TT)]
            nc.vector.tensor_copy(o, ps_l[:]).then_inc(lg_taken, 1)
            for j in range(2):
                dve.wait_ge(y_ready, b * 2 + j + 1)
                if not first:
                    dve.wait_ge(y_stored[j], b * 16)
                nc.vector.tensor_tensor(ysb[:, j], ps_y[:], x1[:, r, 2 * j:2 * j + 2], ALU.add).then_inc(y_taken, 1)

        norm(0, 0, 1)
        norm(1, 1, 1)
        products(0, 0)
        outputs(0, 0, True)
        with dve.Fori(0, NB // 2 - 1) as i:
            for r in (1, 0):
                b = i * 2 + (1 if r else 2)
                norm(b + 1, 1 - r, i + 2)
                products(b, r)
                outputs(b, r, False)
        products(NB - 1, 1)
        outputs(NB - 1, 1, False)
        dve.wait_ge(rs_sqrt, 2)
        nc.vector.reciprocal(rstd3[:], rstd3[:])


def route_stage(nc, ctx, sbt, xs_d, xs_zeroed, ones, x2, rstd3, mv3, logits, gws, gwb, pos, wgt, slot_e):
    def sb(name, shape, dt=F32):
        return sbt(ctx, name, shape, dt)

    def sem(name):
        return ctx.enter_context(nc.semaphore(name))

    lower = sb("lower", [P, P])
    sgb = sb("sgb", [P, 2, NE])
    a = sb("ra", [P, NT, NE])
    b = sb("rb", [P, NT, NE])
    prob = sb("prob", [P, NT, NE])
    oh = [sb(f"oh{r}", [P, NT, NE]) for r in range(2)]
    rank = sb("rank", [P, NT, NE])
    m1 = sb("m1", [P, NT])
    m2 = sb("m2", [P, NT])
    cc = sb("cc", [P, NT])
    desc = sb("desc", [P, NE])
    one64 = sb("one64", [P, NT])
    tot = sb("tot", [P, NE])
    toti = sb("toti", [P, NE], I32)
    incl = sb("incl", [P, NE])
    base = sb("base", [P, NE])
    start = sb("start", [1, NSLOT])
    cmp_ = sb("cmp_", [1, NSLOT, NE])
    cnt = sb("cnt", [1, NSLOT])
    idx = [[sb(f"idx{q}{r}", [P, 1], I32) for r in range(2)] for q in range(2)]
    row = [sb(f"row{q}", [P, D]) for q in range(2)]
    ps_s = ctx.enter_context(nc.psum_tensor("ps_s", [P, 2, NE], F32))
    ps_r = ctx.enter_context(nc.psum_tensor("ps_r", [P, NT, NE], F32))
    ps_n = ctx.enter_context(nc.psum_tensor("ps_n", [P, NT, NE], F32))

    filled = sem("filled")
    lower_ready = sem("lower_ready")
    iotas = sem("iotas")
    sums_ready = sem("sums_ready")
    chosen = sem("chosen")
    ranked = sem("ranked")
    chain = sem("chain")
    exp_in = sem("exp_in")
    exp_out = sem("exp_out")
    pos_ready = sem("pos_ready")
    staged = sem("staged")
    scattered = [sem(f"scattered{q}") for q in range(2)]
    block = ctx.enter_context(nc.Block())

    @block.tensor
    def _(pe):
        for c, w in enumerate((gws, gwb)):
            for k in range(KT):
                mm = nc.tensor.matmul(ps_s[:, c], ones[:], w[:, k], start=k == 0, stop=k == KT - 1)
        mm.then_inc(sums_ready, 1)
        pe.wait_ge(chosen, 1)
        pe.wait_ge(lower_ready, 1)
        nc.tensor.matmul(ps_r[:].rearrange("p t e -> p (t e)"), lower[:], rank[:].rearrange("p t e -> p (t e)"), start=True, stop=True)
        nc.tensor.matmul(ps_n[:].rearrange("p t e -> p (t e)"), ones[:], rank[:].rearrange("p t e -> p (t e)"), start=True, stop=True)\
            .then_inc(ranked, 1)

    @block.scalar
    def _(act):
        act.wait_ge(exp_in, 1)
        nc.scalar.activation(prob[:], a[:], ACT.Exp).then_inc(exp_out, 1)

    @block.gpsimd
    def _(pool):
        nc.gpsimd.memset(lower[:], 1.0).then_inc(filled, 1)
        pool.wait_ge(filled, 1)
        nc.gpsimd.affine_select(out=lower[:], in_=lower[:], compare_op=ALU.is_gt, fill=0.0, base=0,
                                pattern=[[1, P]], channel_multiplier=-1).then_inc(lower_ready, 1)
        nc.gpsimd.iota(desc[:], pattern=[[-1, NE]], base=NE, channel_multiplier=0,
                       allow_small_or_imprecise_dtypes=True).then_inc(iotas, 1)
        nc.gpsimd.iota(start[:], pattern=[[P, NSLOT]], base=0, channel_multiplier=0,
                       allow_small_or_imprecise_dtypes=True).then_inc(iotas, 1)
        pool.wait_ge(pos_ready, 2)
        pool.wait_ge(xs_zeroed, 16 * (NSLOT // ZR))

        def stage(t, q, n):
            if n is not None:
                pool.wait_ge(scattered[q], n * 32)
                pool.wait_ge(staged, t * 3)
            k = slice(t, t + 1) if isinstance(t, int) else bass.ds(t, 1)
            for r in range(2):
                nc.gpsimd.tensor_copy(idx[q][r][:], pos[r][:, k]).then_inc(staged, 1)
            src = x2[:, t] if isinstance(t, int) else x2[:, k].rearrange("p o e -> p (o e)")
            nc.gpsimd.tensor_copy(row[q][:], src).then_inc(staged, 1)

        def scatter(q):
            for r in range(2):
                nc.gpsimd.indirect_dma_start(xs_d[:, :], bass.IndirectOffsetOnAxis(ap=idx[q][r][:, 0:1], axis=0),
                                             row[q][:], None).then_inc(scattered[q], 16)

        stage(0, 0, None)
        stage(1, 1, None)
        pool.wait_ge(staged, 3)
        scatter(0)
        with pool.Fori(1, NT // 2) as i:
            stage(i * 2, 0, i)
            scatter(1)
            stage(i * 2 + 1, 1, i)
            scatter(0)
        pool.wait_ge(staged, NT * 3)
        scatter(1)
        for q in range(2):
            pool.wait_ge(scattered[q], NT // 2 * 32)

    @block.vector
    def _(dve):
        n = [0]

        def then(ins):
            n[0] += 1
            ins.then_inc(chain, 1)
            dve.wait_ge(chain, n[0])

        def over_e(ap):
            return ap.unsqueeze(2).to_broadcast([P, NT, NE])

        def over_t(ap):
            return ap.unsqueeze(1).to_broadcast([P, NT, NE])

        def tt(o, x, y, op):
            return nc.vector.tensor_tensor(o, x, y, op)

        dve.wait_ge(sums_ready, 1)
        then(nc.vector.tensor_copy(sgb[:], ps_s[:]))
        then(nc.vector.memset(one64[:], 1.0))
        then(nc.vector.tensor_copy(m1[:], mv3[:, :, 0]))
        then(tt(a[:], over_e(m1[:]), over_t(sgb[:, 0]), ALU.mult))
        then(tt(a[:], logits[:], a[:], ALU.subtract))
        then(tt(a[:], a[:], over_e(rstd3[:]), ALU.mult))
        then(tt(a[:], a[:], over_t(sgb[:, 1]), ALU.add))
        then(nc.vector.tensor_reduce(m1[:], a[:], AX.X, ALU.max))
        tt(a[:], a[:], over_e(m1[:]), ALU.subtract).then_inc(exp_in, 1)
        dve.wait_ge(exp_out, 1)
        then(nc.vector.tensor_reduce(m1[:], prob[:], AX.X, ALU.add))
        then(nc.vector.reciprocal(m1[:], m1[:]))
        then(tt(prob[:], prob[:], over_e(m1[:]), ALU.mult))
        dve.wait_ge(iotas, 2)

        def choose(p, best, onehot):
            then(nc.vector.tensor_reduce(best[:], p[:], AX.X, ALU.max))
            then(tt(a[:], p[:], over_e(best[:]), ALU.is_equal))
            then(tt(a[:], a[:], over_t(desc[:]), ALU.mult))
            then(nc.vector.tensor_reduce(cc[:], a[:], AX.X, ALU.max))
            then(tt(onehot[:], over_t(desc[:]), over_e(cc[:]), ALU.is_equal))

        choose(prob, m1, oh[0])
        then(nc.vector.scalar_tensor_tensor(out=b[:], in0=oh[0][:], scalar=-2.0, in1=prob[:], op0=ALU.mult, op1=ALU.add))
        choose(b, m2, oh[1])
        then(tt(cc[:], m1[:], m2[:], ALU.add))
        then(nc.vector.tensor_scalar(cc[:], cc[:], EPS, None, ALU.add))
        then(nc.vector.reciprocal(cc[:], cc[:]))
        then(tt(wgt[0][:], m1[:], cc[:], ALU.mult))
        then(tt(wgt[1][:], m2[:], cc[:], ALU.mult))
        tt(rank[:], oh[0][:], oh[1][:], ALU.add).then_inc(chosen, 1)
        dve.wait_ge(ranked, 1)
        then(nc.vector.tensor_copy(b[:], ps_n[:]))
        for e in range(NE):
            s_ = nc.vector.tensor_tensor_scan(a[:, :, e], one64[:], b[:, :, e], 0.0, ALU.mult, ALU.add)
        then(s_)
        then(nc.vector.tensor_copy(tot[:], a[:, NT - 1]))
        then(tt(a[:], a[:], b[:], ALU.subtract))
        then(tt(rank[:], a[:], ps_r[:], ALU.add))
        then(nc.vector.tensor_scalar(toti[:], tot[:], float(P - 1), None, ALU.add))
        then(nc.vector.tensor_scalar(toti[:], toti[:], 7, None, ALU.arith_shift_right))
        then(nc.vector.tensor_copy(tot[:], toti[:]))
        then(nc.vector.tensor_scalar(tot[:], tot[:], float(P), None, ALU.mult))
        then(nc.vector.tensor_tensor_scan(incl[:], one64[:, 0:NE], tot[:], 0.0, ALU.mult, ALU.add))
        then(tt(base[:], incl[:], tot[:], ALU.subtract))
        then(tt(rank[:], rank[:], over_t(base[:]), ALU.add))
        for r in range(2):
            then(tt(a[:], rank[:], oh[r][:], ALU.mult))
            then(nc.vector.tensor_reduce(cc[:], a[:], AX.X, ALU.add))
            nc.vector.tensor_copy(pos[r][:], cc[:]).then_inc(pos_ready, 1)
            dve.wait_ge(pos_ready, r + 1)
        then(tt(cmp_[:], start[:].unsqueeze(2).to_broadcast([1, NSLOT, NE]),
                incl[0:1].unsqueeze(1).to_broadcast([1, NSLOT, NE]), ALU.is_ge))
        then(nc.vector.tensor_reduce(cnt[:], cmp_[:], AX.X, ALU.add))
        then(nc.vector.tensor_scalar(slot_e[:], cnt[:], float(NE - 1), None, ALU.min))


def expert_stage(nc, ctx, sbt, Wg, Wu, Wd, xs_d, yo_d, ident, slot_e):
    def sb(name, shape, dt=F32):
        return sbt(ctx, name, shape, dt)

    def sem(name):
        return ctx.enter_context(nc.semaphore(name))

    wg = sb("wg_e", [P, NE, KT, INTER])
    wu = sb("wu_e", [P, NE, KT, INTER])
    wd = sb("wd_e", [P, NE, IT, D])
    xr = sb("xr", [P, 2, D])
    xT = sb("xT_e", [P, 2, KT, P])
    sg = sb("sg_e", [P, 2, INTER])
    h = sb("h_e", [P, 2, INTER])
    hT = sb("hT_e", [P, 2, IT, P])
    y = sb("y_e", [P, 2, D])
    ps_x = ctx.enter_context(nc.psum_tensor("ps_x", [P, KT, P], F32))
    ps_g = ctx.enter_context(nc.psum_tensor("ps_ge", [P, INTER], F32))
    ps_u = ctx.enter_context(nc.psum_tensor("ps_ue", [P, INTER], F32))
    ps_h = ctx.enter_context(nc.psum_tensor("ps_h", [P, IT, P], F32))
    ps_y = ctx.enter_context(nc.psum_tensor("ps_ye", [P, D], F32))

    w_loaded = sem("we_loaded")
    x_loaded = [sem(f"xe_loaded{r}") for r in range(2)]
    tx_ready = sem("tx_ready")
    xt_taken = sem("xte_taken")
    g_ready = sem("ge_ready")
    sg_ready = sem("sge_ready")
    u_ready = sem("ue_ready")
    h_ready = sem("he_ready")
    th_ready = sem("th_ready")
    ht_taken = sem("hte_taken")
    y_ready = sem("ye_ready")
    y_taken = sem("ye_taken")
    y_stored = [sem(f"ye_stored{r}") for r in range(2)]
    block = ctx.enter_context(nc.Block())

    xs_v = xs_d.rearrange("(s p) d -> s p d", p=P)
    yo_v = yo_d.rearrange("(s p) d -> s p d", p=P)

    def over_slots(eng, step):
        for s in range(3):
            step(Batch(0, s))
        with eng.Fori(0, (NSLOT - 5) // 2) as i:
            step(Batch(i, 3))
            step(Batch(i, 4))
        for s in range(NSLOT - 2, NSLOT + 1):
            step(Batch(0, s))

    def rows_of(view, s):
        return view[s.off] if s.fixed else view[bass.ds(s.v, 1)].rearrange("o p d -> (o p) d")

    @block.sync
    def _(sp):
        for r in range(2):
            sp.dma_start(xr[:, r], xs_v[r]).then_inc(x_loaded[r], 16)
        for e in range(NE):
            for t, src in ((wg, Wg), (wu, Wu), (wd, Wd)):
                sp.dma_start(t[:, e], src[e].rearrange("(k p) n -> p k n", p=P)).then_inc(w_loaded, 16)

        def step(s):
            if s.at_most(NSLOT - 3):
                sp.wait_ge(tx_ready, s.v + 1)
                sp.nop(nofuse=True)
                sp.dma_start(xr[:, s.par], rows_of(xs_v, s.plus(2))).then_inc(x_loaded[s.par], 16)
            if s.at_least(1):
                d = s.plus(-1)
                sp.wait_ge(y_taken, d.v + 1)
                sp.nop(nofuse=True)
                sp.dma_start(rows_of(yo_v, d), y[:, d.par]).then_inc(y_stored[d.par], 16)

        over_slots(sp, step)
        for r in range(2):
            sp.wait_ge(y_stored[r], (NSLOT + 1 - r) // 2 * 16)
            sp.nop(nofuse=True)

    @block.tensor
    def _(pe):
        def expert(s):
            at = slot_e[0:1, s.off:s.off + 1] if s.fixed else slot_e[0:1, bass.ds(s.v, 1)]
            return bass.ds(pe.value_load(at, min_val=0, max_val=NE - 1), 1)

        def weights(w, e, k):
            return w[:, e, k].rearrange("p o n -> p (o n)")

        def turn_rows(s):
            pe.wait_ge(x_loaded[s.par], (s.half() + 1) * 16)
            if s.at_least(1):
                pe.wait_ge(xt_taken, s.v)
            for k in range(KT):
                mm = nc.tensor.transpose(ps_x[:, k], xr[:, s.par, k * P:(k + 1) * P], ident[:])
            mm.then_inc(tx_ready, 1)

        def gate(s, e):
            pe.wait_ge(xt_taken, s.v + 1)
            if s.at_least(1):
                pe.wait_ge(sg_ready, s.v)
            for k in range(KT):
                mm = nc.tensor.matmul(ps_g[:], xT[:, s.par, k], weights(wg, e, k), start=k == 0, stop=k == KT - 1)
            mm.then_inc(g_ready, 1)

        def up(s, e):
            if s.at_least(1):
                pe.wait_ge(h_ready, s.v)
            for k in range(KT):
                mm = nc.tensor.matmul(ps_u[:], xT[:, s.par, k], weights(wu, e, k), start=k == 0, stop=k == KT - 1)
            mm.then_inc(u_ready, 1)

        def turn_hidden(s):
            pe.wait_ge(h_ready, s.v + 1)
            if s.at_least(1):
                pe.wait_ge(ht_taken, s.v)
            for k in range(IT):
                mm = nc.tensor.transpose(ps_h[:, k], h[:, s.par, k * P:(k + 1) * P], ident[:])
            mm.then_inc(th_ready, 1)

        def down(s):
            e = expert(s)
            pe.wait_ge(ht_taken, s.v + 1)
            if s.at_least(1):
                pe.wait_ge(y_taken, s.v)
            for k in range(IT):
                mm = nc.tensor.matmul(ps_y[:], hT[:, s.par, k], weights(wd, e, k), start=k == 0, stop=k == IT - 1)
            mm.then_inc(y_ready, 1)

        def step(s):
            if s.at_most(NSLOT - 2):
                turn_rows(s.plus(1))
            if s.at_most(NSLOT - 1):
                e = expert(s)
                gate(s, e)
            if s.at_least(1):
                turn_hidden(s.plus(-1))
            if s.at_most(NSLOT - 1):
                up(s, e)
            if s.at_least(1):
                down(s.plus(-1))

        turn_rows(Batch(0, 0))
        pe.wait_ge(w_loaded, NE * 3 * 16)
        over_slots(pe, step)

    @block.scalar
    def _(act):
        def step(s):
            if s.at_most(NSLOT - 1):
                act.wait_ge(g_ready, s.v + 1)
                if s.at_least(2):
                    act.wait_ge(h_ready, s.v - 1)
                nc.scalar.activation(sg[:, s.par], ps_g[:], ACT.Silu).then_inc(sg_ready, 1)
            if s.at_least(1):
                d = s.plus(-1)
                act.wait_ge(th_ready, d.v + 1)
                if d.at_least(2):
                    act.wait_ge(y_ready, d.v - 1)
                nc.scalar.activation(hT[:, d.par], ps_h[:], ACT.Copy).then_inc(ht_taken, 1)

        over_slots(act, step)

    @block.vector
    def _(dve):
        def take_rows(s):
            dve.wait_ge(tx_ready, s.v + 1)
            if s.at_least(2):
                dve.wait_ge(u_ready, s.v - 1)
            nc.vector.tensor_copy(xT[:, s.par], ps_x[:]).then_inc(xt_taken, 1)

        def step(s):
            if s.at_most(NSLOT - 2):
                take_rows(s.plus(1))
            if s.at_most(NSLOT - 1):
                dve.wait_ge(u_ready, s.v + 1)
                dve.wait_ge(sg_ready, s.v + 1)
                if s.at_least(2):
                    dve.wait_ge(th_ready, s.v - 1)
                nc.vector.tensor_tensor(h[:, s.par], sg[:, s.par], ps_u[:], ALU.mult).then_inc(h_ready, 1)
            if s.at_least(1):
                d = s.plus(-1)
                dve.wait_ge(y_ready, d.v + 1)
                if d.at_least(2):
                    dve.wait_ge(y_stored[d.par], d.half() * 16)
                nc.vector.tensor_copy(y[:, d.par], ps_y[:]).then_inc(y_taken, 1)

        take_rows(Batch(0, 0))
        over_slots(dve, step)


def combine_stage(nc, ctx, sbt, yo_d, ys_d, out_v, pos, wgt):
    def sb(name, shape, dt=F32):
        return sbt(ctx, name, shape, dt)

    def sem(name):
        return ctx.enter_context(nc.semaphore(name))

    acc = sb("acc", [P, 2, TT, D])
    yr = [[sb(f"yr{q}{r}", [P, D]) for r in range(2)] for q in range(TT)]
    ix = [[sb(f"ix{q}{r}", [P, 1], I32) for r in range(2)] for q in range(TT)]
    acc_loaded = [sem(f"acc_loaded{r}") for r in range(2)]
    stored = [sem(f"stored{r}") for r in range(2)]
    staged = sem("ix_staged")
    gathered = [sem(f"gathered{q}") for q in range(TT)]
    half_done = sem("half_done")
    tile_done = sem("tile_done")
    block = ctx.enter_context(nc.Block())
    ys_v = ys_d.rearrange("(c t) p d -> c p t d", t=TT)

    def batch_of(view, b):
        return view[b.off] if b.fixed else view[bass.ds(b.v, 1)].rearrange("o p t d -> (o p) t d")

    def over_pairs(eng, step):
        step(Batch(0, 0))
        step(Batch(0, 1))
        with eng.Fori(0, NB // 2 - 1) as i:
            step(Batch(i, 2))
            step(Batch(i, 3))

    @block.sync
    def _(sp):
        def step(b):
            if b.at_least(2):
                sp.wait_ge(stored[b.par], b.half() * 16)
                sp.nop(nofuse=True)
            sp.dma_start(acc[:, b.par], batch_of(ys_v, b)).then_inc(acc_loaded[b.par], 16)

        over_pairs(sp, step)

    @block.scalar
    def _(act):
        def step(b):
            act.wait_ge(tile_done, b.v * TT + TT)
            act.dma_start(batch_of(out_v, b), acc[:, b.par]).then_inc(stored[b.par], 16)

        over_pairs(act, step)
        for r in range(2):
            act.wait_ge(stored[r], NB // 2 * 16)

    @block.gpsimd
    def _(pool):
        def stage(b, q):
            if b.at_least(1):
                pool.wait_ge(tile_done, b.v * TT + q - TT + 1)
                pool.wait_ge(staged, (b.v * TT + q) * 2)
            k = slice(b.off * TT + q, b.off * TT + q + 1) if b.fixed else bass.ds(b.v * TT + q, 1)
            for r in range(2):
                nc.gpsimd.tensor_copy(ix[q][r][:], pos[r][:, k]).then_inc(staged, 1)

        def gather(q):
            for r in range(2):
                nc.gpsimd.indirect_dma_start(yr[q][r][:], None, yo_d[:, :],
                                             bass.IndirectOffsetOnAxis(ap=ix[q][r][:, 0:1], axis=0))\
                    .then_inc(gathered[q], 16)

        def step(b):
            for q in range(TT):
                if b.fixed and b.off == 0 and q == 0:
                    continue
                stage(b, q)
                if b.fixed and b.off == 0:
                    pool.wait_ge(staged, q * 2)
                gather((q - 1) % TT)

        stage(Batch(0, 0), 0)
        over_pairs(pool, step)
        pool.wait_ge(staged, NT * 2)
        gather(TT - 1)

    @block.vector
    def _(dve):
        def step(b):
            dve.wait_ge(acc_loaded[b.par], (b.half() + 1) * 16)
            for q in range(TT):
                dve.wait_ge(gathered[q], b.v * 32 + 32)
                k = slice(b.off * TT + q, b.off * TT + q + 1) if b.fixed else bass.ds(b.v * TT + q, 1)
                nc.vector.scalar_tensor_tensor(out=acc[:, b.par, q], in0=yr[q][0][:], scalar=wgt[0][:, k],
                                               in1=acc[:, b.par, q], op0=ALU.mult, op1=ALU.add).then_inc(half_done, 1)
                dve.wait_ge(half_done, b.v * TT + q + 1)
                nc.vector.scalar_tensor_tensor(out=acc[:, b.par, q], in0=yr[q][1][:], scalar=wgt[1][:, k],
                                               in1=acc[:, b.par, q], op0=ALU.mult, op1=ALU.add).then_inc(tile_done, 1)

        over_pairs(dve, step)


def kernel(**inputs):
    import numpy as _np
    import concourse.bacc as _bacc
    from concourse import mybir as _mybir
    from concourse.bass_utils import run_bass_kernel_spmd as _run

    ins = ["L0_attn_x", "L0_attn_Wq", "L0_attn_bq", "L0_attn_Wk", "L0_attn_bk", "L0_attn_Wv", "L0_attn_bv",
           "L0_attn_Wo", "L0_attn_bo", "L0_attn_J_attn", "L0_attn_lambda_attn", "L0_ffn_ln_scale", "L0_ffn_ln_bias",
           "L0_ffn_gate_w", "L0_ffn_Wg", "L0_ffn_Wu", "L0_ffn_Wd", "L0_ffn_sWg", "L0_ffn_sWu", "L0_ffn_sWd"]
    turned = {"L0_attn_Wq", "L0_attn_Wk", "L0_attn_Wv", "L0_attn_Wo", "L0_ffn_gate_w"}
    nc = _bacc.Bacc("TRN2", target_bir_lowering=False, num_devices=1)
    arrays, args = {}, []
    for name in ins:
        a = _np.asarray(inputs[name])
        if name in turned:
            a = a.T
        if a.ndim == 0:
            a = a.reshape(1)
        a = _np.ascontiguousarray(a)
        arrays[f"in_{name}_dram"] = a
        args.append(nc.dram_tensor(f"in_{name}_dram", a.shape, _mybir.dt.from_np(a.dtype), kind="ExternalInput").ap())
    args.append(nc.dram_tensor("out_0_dram", (NB, S, D), F32, kind="ExternalOutput").ap())
    build(nc, *args)
    r = _run(nc, [arrays], core_ids=[0])
    return r.results[0]["out_0_dram"]
```

```python
import concourse.bass as bass
from concourse import mybir
from contextlib import ExitStack


F32 = mybir.dt.float32
F32R = mybir.dt.float32r
BF16 = mybir.dt.bfloat16
I32 = mybir.dt.int32
ALU = mybir.AluOpType
ACT = mybir.ActivationFunctionType
AX = mybir.AxisListType

P = 128
NB, S, D = 16, 512, 256
H, HD = 16, 16
KT = D // P
TT = S // P
NT = NB * TT
HG = 4
G = H // HG
PG = P // HD
NE, INTER = 8, 512
IT = INTER // P
EPS = 1e-5
MASK = -1e30
NSLOT = 2 * NT + NE - 1
ZR = 3
LEAD = 7
STEPS = G * TT
STACK = 3 * 2 * HD
MROW = STACK
LOADS = 16 * 12
PROLOGUE, TAIL = -1, NB
SHARED_FIRST = 9


class Batch:

    def __init__(self, i, off):
        self.i, self.off = i, off
        self.v = off if isinstance(i, int) and i == 0 else i * 2 + off
        self.par = off % 2
        self.fixed = isinstance(i, int)

    def plus(self, k):
        return Batch(self.i, self.off + k)

    def half(self):
        return self.off // 2 if self.fixed else self.i + self.off // 2

    def at_least(self, n):
        return (not self.fixed) or self.off >= n

    def at_most(self, n):
        return (not self.fixed) or self.off <= n


def over_batches(eng, batch):
    batch(Batch(0, PROLOGUE))
    batch(Batch(0, 0))
    with eng.Fori(0, NB // 2 - 2) as i:
        batch(Batch(i, 1))
        batch(Batch(i, 2))
    for last in (NB - 3, NB - 2, NB - 1, TAIL):
        batch(Batch(0, last))


PIECES = [
    (0, 0, "xt", 0, 1), (0, 1, "xt", 1, 1),
    (1, 0, "ot", 3, -1), (1, 1, "mt", 1, 0),
    (2, 0, "k", 0, 1), (2, 1, "k", 1, 1),
    (3, 0, "q", 0, 1), (3, 1, "q", 1, 1),
    (4, 0, "qj", 0, 1), (4, 1, "qj", 1, 1),
    (5, 0, "ot", 0, 0), (5, 1, "mt", 2, 0),
    (6, 1, "v", 0, 1),
    (7, 1, "v", 1, 1),
    (8, 0, "ont", 0, -1),
    (9, 0, "ot", 1, 0), (9, 1, "mt", 3, 0),
    (10, 0, "ont", 1, -1),
    (11, 0, "out", 0, -1),
    (12, 0, "out", 1, -1),
    (13, 0, "ot", 2, 0), (13, 1, "mt", 0, 1),
]
PER_BATCH = {"xt": 2, "k": 2, "q": 2, "qj": 2, "v": 2, "mt": G, "ot": G, "ont": 2, "out": 2}


def piece_exists(b, rel):
    d = b.plus(rel)
    return d.at_least(0) and d.at_most(NB - 1)


def pieces_at(b, n, place):
    found = []
    for at, (step, pl, kind, j, rel) in enumerate(PIECES):
        if step == n and pl == place and piece_exists(b, rel):
            found.append((kind, j, b.plus(rel), piece_before(b, at)))
    return found


def piece_before(b, at):
    for bb, upto in ((b, at), (b.plus(-1), len(PIECES))):
        if bb.fixed and bb.off < PROLOGUE:
            return None
        for _, _, kind, j, rel in reversed(PIECES[:upto]):
            if piece_exists(bb, rel):
                return kind, j, bb.plus(rel)
    return None


def slot(d, g):
    return HG * (2 * d.par + g if g < 2 else 2 + g)


def build(nc, x, wqT, bq, wkT, bk, wvT, bv, woT, bo, J, lam, lns, lnb, gwT, Wg, Wu, Wd, sWg, sWu, sWd, out):
    x_v = x.rearrange("b (t p) d -> b p t d", p=P)
    k_parts = nc.dram_tensor("k_parts", [2, 2, 2, H, HD, S], F32, kind="Internal").ap()
    q_parts = nc.dram_tensor("q_parts", [2, 2, 2, H, HD, S], F32, kind="Internal").ap()
    x1_d = nc.dram_tensor("x1_d", [NB, P, TT, D], F32, kind="Internal").ap()
    ys_d = nc.dram_tensor("ys_d", [NT, P, D], F32, kind="Internal").ap()
    xs_d = nc.dram_tensor("xs_d", [NSLOT * P, D], F32, kind="Internal").ap()
    yo_d = nc.dram_tensor("yo_d", [NSLOT * P, D], F32, kind="Internal").ap()

    top = ExitStack()
    with top:
        def sbt(ctx, name, shape, dt=F32):
            return ctx.enter_context(nc.sbuf_tensor(name, shape, dt))

        ident = sbt(top, "ident", [P, P])
        ones = sbt(top, "ones", [P, P])
        mv2 = sbt(top, "mv2", [P, NT, 2])
        eps = sbt(top, "eps", [P, 1])
        xs_zeroed = top.enter_context(nc.semaphore("xs_zeroed"))

        with ExitStack() as c:
            attention_stage(nc, c, sbt, x_v, wqT, bq, wkT, bk, wvT, bv, woT, bo, J, lam,
                            k_parts, q_parts, x1_d, xs_d, ident, ones, mv2, eps, xs_zeroed)
        with ExitStack() as c:
            moe_stages(nc, c, sbt, lns, lnb, gwT, Wg, Wu, Wd, sWg, sWu, sWd, out,
                       x1_d, ys_d, xs_d, yo_d, ident, ones, mv2, eps)


def attention_stage(nc, ctx, sbt, x_v, wqT, bq, wkT, bk, wvT, bv, woT, bo, J, lam,
                    k_parts, q_parts, x1_d, xs_d, ident, ones, mv2, eps, xs_zeroed):
    def sb(name, shape, dt=F32):
        return sbt(ctx, name, shape, dt)

    def sem(name):
        return ctx.enter_context(nc.semaphore(name))

    wq = sb("wq", [P, KT, D])
    wk = sb("wk", [P, KT, D])
    wv = sb("wv", [P, KT, D])
    wo = sb("wo", [P, KT, D])
    bq_c = sb("bq_c", [P, 2])
    bk_c = sb("bk_c", [P, 2])
    bv_b = sb("bv_b", [P, D])
    bo_b = sb("bo_b", [P, D])
    lam_b = sb("lam_b", [P, 1])
    jb = sb("jb", [P, 2, P])
    ident_bf = sb("ident_bf", [P, P], BF16)
    mask_bf = sb("mask_bf", [P, P], BF16)
    mv1 = sb("mv1", [P, NT, 2])
    rstd1 = sb("rstd1", [P, NT])
    st1 = sb("st1", [P, 2, TT, 6])
    zrows = sb("zrows", [P, ZR * D])
    pace_v = sb("pace_v", [1, 1])

    with ExitStack() as c1:
        mvt = sbt(c1, "mvt", [P, 2, TT, 2])
        xs1 = sbt(c1, "xs1", [P, 4, TT, D])
        s_w = c1.enter_context(nc.semaphore("s_w"))
        s_j = c1.enter_context(nc.semaphore("s_j"))
        s_x = [c1.enter_context(nc.semaphore(f"s_x{r}")) for r in range(4)]
        s_jz = c1.enter_context(nc.semaphore("s_jz"))
        s_id0 = c1.enter_context(nc.semaphore("s_id0"))
        s_id = c1.enter_context(nc.semaphore("s_id"))
        s_st = c1.enter_context(nc.semaphore("s_st"))
        s_ag = c1.enter_context(nc.semaphore("s_ag"))
        s_cp = c1.enter_context(nc.semaphore("s_cp"))
        s_ep = c1.enter_context(nc.semaphore("s_ep"))
        s_sq = c1.enter_context(nc.semaphore("s_sq"))
        block = c1.enter_context(nc.Block())

        @block.sync
        def _(sp):
            for r in range(4):
                sp.dma_start(xs1[:, r], x_v[r]).then_inc(s_x[r], 16)
            with sp.Fori(1, NB // 4) as i:
                for r in range(4):
                    sp.wait_ge(s_st, (i - 1) * 16 + 4 * r + 4)
                    sp.nop(nofuse=True)
                    sp.dma_start(xs1[:, r], x_v[bass.ds(i * 4 + r, 1)].rearrange("o p t d -> (o p) t d")).then_inc(s_x[r], 16)
            sp.wait_ge(s_w, 16 * 11)
            sp.nop(nofuse=True)
            sp.wait_ge(s_j, 16 * H)
            sp.nop(nofuse=True)

        @block.scalar
        def _(act):
            for t, src in ((wq, wqT), (wk, wkT), (wv, wvT), (wo, woT)):
                act.dma_start(t[:], src.rearrange("(k p) n -> p k n", p=P)).then_inc(s_w, 16)
            for g in range(2):
                for t, src in ((bq_c, bq), (bk_c, bk)):
                    act.dma_start(t[:, g:g + 1], src[g * P:(g + 1) * P].rearrange("(p o) -> p o", o=1)).then_inc(s_w, 16)
            act.dma_start(bv_b[:], bv.rearrange("(o n) -> o n", o=1).to_broadcast([P, D])).then_inc(s_w, 16)
            act.dma_start(bo_b[:], bo.rearrange("(o n) -> o n", o=1).to_broadcast([P, D])).then_inc(s_w, 16)
            act.dma_start(lam_b[:], lam.rearrange("(o n) -> o n", o=1).to_broadcast([P, 1])).then_inc(s_w, 16)
            act.wait_ge(s_jz, 1)
            for h in range(H):
                r = (h % PG) * HD
                act.dma_start(jb[r:r + HD, h // PG, r:r + HD], J[h]).then_inc(s_j, 16)
            act.wait_ge(s_ep, 1)
            act.wait_ge(s_cp, NB)
            nc.scalar.activation(rstd1[:], mv1[:, :, 1], ACT.Sqrt, bias=eps[:, 0:1]).then_inc(s_sq, 1)

        @block.gpsimd
        def _(pool):
            nc.gpsimd.memset(jb[:], 0.0).then_inc(s_jz, 1)
            nc.gpsimd.memset(zrows[:], 0.0)
            nc.gpsimd.memset(ident[:], 0.0).then_inc(s_id0, 1)
            nc.gpsimd.memset(ident_bf[:], 0.0).then_inc(s_id0, 1)
            nc.gpsimd.memset(mask_bf[:], 0.0).then_inc(s_id0, 1)
            nc.gpsimd.memset(ones[:], 1.0).then_inc(s_id0, 1)
            pool.wait_ge(s_id0, 4)
            for t in (ident, ident_bf):
                nc.gpsimd.affine_select(out=t[:], in_=t[:], compare_op=ALU.not_equal, fill=1.0, base=0,
                                        pattern=[[-1, P]], channel_multiplier=1).then_inc(s_id, 1)
            nc.gpsimd.affine_select(out=mask_bf[:], in_=mask_bf[:], compare_op=ALU.is_ge, fill=MASK, base=0,
                                    pattern=[[-1, P]], channel_multiplier=1).then_inc(s_id, 1)
            pool.wait_ge(s_w, 16 * 11)
            pool.wait_ge(s_j, 16 * H)
            nc.gpsimd.tensor_scalar(jb[:], jb[:], lam_b[:, 0:1], None, ALU.mult).then_inc(s_id, 1)

        @block.vector
        def _(dve):
            nc.vector.memset(eps[:], EPS).then_inc(s_ep, 1)

            def stats(i, r, first):
                dve.wait_ge(s_x[r], i * 16 + 16 if not first else 16)
                for t in range(TT):
                    if not (first and r < 2):
                        dve.wait_ge(s_ag, (i * 16 if not first else 0) + 4 * r - 4)
                    nc.vector.bn_stats(st1[:, r % 2, t], xs1[:, r, t]).then_inc(s_st, 1)
                dve.wait_ge(s_st, (i * 16 if not first else 0) + 4 * r + TT)
                nc.vector.tensor_copy(pace_v[:], eps[0:1])
                for t in range(TT):
                    a = nc.vector.bn_aggr(mvt[:, r % 2, t], st1[:, r % 2, t])
                a.then_inc(s_ag, 4)
                dve.wait_ge(s_ag, (i * 16 if not first else 0) + 4 * r + TT)
                nc.vector.tensor_copy(mv1[:, 4 * r:4 * r + TT] if first else mv1[:, bass.ds(i * 16 + 4 * r, TT)], mvt[:, r % 2])\
                    .then_inc(s_cp, 1)

            for r in range(4):
                stats(0, r, True)
            with dve.Fori(1, NB // 4) as i:
                for r in range(4):
                    stats(i, r, False)
            dve.wait_ge(s_sq, 1)
            nc.vector.reciprocal(rstd1[:], rstd1[:])

    qs = sb("qs", [P, 6 * HG, S], F32R)
    ks = sb("ks", [P, 6 * HG, S], F32R)
    xn = sb("xn", [P, TT, D])
    xT = sb("xT", [P, KT, S])
    lin = sb("lin", [P, 2, S])
    th = sb("th", [P, 2, S])
    part = {n: sb("part_" + n, [P, 2, S], F32R) for n in ("kh", "kl", "th", "tl")}
    vt = sb("vt", [P, 2, TT, H, 2 * HD])
    probs = sb("probs", [P, 2, HG, S])
    mx = sb("mx", [P, 2, TT, HG])
    nm = sb("nm", [P, TT, P], F32R)
    mT = sb("mT", [P, S], F32R)
    osb = sb("osb", [P, S])
    rec = sb("rec", [P, TT, HG])
    on = sb("on", [P, 2, TT, D])
    onT = sb("onT", [P, KT, S])
    xres = sb("xres", [P, TT, D])
    st2 = sb("st2", [P, TT, 6])
    mvs = sb("mvs", [P, TT, 2])
    pace = sb("pace", [1, 2])

    ps_rows = [ctx.enter_context(nc.psum_tensor(f"ps_rows{r}", [P, S], F32)) for r in range(2)]
    ps_cols = [ctx.enter_context(nc.psum_tensor(f"ps_cols{r}", [P, 2, S], F32)) for r in range(2)]
    ps_o = ctx.enter_context(nc.psum_tensor("ps_o", [P, S], F32))
    ps_m = ctx.enter_context(nc.psum_tensor("ps_m", [P, S], F32))

    rows_ready = sem("rows_ready")
    max_done = sem("max_done")
    nm_ready = sem("nm_ready")
    nmh_ready = sem("nmh_ready")
    mrow_loaded = sem("mrow_loaded")
    cols_ready = sem("cols_ready")
    exp_done = sem("exp_done")
    sel_done = sem("sel_done")
    pv_done = sem("pv_done")
    o_taken = sem("o_taken")
    ready = {k: sem(k + "_ready") for k in PER_BATCH}
    taken = {k: sem(k + "_taken") for k in PER_BATCH}
    x_loaded = sem("x_loaded")
    xn_ready = sem("xn_ready")
    xres_loaded = sem("xres_loaded")
    xres_ready = sem("xres_ready")
    kth_done = sem("kth_done")
    hi_done = sem("hi_done")
    thi_done = sem("thi_done")
    lo_done = sem("lo_done")
    tlo_done = sem("tlo_done")
    lin_out = [sem(f"lin_out{r}") for r in range(2)]
    tan_out = [sem(f"tan_out{r}") for r in range(2)]
    stack01 = [sem(f"stack01_{r}") for r in range(2)]
    stack23 = [sem(f"stack23_{r}") for r in range(2)]
    rec_ready = sem("rec_ready")
    x1_stored = [sem(f"x1_stored{r}") for r in range(2)]
    st2_ready = sem("st2_ready")
    mvs_ready = sem("mvs_ready")
    const_ready = sem("const_ready")

    def count(kind, j, b):
        return b.v * PER_BATCH[kind] + j + 1

    def unit(b, n):
        m = n + LEAD
        return b.plus(m // STEPS), (m % STEPS) // TT, m % TT

    block = ctx.enter_context(nc.Block())

    @block.tensor
    def _(pe):
        def piece(b, n, place):
            for kind, j, d, before in pieces_at(b, n, place):
                if before:
                    pe.wait_ge(taken[before[0]], count(*before))
                if kind == "xt":
                    pe.wait_ge(xn_ready, d.v + 1)
                    for t in range(TT):
                        mm = nc.tensor.transpose(ps_m[:, t * P:(t + 1) * P], xn[:, t, j * P:(j + 1) * P], ident[:])
                elif kind in ("k", "q"):
                    pe.wait_ge(taken["xt"], count("xt", 1, d))
                    w = wk if kind == "k" else wq
                    for k in range(KT):
                        mm = nc.tensor.matmul(ps_m[:], w[:, k, j * P:(j + 1) * P], xT[:, k], start=k == 0, stop=k == KT - 1)
                elif kind == "qj":
                    pe.wait_ge(kth_done, d.v * 4 + 3 + j)
                    mm = nc.tensor.matmul(ps_m[:], jb[:, j], th[:, j], start=True, stop=True)
                elif kind == "v":
                    for tt in range(2):
                        t = 2 * j + tt
                        for k in range(KT):
                            mm = nc.tensor.matmul(ps_m[:, tt * D:(tt + 1) * D], xT[:, k, t * P:(t + 1) * P], wv[:, k],
                                                  start=k == 0, stop=k == KT - 1)
                elif kind == "mt":
                    pe.wait_ge(nm_ready, d.v * G + j + 1)
                    for t in range(TT):
                        mm = nc.tensor.transpose(ps_m[:, t * P:(t + 1) * P], nm[:, t].bitcast(F32), ident[:])
                elif kind == "ot":
                    pe.wait_ge(o_taken, d.v * G + j + 1)
                    for t in range(TT):
                        mm = nc.tensor.transpose(ps_m[:, t * P:(t + 1) * P], osb[:, t * P:(t + 1) * P], ident[:])
                elif kind == "ont":
                    pe.wait_ge(taken["ot"], count("ot", G - 1, d))
                    for t in range(TT):
                        mm = nc.tensor.transpose(ps_m[:, t * P:(t + 1) * P], on[:, d.par, t, j * P:(j + 1) * P], ident[:])
                elif kind == "out":
                    pe.wait_ge(taken["ont"], count("ont", 1, d))
                    for tt in range(2):
                        t = 2 * j + tt
                        for k in range(KT):
                            mm = nc.tensor.matmul(ps_m[:, tt * D:(tt + 1) * D], onT[:, k, t * P:(t + 1) * P], wo[:, k],
                                                  start=k == 0, stop=k == KT - 1)
                mm.then_inc(ready[kind], 1)

        def rows(b, n, h):
            d, g, it = unit(b, n)
            if not (d.at_least(0) and d.at_most(NB - 1)):
                return
            first = d.fixed and d.off == 0 and g == 0 and it == 0 and h < 2
            if g != 1 and it == 0 and h == 0:
                if g == 0:
                    pe.wait_ge(stack01[d.par], (d.half() + 1) * LOADS)
                else:
                    pe.wait_ge(stack23[g - 2], (d.v + 1) * LOADS)
            if not first:
                pe.wait_ge(max_done, d.v * (STEPS * HG) + (g * TT + it) * HG + h - 1)
            hh = slot(d, g) + h
            bank = ps_rows[h % 2]
            nc.tensor.matmul(bank[:, 0:(it + 1) * P], qs[0:STACK, hh, it * P:(it + 1) * P],
                             ks[0:STACK, hh, 0:(it + 1) * P], start=True, stop=False)
            nc.tensor.matmul(bank[:, it * P:(it + 1) * P], ident_bf[:], mask_bf[:], start=False, stop=True)\
                .then_inc(rows_ready, 1)

        def cols(b, n, pair):
            g, jt = n // TT, n % TT
            if pair == 0 and jt == 0:
                pe.wait_ge(mrow_loaded, (b.v * G + g + 1) * 16 * HG)
            if not (b.fixed and b.off == 0 and n == 0):
                pe.wait_ge(exp_done, (b.v * STEPS + n) * 2 + pair - 1)
            for e in range(2):
                hh = slot(b, g) + 2 * pair + e
                mm = nc.tensor.matmul(ps_cols[pair][:, e, jt * P:S], ks[0:MROW + 2, hh, jt * P:(jt + 1) * P],
                                      qs[0:MROW + 2, hh, jt * P:S], start=True, stop=True)
            mm.then_inc(cols_ready, 1)

        def pv(b, n):
            g, jt = n // TT, n % TT
            pe.wait_ge(sel_done, b.v * STEPS + n + 1)
            if n == 0:
                pe.wait_ge(taken["v"], count("v", 1, b))
            if jt == 0 and not (b.fixed and b.off == 0 and g == 0):
                pe.wait_ge(o_taken, b.v * G + g)
            for h in range(HG):
                mm = nc.tensor.matmul(ps_o[2 * HD * h:2 * HD * (h + 1), jt * P:S], vt[:, b.par, jt, g * HG + h],
                                      probs[:, n % 2, h, jt * P:S], start=jt == 0, stop=jt == TT - 1)
            mm.then_inc(pv_done, 1)

        def batch(b):
            att = b.at_least(0) and b.at_most(NB - 1)
            for n in range(STEPS):
                rows(b, n, 0)
                if att:
                    cols(b, n, 0)
                rows(b, n, 1)
                piece(b, n, 0)
                rows(b, n, 2)
                if att:
                    cols(b, n, 1)
                rows(b, n, 3)
                if n > 0 and att:
                    pv(b, n - 1)
                if n == 0 and b.at_least(1):
                    pv(b.plus(-1), STEPS - 1)
                piece(b, n, 1)

        pe.wait_ge(const_ready, 3)
        over_batches(pe, batch)

    @block.scalar
    def _(act):
        def piece(b, n, place):
            for kind, j, d, _ in pieces_at(b, n, place):
                if kind == "xt":
                    act.wait_ge(ready[kind], count(kind, j, d))
                    nc.scalar.activation(xT[:, j], ps_m[:], ACT.Copy).then_inc(taken[kind], 1)
                elif kind in ("k", "q"):
                    c = 0 if kind == "k" else 2
                    act.wait_ge(taken[kind], count(kind, j, d))
                    if kind == "k":
                        if d.at_least(1):
                            act.wait_ge(ready["qj"], d.v * 2 + j - 1)
                    else:
                        act.wait_ge(tlo_done, d.v * 2 + 1 + j)
                    nc.scalar.activation(th[:, j], lin[:, j], ACT.Tanh, scale=1.0 if kind == "k" else 4.0)\
                        .then_inc(kth_done, 1)
                    if kind == "q" or d.at_least(1):
                        act.wait_ge(lin_out[j], (d.v * 2 + c // 2) * 32)
                    nc.scalar.activation(part["kh"][:, j], lin[:, j], ACT.Copy).then_inc(hi_done, 1)
                    if kind == "k":
                        if d.at_least(1):
                            act.wait_ge(tan_out[j], d.v * 64)
                        act.wait_ge(kth_done, d.v * 4 + j + 1)
                        nc.scalar.activation(part["th"][:, j], th[:, j], ACT.Copy).then_inc(thi_done, 1)
                elif kind == "qj":
                    act.wait_ge(ready[kind], count(kind, j, d))
                    act.wait_ge(tan_out[j], d.v * 64 + 32)
                    nc.scalar.activation(part["th"][:, j], ps_m[:], ACT.Copy).then_inc(thi_done, 1)
                elif kind == "mt":
                    act.wait_ge(ready[kind], count(kind, j, d))
                    if j > 0 or d.at_least(1):
                        act.wait_ge(mrow_loaded, (d.v * G + j) * 16 * HG)
                    nc.scalar.activation(mT[0:2 * HG], ps_m[0:2 * HG], ACT.Copy).then_inc(taken[kind], 1)
                elif kind == "ont":
                    act.wait_ge(ready[kind], count(kind, j, d))
                    nc.scalar.activation(onT[:, j], ps_m[:], ACT.Copy).then_inc(taken[kind], 1)

        def exps(b, n, pair):
            g, jt = n // TT, n % TT
            act.wait_ge(cols_ready, (b.v * STEPS + n) * 2 + pair + 1)
            if pair == 0 and not (b.fixed and b.off == 0 and n < 2):
                act.wait_ge(pv_done, b.v * STEPS + n - 1)
            nc.scalar.activation(probs[:, n % 2, 2 * pair:2 * pair + 2, jt * P:S], ps_cols[pair][:, :, jt * P:S],
                                 ACT.Exp).then_inc(exp_done, 1)

        def o_copy(b, g):
            act.wait_ge(pv_done, b.v * STEPS + (g + 1) * TT)
            if g > 0 or b.at_least(1):
                act.wait_ge(ready["ot"], b.v * G + g)
            nc.scalar.activation(osb[:], ps_o[:], ACT.Copy).then_inc(o_taken, 1)

        def batch(b):
            att = b.at_least(0) and b.at_most(NB - 1)
            for n in range(STEPS):
                if att:
                    exps(b, n, 0)
                piece(b, n, 0)
                if att:
                    exps(b, n, 1)
                if n % TT == 0:
                    if n > 0 and att:
                        o_copy(b, n // TT - 1)
                    if n == 0 and b.at_least(1):
                        o_copy(b.plus(-1), G - 1)
                piece(b, n, 1)

        over_batches(act, batch)

    @block.vector
    def _(dve):
        def layer_norm(d):
            dve.wait_ge(x_loaded, (d.v + 1) * 16)
            for t in range(TT):
                if d.fixed:
                    m, r = mv1[:, d.off * TT + t, 0:1], rstd1[:, d.off * TT + t:d.off * TT + t + 1]
                else:
                    m = mv1[:, bass.ds(d.v * TT + t, 1), 0]
                    r = rstd1[:, bass.ds(d.v * TT + t, 1)]
                ts = nc.vector.tensor_scalar(xn[:, t], xn[:, t], m, r, ALU.subtract, ALU.mult)
            ts.then_inc(xn_ready, 1)

        def maximum(b, n, h):
            d, g, it = unit(b, n)
            if not (d.at_least(0) and d.at_most(NB - 1)):
                return
            gb = g % 2
            dve.wait_ge(rows_ready, d.v * (STEPS * HG) + (g * TT + it) * HG + h + 1)
            nc.vector.tensor_reduce(mx[:, gb, it, h:h + 1], ps_rows[h % 2][:, 0:(it + 1) * P], AX.X, ALU.max)\
                .then_inc(max_done, 1)
            if it == TT - 1 and h == HG - 1:
                dve.wait_ge(max_done, d.v * (STEPS * HG) + (g + 1) * TT * HG)
                if g > 0 or d.at_least(1):
                    dve.wait_ge(ready["mt"], d.v * G + g)
                pair = nm[:, :, 0:2 * HG].rearrange("p t (h two) -> p t h two", two=2)
                nc.vector.tensor_scalar(pair[:, :, :, 0], mx[:, gb], -1.0, None, ALU.mult).then_inc(nmh_ready, 1)
                dve.wait_ge(nmh_ready, d.v * G + g + 1)
                nc.vector.scalar_tensor_tensor(out=pair[:, :, :, 1], in0=mx[:, gb], scalar=-1.0,
                                               in1=pair[:, :, :, 0].bitcast(F32), op0=ALU.mult, op1=ALU.subtract)\
                    .then_inc(nm_ready, 1)

        def piece(b, n, place):
            for kind, j, d, _ in pieces_at(b, n, place):
                if kind in ("xt", "mt", "ont"):
                    continue
                dve.wait_ge(ready[kind], count(kind, j, d))
                if kind == "k":
                    if d.at_least(1):
                        dve.wait_ge(lo_done, d.v * 4 - 1 + j)
                    nc.vector.tensor_scalar(lin[:, j], ps_m[:], bk_c[:, j:j + 1], None, ALU.add).then_inc(taken[kind], 1)
                elif kind == "q":
                    dve.wait_ge(lo_done, d.v * 4 + 1 + j)
                    nc.vector.tensor_scalar(lin[:, j], ps_m[:], bq_c[:, j:j + 1], 0.25, ALU.add, ALU.mult)\
                        .then_inc(taken[kind], 1)
                elif kind == "qj":
                    dve.wait_ge(thi_done, d.v * 4 + 3 + j)
                    dve.wait_ge(tan_out[j], d.v * 64 + 32)
                    nc.vector.tensor_tensor(part["tl"][:, j], ps_m[:], part["th"][:, j].bitcast(F32), ALU.subtract)\
                        .then_inc(taken[kind], 1)
                elif kind == "v":
                    for tt in range(2):
                        a = nc.vector.tensor_tensor(
                            vt[:, d.par, 2 * j + tt, :, 0:HD],
                            ps_m[:, tt * D:(tt + 1) * D].rearrange("p (h e) -> p h e", h=H),
                            bv_b[:].rearrange("p (h e) -> p h e", h=H), ALU.add)
                    a.then_inc(taken[kind], 1)
                elif kind == "ot":
                    pso = ps_m[:].rearrange("p (t h e) -> p t h e", t=TT, h=HG)
                    nc.vector.reciprocal(rec[:], pso[:, :, :, HD]).then_inc(rec_ready, 1)
                    dve.wait_ge(rec_ready, d.v * G + j + 1)
                    nc.vector.tensor_tensor(
                        on[:, d.par, :, j * HG * HD:(j + 1) * HG * HD].rearrange("p t (h e) -> p t h e", h=HG),
                        pso[:, :, :, 0:HD], rec[:].unsqueeze(3).to_broadcast([P, TT, HG, HD]), ALU.mult)\
                        .then_inc(taken[kind], 1)
                elif kind == "out":
                    dve.wait_ge(xres_ready, d.v + 1)
                    x1 = xres[:, 2 * j:2 * j + 2]
                    nc.vector.tensor_tensor(x1, ps_m[:].rearrange("p (t e) -> p t e", t=2), x1, ALU.add)\
                        .then_inc(taken[kind], 1)

        def statistics(d, t):
            if t == 0 or t == 2:
                dve.wait_ge(taken["out"], count("out", t // 2, d))
            nc.vector.bn_stats(st2[:, t], xres[:, t]).then_inc(st2_ready, 1)
            if t == TT - 1:
                dve.wait_ge(st2_ready, (d.v + 1) * TT)
                nc.vector.tensor_copy(pace_v[:], eps[0:1])
                for k in range(TT):
                    s_ = nc.vector.bn_aggr(mvs[:, k], st2[:, k])
                s_.then_inc(mvs_ready, 1)
                dve.wait_ge(mvs_ready, d.v + 1)
                at = d.v * TT
                nc.vector.tensor_copy(mv2[:, at:at + TT] if d.fixed else mv2[:, bass.ds(at, TT)], mvs[:])

        def batch(b):
            for n in range(STEPS):
                maximum(b, n, 0)
                maximum(b, n, 1)
                piece(b, n, 0)
                maximum(b, n, 2)
                maximum(b, n, 3)
                piece(b, n, 1)
                if 11 <= n < 11 + TT and piece_exists(b, -1):
                    statistics(b.plus(-1), n - 11)
                if n == 9 and b.plus(2).at_most(NB - 1):
                    layer_norm(b.plus(2))

        layer_norm(Batch(0, 0))
        nc.vector.memset(nm[:].bitcast(F32), 0.0).then_inc(const_ready, 1)
        nc.vector.memset(vt[:, :, :, :, HD:2 * HD], 1.0).then_inc(const_ready, 1)
        over_batches(dve, batch)

    @block.gpsimd
    def _(pool):
        def piece(b, n, place):
            for kind, j, d, _ in pieces_at(b, n, place):
                if kind in ("k", "q"):
                    c = 0 if kind == "k" else 2
                    pool.wait_ge(hi_done, d.v * 4 + c + j + 1)
                    if kind == "q" or d.at_least(1):
                        pool.wait_ge(lin_out[j], (d.v * 2 + c // 2) * 32)
                    nc.gpsimd.tensor_tensor(part["kl"][:, j], lin[:, j], part["kh"][:, j].bitcast(F32), ALU.subtract)\
                        .then_inc(lo_done, 1)
                    if kind == "k":
                        pool.wait_ge(thi_done, d.v * 4 + j + 1)
                        if d.at_least(1):
                            pool.wait_ge(tan_out[j], d.v * 64)
                        nc.gpsimd.tensor_tensor(part["tl"][:, j], th[:, j], part["th"][:, j].bitcast(F32), ALU.subtract)\
                            .then_inc(tlo_done, 1)

        def select(b, n):
            jt = n % TT
            pool.wait_ge(exp_done, (b.v * STEPS + n) * 2 + 2)
            nc.gpsimd.tensor_tensor(pace[:, n % 2:n % 2 + 1], eps[0:1], eps[0:1], ALU.add)
            blk = probs[:, n % 2, :, jt * P:(jt + 1) * P]
            nc.gpsimd.affine_select(out=blk, in_=blk, compare_op=ALU.is_ge, fill=0.0, base=0,
                                    pattern=[[0, HG], [1, P]], channel_multiplier=-1).then_inc(sel_done, 1)

        def batch(b):
            att = b.at_least(0) and b.at_most(NB - 1)
            for n in range(STEPS):
                piece(b, n, 0)
                if att:
                    select(b, n)
                piece(b, n, 1)
                if n == 6 and piece_exists(b, -1):
                    d = b.plus(-1)
                    pool.wait_ge(xres_loaded, (d.v + 1) * 16)
                    nc.gpsimd.tensor_tensor(xres[:], xres[:], bo_b[:].unsqueeze(1).to_broadcast([P, TT, D]), ALU.add)\
                        .then_inc(xres_ready, 1)

        nc.gpsimd.memset(ks[MROW:P].bitcast(F32), 1.0).then_inc(const_ready, 1)
        over_batches(pool, batch)

    @block.sync
    def _(sp):
        assert NSLOT == (NB - 1) * ZR * ZR
        xs_z = xs_d.rearrange("(a p s) d -> a p (s d)", p=P, s=ZR)

        def store(d, kind, j, row, done, tile, out_sem):
            dram = k_parts if kind == "k" else q_parts
            sp.wait_ge(*done)
            sp.nop(nofuse=True)
            sp.dma_start(dram[d.par, row[0], row[1], j * PG:(j + 1) * PG].rearrange("h r t -> (h r) t"), part[tile][:, j].bitcast(F32))\
                .then_inc(out_sem[j], 16)

        def store_parts(d, kind, j):
            if kind == "k" and j == 0 and d.at_least(2):
                sp.wait_ge(stack23[1], (d.v - 1) * LOADS)
                sp.nop(nofuse=True)
            if kind in ("k", "q"):
                n = d.v * 4 + (0 if kind == "k" else 2) + j + 1
                store(d, kind, j, (0, 0), (hi_done, n), "kh", lin_out)
                store(d, kind, j, (1, 0), (lo_done, n), "kl", lin_out)
            if kind in ("k", "qj"):
                n = d.v * 4 + (0 if kind == "k" else 2) + j + 1
                store(d, kind, j, (0, 1), (thi_done, n), "th", tan_out)
                store(d, kind, j, (1, 1), (tlo_done, d.v * 2 + j + 1) if kind == "k" else (taken["qj"], count("qj", j, d)),
                      "tl", tan_out)

        def load_stack(d, g, groups, stack, dram, pair, done, sides=(0, 1)):
            for a, part_no in enumerate(pair):
                for c in sides:
                    r = (2 * a + c) * HD
                    sp.dma_start(stack[r:r + HD, slot(d, g):slot(d, g) + HG * groups].bitcast(F32),
                                 dram[d.par, part_no, c, HG * g:HG * (g + groups)].rearrange("h r t -> r h t"))\
                        .then_inc(done, 16)

        KEY_PARTS, QUERY_PARTS = (0, 1, 0), (0, 0, 1)

        def load_keys01(d):
            for j in range(2):
                sp.wait_ge(lin_out[j], d.v * 64 + 32)
                sp.nop(nofuse=True)
                sp.wait_ge(tan_out[j], d.v * 64 + 32)
                sp.nop(nofuse=True)
            if d.at_least(2):
                sp.wait_ge(cols_ready, (d.v - 1) * STEPS * 2)
                sp.nop(nofuse=True)
            load_stack(d, 0, 2, ks, k_parts, KEY_PARTS, stack01[d.par])

        def load_queries01(d, side):
            for j in range(2):
                sp.wait_ge((lin_out, tan_out)[side][j], (d.v + 1) * 64)
                sp.nop(nofuse=True)
            load_stack(d, 0, 2, qs, q_parts, QUERY_PARTS, stack01[d.par], (side,))

        def load_group(d, g):
            if d.at_least(1):
                sp.wait_ge(cols_ready, ((d.v - 1) * STEPS + (g + 1) * TT) * 2)
                sp.nop(nofuse=True)
            load_stack(d, g, 1, ks, k_parts, KEY_PARTS, stack23[g - 2])
            load_stack(d, g, 1, qs, q_parts, QUERY_PARTS, stack23[g - 2])

        def max_rows(d, g):
            sp.wait_ge(taken["mt"], d.v * G + g + 1)
            sp.nop(nofuse=True)
            for h in range(HG):
                sp.dma_start(qs[MROW:MROW + 2, slot(d, g) + h].bitcast(F32), mT[2 * h:2 * h + 2, :].bitcast(F32)).then_inc(mrow_loaded, 16)

        def x_of(view, d):
            return view[d.off] if d.fixed else view[bass.ds(d.v, 1)].rearrange("o p t e -> (o p) t e")

        def batch(b):
            for n in range(STEPS):
                if n == 3 and b.plus(2).at_most(NB - 1):
                    sp.wait_ge(ready["xt"], (b.v + 2) * 2)
                    sp.nop(nofuse=True)
                    sp.dma_start(xn[:], x_of(x_v, b.plus(2))).then_inc(x_loaded, 16)
                if n == 0 and b.at_least(0) and b.at_most(NB - 1):
                    load_group(b, 3)
                for place in range(2):
                    for kind, j, d, _ in pieces_at(b, n, place):
                        if kind in ("k", "q", "qj"):
                            store_parts(d, kind, j)
                            if (kind, j) == ("q", 1):
                                load_keys01(d)
                            if (kind, j) == ("qj", 1):
                                load_queries01(d, 0)
                                load_queries01(d, 1)
                        elif kind == "mt":
                            max_rows(d, j)
                        elif kind == "out":
                            sp.wait_ge(taken["out"], count("out", j, d))
                            sp.nop(nofuse=True)
                            sp.dma_start(x_of(x1_d, d)[:, 2 * j:2 * j + 2], xres[:, 2 * j:2 * j + 2]).then_inc(x1_stored[j], 16)
                if n == 12 and b.plus(1).at_most(NB - 1):
                    load_group(b.plus(1), 2)
                if n in (9, 10, 11) and b.at_least(0) and b.at_most(NB - 2):
                    at = b.v * ZR + n - 9
                    dest = xs_z[at] if b.fixed else xs_z[bass.ds(at, 1)].rearrange("o p n -> (o p) n")
                    sp.dma_start(dest, zrows[:]).then_inc(xs_zeroed, 16)
                if n == 15 and b.at_least(0) and b.at_most(NB - 1):
                    if b.at_least(1):
                        sp.wait_ge(x1_stored[0], b.v * 16)
                        sp.nop(nofuse=True)
                        sp.wait_ge(x1_stored[1], b.v * 16)
                        sp.nop(nofuse=True)
                        sp.wait_ge(st2_ready, b.v * TT)
                        sp.nop(nofuse=True)
                    sp.dma_start(xres[:], x_of(x_v, b)).then_inc(xres_loaded, 16)

        sp.dma_start(xn[:], x_of(x_v, Batch(0, 0))).then_inc(x_loaded, 16)
        over_batches(sp, batch)
        for j in range(2):
            sp.wait_ge(x1_stored[j], NB * 16)
        sp.wait_ge(xs_zeroed, NSLOT // ZR * 16)


def moe_stages(nc, ctx, sbt, lns, lnb, gwT, Wg, Wu, Wd, sWg, sWu, sWd, out,
               x1_d, ys_d, xs_d, yo_d, ident, ones, mv2, eps):
    pos = sbt(ctx, "pos", [P, NT, 2], I32)
    wgt = [sbt(ctx, f"wgt{r}", [P, NT]) for r in range(2)]
    slot_e = sbt(ctx, "slot_e", [1, NSLOT], I32)
    rstd2 = sbt(ctx, "rstd2", [P, NT])
    shared_weights = (sWg, sWu, sWd)

    with ExitStack() as c:
        xall = sbt(c, "xall", [P, NT, D])
        with ExitStack() as c1:
            rr = sbt(c1, "rr", [P, NT])
            logits = sbt(c1, "logits", [P, NT, NE])
            gws = sbt(c1, "gws", [P, KT, NE])
            gwb = sbt(c1, "gwb", [P, KT, NE])
            with ExitStack() as c2:
                gate_stage(nc, c2, sbt, lns, lnb, gwT, x1_d, ident, mv2, eps, rstd2, rr, logits, gws, gwb)
            with ExitStack() as c2:
                route_stage(nc, c2, sbt, x1_d, xall, ones, mv2, rr, logits, gws, gwb, pos, wgt, slot_e)
        with ExitStack() as c1:
            scatter_stage(nc, c1, sbt, shared_weights, x1_d, xall, ys_d, xs_d, ident, mv2, rstd2, pos)
    with ExitStack() as c:
        expert_stage(nc, c, sbt, Wg, Wu, Wd, xs_d, yo_d, ident, slot_e)
    with ExitStack() as c:
        combine_stage(nc, c, sbt, shared_weights, x1_d, yo_d, ys_d, out, ident, mv2, rstd2, pos, wgt)


def gate_stage(nc, ctx, sbt, lns, lnb, gwT, x1_d, ident, mv2, eps, rstd2, rr, logits, gws, gwb):
    def sb(name, shape, dt=F32):
        return sbt(ctx, name, shape, dt)

    def sem(name):
        return ctx.enter_context(nc.semaphore(name))

    RING = 4
    sc = sb("ln_sc", [P, KT])
    bi = sb("ln_bi", [P, KT])
    gw = sb("gw", [P, KT, NE])
    v3 = sb("v3", [P, NT])
    x1 = sb("x1g", [P, RING, TT, D])
    xT = sb("x1gT", [P, 2, KT, S])
    ps_t = [ctx.enter_context(nc.psum_tensor(f"ps_gt{r}", [P, S], F32)) for r in range(4)]
    ps_l = [ctx.enter_context(nc.psum_tensor(f"ps_gl{r}", [P, TT, NE], F32)) for r in range(2)]

    w_loaded = sem("wg_loaded")
    x_loaded = [sem(f"xg_loaded{r}") for r in range(RING)]
    gw_ready = sem("gw_ready")
    turned = sem("turned")
    turned_taken = sem("turned_taken")
    lg_ready = sem("lg_ready")
    lg_taken = sem("lg_taken")
    root = sem("root")
    rs_ready = sem("rs_ready")
    block = ctx.enter_context(nc.Block())

    def over_fours(eng, step):
        for r in range(RING):
            step(0, r)
        with eng.Fori(1, NB // RING) as i:
            for r in range(RING):
                step(i, r)

    @block.sync
    def _(sp):
        for t, src in ((gw, gwT),):
            sp.dma_start(t[:], src.rearrange("(k p) n -> p k n", p=P)).then_inc(w_loaded, 16)
        for k in range(KT):
            for t, src in ((sc, lns), (bi, lnb)):
                sp.dma_start(t[:, k:k + 1], src[k * P:(k + 1) * P].rearrange("(p o) -> p o", o=1)).then_inc(w_loaded, 16)

        def step(i, r):
            if isinstance(i, int):
                sp.dma_start(x1[:, r], x1_d[r]).then_inc(x_loaded[r], 16)
            else:
                sp.wait_ge(turned, (i * RING + r - RING + 1) * KT)
                sp.nop(nofuse=True)
                sp.dma_start(x1[:, r], x1_d[bass.ds(i * RING + r, 1)].rearrange("o p t d -> (o p) t d")).then_inc(x_loaded[r], 16)

        over_fours(sp, step)

    @block.tensor
    def _(pe):
        def step(i, r):
            b = i * RING + r
            later = not isinstance(i, int)
            pe.wait_ge(x_loaded[r], (i + 1) * 16)
            for k in range(KT):
                bank = KT * (r % 2) + k
                if later or r >= 2:
                    pe.wait_ge(turned_taken, (b - 2) * KT + k + 1)
                for t in range(TT):
                    mm = nc.tensor.transpose(ps_t[bank][:, t * P:(t + 1) * P], x1[:, r, t, k * P:(k + 1) * P], ident[:])
                mm.then_inc(turned, 1)
            if later or r >= 1:
                products(b - 1, (r - 1) % 2, later or r >= 3)

        def products(b, par, later):
            pe.wait_ge(turned_taken, (b + 1) * KT)
            if later:
                pe.wait_ge(lg_taken, b - 1)
            for t in range(TT):
                for k in range(KT):
                    mm = nc.tensor.matmul(ps_l[par][:, t], xT[:, par, k, t * P:(t + 1) * P], gws[:, k],
                                          start=k == 0, stop=k == KT - 1)
            mm.then_inc(lg_ready, 1)

        pe.wait_ge(gw_ready, KT)
        over_fours(pe, step)
        products(NB - 1, 1, True)

    @block.scalar
    def _(act):
        nc.scalar.activation(rstd2[:], mv2[:, :, 1], ACT.Sqrt, bias=eps[:, 0:1]).then_inc(root, 1)

        def step(i, r):
            b = i * RING + r
            for k in range(KT):
                act.wait_ge(turned, b * KT + k + 1)
                if not isinstance(i, int) or r >= 2:
                    act.wait_ge(lg_ready, b - 1)
                nc.scalar.activation(xT[:, r % 2, k], ps_t[KT * (r % 2) + k][:], ACT.Copy).then_inc(turned_taken, 1)

        over_fours(act, step)
        act.wait_ge(rs_ready, 3)
        nc.scalar.activation(rr[:], v3[:], ACT.Sqrt, bias=eps[:, 0:1]).then_inc(root, 1)

    @block.vector
    def _(dve):
        dve.wait_ge(w_loaded, 16 * 5)
        for k in range(KT):
            nc.vector.tensor_scalar(gwb[:, k], gw[:, k], bi[:, k:k + 1], None, ALU.mult)
            nc.vector.tensor_scalar(gws[:, k], gw[:, k], sc[:, k:k + 1], None, ALU.mult).then_inc(gw_ready, 1)
        dve.wait_ge(root, 1)
        nc.vector.reciprocal(rstd2[:], rstd2[:]).then_inc(rs_ready, 1)
        dve.wait_ge(rs_ready, 1)
        nc.vector.tensor_tensor(v3[:], mv2[:, :, 1], rstd2[:], ALU.mult).then_inc(rs_ready, 1)
        dve.wait_ge(rs_ready, 2)
        nc.vector.tensor_tensor(v3[:], v3[:], rstd2[:], ALU.mult).then_inc(rs_ready, 1)

        def step(i, r):
            b = i * RING + r
            dve.wait_ge(lg_ready, b + 1)
            o = logits[:, b * TT:(b + 1) * TT] if isinstance(i, int) else logits[:, bass.ds(b * TT, TT)]
            nc.vector.tensor_copy(o, ps_l[r % 2][:]).then_inc(lg_taken, 1)

        over_fours(dve, step)
        dve.wait_ge(root, 2)
        nc.vector.reciprocal(rr[:], rr[:]).then_inc(rs_ready, 1)
        dve.wait_ge(rs_ready, 4)
        nc.vector.tensor_tensor(rr[:], rr[:], rstd2[:], ALU.mult)


class SharedExpert:

    def __init__(self, nc, ctx, sbt, tag, base, count, weights, x1_d, ys_d, ident, mv2, rstd2):
        def sb(name, shape, dt=F32):
            return sbt(ctx, name + tag, shape, dt)

        def sem(name):
            return ctx.enter_context(nc.semaphore(name + tag))

        self.nc, self.base, self.count, self.weights = nc, base, count, weights
        self.x1_d, self.ys_d, self.ident, self.mv2, self.rstd2 = x1_d, ys_d, ident, mv2, rstd2
        self.wg = sb("swg", [P, KT, INTER])
        self.wu = sb("swu", [P, KT, INTER])
        self.wd = sb("swd", [P, IT, D])
        self.x1 = sb("x1s", [P, 2, TT, D])
        self.x2 = sb("x2n", [P, 2, TT, D])
        self.x2T = sb("x2T", [P, 2, KT, S])
        self.sg = sb("sg", [P, 2, S])
        self.hT = sb("hT", [P, 2, IT, S])
        self.ysb = sb("ysb", [P, 2, 2, D])
        self.ps_t = [ctx.enter_context(nc.psum_tensor(f"ps_t{r}" + tag, [P, S], F32)) for r in range(2)]
        self.ps_g = [ctx.enter_context(nc.psum_tensor(f"ps_g{r}" + tag, [P, S], F32)) for r in range(2)]
        self.ps_u = [ctx.enter_context(nc.psum_tensor(f"ps_u{r}" + tag, [P, S], F32)) for r in range(2)]
        self.ps_y = [ctx.enter_context(nc.psum_tensor(f"ps_y{r}" + tag, [P, 2, D], F32)) for r in range(2)]
        self.w_loaded = sem("w_loaded")
        self.x1_loaded = [sem(f"x1_loaded{r}") for r in range(2)]
        self.x2_ready = sem("x2_ready")
        self.xt_ready = sem("xt_ready")
        self.xt_taken = sem("xt_taken")
        self.g_ready = sem("g_ready")
        self.u_ready = sem("u_ready")
        self.sg_ready = sem("sg_ready")
        self.h_ready = sem("h_ready")
        self.y_ready = sem("y_ready")
        self.y_taken = sem("y_taken")
        self.y_stored = [sem(f"y_stored{r}") for r in range(2)]

    def has(self, s):
        return s.at_least(0) and s.at_most(self.count - 1)

    def batch_of(self, view, s):
        return view[self.base + s.off] if s.fixed else view[bass.ds(s.v + self.base, 1)].rearrange("o p t d -> (o p) t d")

    def load_weights(self, eng):
        for t, src in zip((self.wg, self.wu, self.wd), self.weights):
            eng.dma_start(t[:], src.rearrange("(k p) n -> p k n", p=P)).then_inc(self.w_loaded, 16)

    def load(self, eng, s):
        if not self.has(s):
            return
        if s.at_least(2):
            eng.wait_ge(self.y_taken, (s.v - 1) * 2)
            eng.nop(nofuse=True)
        eng.dma_start(self.x1[:, s.par], self.batch_of(self.x1_d, s)).then_inc(self.x1_loaded[s.par], 16)

    def store(self, eng, s):
        if not self.has(s):
            return
        ys_v = self.ys_d.rearrange("(c t) p d -> c p t d", t=TT)
        for j in range(2):
            eng.wait_ge(self.y_taken, s.v * 2 + j + 1)
            eng.nop(nofuse=True)
            eng.dma_start(self.batch_of(ys_v, s)[:, 2 * j:2 * j + 2], self.ysb[:, j]).then_inc(self.y_stored[j], 16)

    def transposes(self, pe, s):
        if not self.has(s):
            return
        nc = self.nc
        pe.wait_ge(self.x2_ready, s.v + 1)
        for k in range(KT):
            if s.at_least(1):
                pe.wait_ge(self.xt_taken, (s.v - 1) * KT + k + 1)
            for t in range(TT):
                mm = nc.tensor.transpose(self.ps_t[k][:, t * P:(t + 1) * P], self.x2[:, s.par, t, k * P:(k + 1) * P], self.ident[:])
            mm.then_inc(self.xt_ready, 1)

    def gate_up(self, pe, s, i):
        nc = self.nc
        if i == 0:
            pe.wait_ge(self.xt_taken, (s.v + 1) * KT)
        for w, bank, freed, done in ((self.wg, self.ps_g, self.sg_ready, self.g_ready),
                                     (self.wu, self.ps_u, self.h_ready, self.u_ready)):
            if i >= 2 or s.at_least(1):
                pe.wait_ge(freed, s.v * IT + i - 1)
            for k in range(KT):
                mm = nc.tensor.matmul(bank[i % 2][:], w[:, k, i * P:(i + 1) * P], self.x2T[:, s.par, k],
                                      start=k == 0, stop=k == KT - 1)
            mm.then_inc(done, 1)

    def down(self, pe, s):
        nc = self.nc
        pe.wait_ge(self.h_ready, s.v * IT + IT)
        for j in range(2):
            if s.at_least(1):
                pe.wait_ge(self.y_taken, s.v * 2 + j - 1)
            for tt in range(2):
                t = 2 * j + tt
                for i in range(IT):
                    mm = nc.tensor.matmul(self.ps_y[j][:, tt], self.hT[:, s.par, i, t * P:(t + 1) * P], self.wd[:, i],
                                          start=i == 0, stop=i == IT - 1)
            mm.then_inc(self.y_ready, 1)

    def tensor_round(self, pe, s):
        if self.has(s):
            self.gate_up(pe, s, 0)
        if self.has(s.plus(-1)):
            self.down(pe, s.plus(-1))
        if self.has(s):
            for i in range(1, IT):
                self.gate_up(pe, s, i)
                if i == 2:
                    self.transposes(pe, s.plus(1))

    def copies(self, act, s):
        if not self.has(s):
            return
        for k in range(KT):
            act.wait_ge(self.xt_ready, s.v * KT + k + 1)
            if s.at_least(2):
                act.wait_ge(self.u_ready, (s.v - 1) * IT)
            self.nc.scalar.activation(self.x2T[:, s.par, k], self.ps_t[k][:], ACT.Copy).then_inc(self.xt_taken, 1)

    def scalar_round(self, act, s):
        if not self.has(s):
            return
        for i in range(IT):
            act.wait_ge(self.g_ready, s.v * IT + i + 1)
            if i >= 2 or s.at_least(1):
                act.wait_ge(self.h_ready, s.v * IT + i - 1)
            self.nc.scalar.activation(self.sg[:, i % 2], self.ps_g[i % 2][:], ACT.Silu).then_inc(self.sg_ready, 1)
            if i == 2:
                self.copies(act, s.plus(1))

    def norm(self, dve, s):
        if not self.has(s):
            return
        dve.wait_ge(self.x1_loaded[s.par], (s.half() + 1) * 16)
        if s.at_least(2):
            dve.wait_ge(self.xt_ready, (s.v - 1) * KT)
        for t in range(TT):
            at = (s.v + self.base) * TT + t
            if s.fixed:
                m, rs = self.mv2[:, at, 0:1], self.rstd2[:, at:at + 1]
            else:
                m, rs = self.mv2[:, bass.ds(at, 1), 0], self.rstd2[:, bass.ds(at, 1)]
            a = self.nc.vector.tensor_scalar(self.x2[:, s.par, t], self.x1[:, s.par, t], m, rs, ALU.subtract, ALU.mult)
        a.then_inc(self.x2_ready, 1)

    def product(self, dve, s, i):
        dve.wait_ge(self.u_ready, s.v * IT + i + 1)
        dve.wait_ge(self.sg_ready, s.v * IT + i + 1)
        self.nc.vector.tensor_tensor(self.hT[:, s.par, i], self.sg[:, i % 2], self.ps_u[i % 2][:], ALU.mult)\
            .then_inc(self.h_ready, 1)

    def outputs(self, dve, s):
        for j in range(2):
            dve.wait_ge(self.y_ready, s.v * 2 + j + 1)
            if s.at_least(1):
                dve.wait_ge(self.y_stored[j], s.v * 16)
            self.nc.vector.tensor_tensor(self.ysb[:, j], self.ps_y[j][:], self.x1[:, s.par, 2 * j:2 * j + 2], ALU.add)\
                .then_inc(self.y_taken, 1)

    def vector_unit(self, dve, s, i):
        if self.has(s):
            self.product(dve, s, i)
        if i == 0 and self.has(s.plus(-1)):
            self.outputs(dve, s.plus(-1))
        if i == 1 and s.at_least(1):
            self.norm(dve, s.plus(1))


def over_rounds(eng, pairs, tail, step):
    step(Batch(0, 0))
    step(Batch(0, 1))
    with eng.Fori(0, pairs) as i:
        step(Batch(i, 2))
        step(Batch(i, 3))
    for s in range(2 + 2 * pairs, 2 + 2 * pairs + tail):
        step(Batch(0, s))


def route_stage(nc, ctx, sbt, x1_d, xall, ones, mv2, rr, logits, gws, gwb, pos, wgt, slot_e):
    def sb(name, shape, dt=F32):
        return sbt(ctx, name, shape, dt)

    def sem(name):
        return ctx.enter_context(nc.semaphore(name))

    lower = sb("lower", [P, P])
    sgb = sb("sgb", [P, 2, NE])
    a = sb("ra", [P, NT, NE])
    b = sb("rb", [P, NT, NE])
    prob = sb("prob", [P, NT, NE])
    oh = [sb(f"oh{r}", [P, NT, NE]) for r in range(2)]
    rank = sb("rank", [P, NT, NE])
    m1 = sb("m1", [P, NT])
    m2 = sb("m2", [P, NT])
    cc = sb("cc", [P, NT])
    desc = sb("desc", [P, NE])
    one64 = sb("one64", [P, NT])
    tot = sb("tot", [P, NE])
    toti = sb("toti", [P, NE], I32)
    incl = sb("incl", [P, NE])
    base = sb("base", [P, NE])
    start = sb("start", [1, NSLOT])
    cmp_ = sb("cmp_", [1, NSLOT, NE])
    cnt = sb("cnt", [1, NSLOT])
    ps_s = ctx.enter_context(nc.psum_tensor("ps_s", [P, 2, NE], F32))
    ps_r = ctx.enter_context(nc.psum_tensor("ps_r", [P, NT, NE], F32))
    ps_n = ctx.enter_context(nc.psum_tensor("ps_n", [P, NT, NE], F32))

    filled = sem("filled")
    lower_ready = sem("lower_ready")
    iotas = sem("iotas")
    sums_ready = sem("sums_ready")
    chosen = sem("chosen")
    ranked = sem("ranked")
    chain = sem("chain")
    exp_in = sem("exp_in")
    exp_out = sem("exp_out")
    pos_ready = sem("pos_ready")
    x_loaded = sem("xa_loaded")
    block = ctx.enter_context(nc.Block())

    @block.tensor
    def _(pe):
        for c, w in enumerate((gws, gwb)):
            for k in range(KT):
                mm = nc.tensor.matmul(ps_s[:, c], ones[:], w[:, k], start=k == 0, stop=k == KT - 1)
        mm.then_inc(sums_ready, 1)
        pe.wait_ge(chosen, 1)
        pe.wait_ge(lower_ready, 1)
        nc.tensor.matmul(ps_r[:].rearrange("p t e -> p (t e)"), lower[:], rank[:].rearrange("p t e -> p (t e)"), start=True, stop=True)
        nc.tensor.matmul(ps_n[:].rearrange("p t e -> p (t e)"), ones[:], rank[:].rearrange("p t e -> p (t e)"), start=True, stop=True)\
            .then_inc(ranked, 1)

    @block.scalar
    def _(act):
        act.wait_ge(exp_in, 1)
        nc.scalar.activation(prob[:], a[:], ACT.Exp).then_inc(exp_out, 1)

    @block.gpsimd
    def _(pool):
        nc.gpsimd.memset(lower[:], 1.0).then_inc(filled, 1)
        pool.wait_ge(filled, 1)
        nc.gpsimd.affine_select(out=lower[:], in_=lower[:], compare_op=ALU.is_gt, fill=0.0, base=0,
                                pattern=[[1, P]], channel_multiplier=-1).then_inc(lower_ready, 1)
        nc.gpsimd.iota(desc[:], pattern=[[-1, NE]], base=NE, channel_multiplier=0,
                       allow_small_or_imprecise_dtypes=True).then_inc(iotas, 1)
        nc.gpsimd.iota(start[:], pattern=[[P, NSLOT]], base=0, channel_multiplier=0,
                       allow_small_or_imprecise_dtypes=True).then_inc(iotas, 1)

    @block.sync
    def _(sp):
        x1_v = x1_d.rearrange("b p t d -> p b t d")
        n = NB // 4
        for c in range(4):
            sp.dma_start(xall[:, c * n * TT:(c + 1) * n * TT].rearrange("p (b t) d -> p b t d", t=TT), x1_v[:, c * n:(c + 1) * n])\
                .then_inc(x_loaded, 16)
        sp.wait_ge(x_loaded, 4 * 16)

    @block.vector
    def _(dve):
        n = [0]

        def then(ins):
            n[0] += 1
            ins.then_inc(chain, 1)
            dve.wait_ge(chain, n[0])

        def over_e(ap):
            return ap.unsqueeze(2).to_broadcast([P, NT, NE])

        def over_t(ap):
            return ap.unsqueeze(1).to_broadcast([P, NT, NE])

        def tt(o, x, y, op):
            return nc.vector.tensor_tensor(o, x, y, op)

        dve.wait_ge(sums_ready, 1)
        then(nc.vector.tensor_copy(sgb[:], ps_s[:]))
        then(nc.vector.memset(one64[:], 1.0))
        then(nc.vector.tensor_copy(m1[:], mv2[:, :, 0]))
        then(tt(a[:], over_e(m1[:]), over_t(sgb[:, 0]), ALU.mult))
        then(tt(a[:], logits[:], a[:], ALU.subtract))
        then(tt(a[:], a[:], over_e(rr[:]), ALU.mult))
        then(tt(a[:], a[:], over_t(sgb[:, 1]), ALU.add))
        then(nc.vector.tensor_reduce(m1[:], a[:], AX.X, ALU.max))
        tt(a[:], a[:], over_e(m1[:]), ALU.subtract).then_inc(exp_in, 1)
        dve.wait_ge(exp_out, 1)
        then(nc.vector.tensor_reduce(m1[:], prob[:], AX.X, ALU.add))
        then(nc.vector.reciprocal(m1[:], m1[:]))
        then(tt(prob[:], prob[:], over_e(m1[:]), ALU.mult))
        dve.wait_ge(iotas, 2)

        def choose(p, best, onehot):
            then(nc.vector.tensor_reduce(best[:], p[:], AX.X, ALU.max))
            then(tt(a[:], p[:], over_e(best[:]), ALU.is_equal))
            then(tt(a[:], a[:], over_t(desc[:]), ALU.mult))
            then(nc.vector.tensor_reduce(cc[:], a[:], AX.X, ALU.max))
            then(tt(onehot[:], over_t(desc[:]), over_e(cc[:]), ALU.is_equal))

        choose(prob, m1, oh[0])
        then(nc.vector.scalar_tensor_tensor(out=b[:], in0=oh[0][:], scalar=-2.0, in1=prob[:], op0=ALU.mult, op1=ALU.add))
        choose(b, m2, oh[1])
        then(tt(cc[:], m1[:], m2[:], ALU.add))
        then(nc.vector.tensor_scalar(cc[:], cc[:], EPS, None, ALU.add))
        then(nc.vector.reciprocal(cc[:], cc[:]))
        then(tt(wgt[0][:], m1[:], cc[:], ALU.mult))
        then(tt(wgt[1][:], m2[:], cc[:], ALU.mult))
        tt(rank[:], oh[0][:], oh[1][:], ALU.add).then_inc(chosen, 1)
        dve.wait_ge(ranked, 1)
        then(nc.vector.tensor_copy(b[:], ps_n[:]))
        for e in range(NE):
            s_ = nc.vector.tensor_tensor_scan(a[:, :, e], one64[:], b[:, :, e], 0.0, ALU.mult, ALU.add)
        then(s_)
        then(nc.vector.tensor_copy(tot[:], a[:, NT - 1]))
        then(tt(a[:], a[:], b[:], ALU.subtract))
        then(tt(rank[:], a[:], ps_r[:], ALU.add))
        then(nc.vector.tensor_scalar(toti[:], tot[:], float(P - 1), None, ALU.add))
        then(nc.vector.tensor_scalar(toti[:], toti[:], 7, None, ALU.arith_shift_right))
        then(nc.vector.tensor_copy(tot[:], toti[:]))
        then(nc.vector.tensor_scalar(tot[:], tot[:], float(P), None, ALU.mult))
        then(nc.vector.tensor_tensor_scan(incl[:], one64[:, 0:NE], tot[:], 0.0, ALU.mult, ALU.add))
        then(tt(base[:], incl[:], tot[:], ALU.subtract))
        then(tt(rank[:], rank[:], over_t(base[:]), ALU.add))
        for r in range(2):
            then(tt(a[:], rank[:], oh[r][:], ALU.mult))
            then(nc.vector.tensor_reduce(cc[:], a[:], AX.X, ALU.add))
            nc.vector.tensor_copy(pos[:, :, r], cc[:]).then_inc(pos_ready, 1)
            dve.wait_ge(pos_ready, r + 1)
        then(tt(cmp_[:], start[:].unsqueeze(2).to_broadcast([1, NSLOT, NE]),
                incl[0:1].unsqueeze(1).to_broadcast([1, NSLOT, NE]), ALU.is_ge))
        then(nc.vector.tensor_reduce(cnt[:], cmp_[:], AX.X, ALU.add))
        then(nc.vector.tensor_scalar(slot_e[:], cnt[:], float(NE - 1), None, ALU.min))


def scatter_stage(nc, ctx, sbt, shared_weights, x1_d, xall, ys_d, xs_d, ident, mv2, rstd2, pos):
    FIRST, RING = SHARED_FIRST, 4
    idx = [sbt(ctx, f"idx{q}", [P, 2], I32) for q in range(RING)]
    row = [sbt(ctx, f"row{q}", [P, D]) for q in range(RING)]
    staged = ctx.enter_context(nc.semaphore("staged"))
    normed = ctx.enter_context(nc.semaphore("normed"))
    scattered = [ctx.enter_context(nc.semaphore(f"scattered{q}")) for q in range(RING)]
    se = SharedExpert(nc, ctx, sbt, "_1", 0, FIRST, shared_weights, x1_d, ys_d, ident, mv2, rstd2)
    block = ctx.enter_context(nc.Block())

    def rounds(eng, step):
        over_rounds(eng, (FIRST - 3) // 2, FIRST - 1 - (FIRST - 3) // 2 * 2, step)

    @block.sync
    def _(sp):
        se.load(sp, Batch(0, 0))
        se.load_weights(sp)
        se.load(sp, Batch(0, 1))

        def step(s):
            se.store(sp, s.plus(-1))
            if s.at_least(1):
                se.load(sp, s.plus(1))

        rounds(sp, step)
        for j in range(2):
            sp.wait_ge(se.y_stored[j], FIRST * 16)

    @block.tensor
    def _(pe):
        se.transposes(pe, Batch(0, 0))
        pe.wait_ge(se.w_loaded, 3 * 16)
        rounds(pe, lambda s: se.tensor_round(pe, s))

    @block.scalar
    def _(act):
        se.copies(act, Batch(0, 0))
        rounds(act, lambda s: se.scalar_round(act, s))

    @block.vector
    def _(dve):
        se.norm(dve, Batch(0, 0))
        se.norm(dve, Batch(0, 1))

        def norm_tile(s, c):
            at = s.v * 2 * TT + c
            k = slice(at, at + 1) if s.fixed else bass.ds(at, 1)
            tile = xall[:, at] if s.fixed else xall[:, k].rearrange("p o e -> p (o e)")
            mean = mv2[:, at, 0:1] if s.fixed else mv2[:, k, 0]
            nc.vector.tensor_scalar(tile, tile, mean, rstd2[:, k], ALU.subtract, ALU.mult).then_inc(normed, 1)

        def step(s):
            for i in range(IT):
                if s.at_most(NB // 2 - 1):
                    norm_tile(s, 2 * i)
                    norm_tile(s, 2 * i + 1)
                se.vector_unit(dve, s, i)

        rounds(dve, step)

    @block.gpsimd
    def _(pool):
        def stage(t, q, n):
            if n is not None:
                pool.wait_ge(scattered[q], n * 32)
            if n is not None or q > 0:
                pool.wait_ge(staged, t * 2)
            k = slice(t, t + 1) if isinstance(t, int) else bass.ds(t, 1)
            one = (lambda ap: ap[:, t]) if isinstance(t, int) else (lambda ap: ap[:, k].rearrange("p o e -> p (o e)"))
            nc.gpsimd.tensor_copy(idx[q][:], one(pos)).then_inc(staged, 1)
            pool.wait_ge(normed, t + 1)
            nc.gpsimd.tensor_copy(row[q][:], one(xall)).then_inc(staged, 1)

        def scatter(q):
            for r in range(2):
                nc.gpsimd.indirect_dma_start(xs_d[:, :], bass.IndirectOffsetOnAxis(ap=idx[q][:, r:r + 1], axis=0),
                                             row[q][:], None).then_inc(scattered[q], 16)

        stage(0, 0, None)
        for q in range(1, RING):
            stage(q, q, None)
            scatter(q - 1)
        with pool.Fori(1, NT // RING) as i:
            for q in range(RING):
                stage(i * RING + q, q, i)
                scatter((q - 1) % RING)
        pool.wait_ge(staged, NT * 2)
        scatter(RING - 1)
        for q in range(RING):
            pool.wait_ge(scattered[q], NT // RING * 32)


def expert_stage(nc, ctx, sbt, Wg, Wu, Wd, xs_d, yo_d, ident, slot_e):
    def sb(name, shape, dt=F32):
        return sbt(ctx, name, shape, dt)

    def sem(name):
        return ctx.enter_context(nc.semaphore(name))

    wg = sb("wg_e", [P, NE, KT, INTER])
    wu = sb("wu_e", [P, NE, KT, INTER])
    wd = sb("wd_e", [P, NE, IT, D])
    xr = sb("xr", [P, 2, D])
    xT = sb("xT_e", [P, 2, KT, P])
    sg = sb("sg_e", [P, 2, INTER])
    h = sb("h_e", [P, 2, INTER])
    hT = sb("hT_e", [P, 2, IT, P])
    y = sb("y_e", [P, 2, D])
    ps_x = ctx.enter_context(nc.psum_tensor("ps_x", [P, KT, P], F32))
    ps_g = ctx.enter_context(nc.psum_tensor("ps_ge", [P, INTER], F32))
    ps_u = ctx.enter_context(nc.psum_tensor("ps_ue", [P, INTER], F32))
    ps_h = ctx.enter_context(nc.psum_tensor("ps_h", [P, IT, P], F32))
    ps_y = ctx.enter_context(nc.psum_tensor("ps_ye", [P, D], F32))

    w_loaded = sem("we_loaded")
    x_loaded = [sem(f"xe_loaded{r}") for r in range(2)]
    tx_ready = sem("tx_ready")
    xt_taken = sem("xte_taken")
    g_ready = sem("ge_ready")
    sg_ready = sem("sge_ready")
    u_ready = sem("ue_ready")
    h_ready = sem("he_ready")
    th_ready = sem("th_ready")
    ht_taken = sem("hte_taken")
    y_ready = sem("ye_ready")
    y_taken = sem("ye_taken")
    y_stored = [sem(f"ye_stored{r}") for r in range(2)]
    block = ctx.enter_context(nc.Block())

    xs_v = xs_d.rearrange("(s p) d -> s p d", p=P)
    yo_v = yo_d.rearrange("(s p) d -> s p d", p=P)

    def over_slots(eng, step):
        for s in range(3):
            step(Batch(0, s))
        with eng.Fori(0, (NSLOT - 5) // 2) as i:
            step(Batch(i, 3))
            step(Batch(i, 4))
        for s in range(NSLOT - 2, NSLOT + 1):
            step(Batch(0, s))

    def rows_of(view, s):
        return view[s.off] if s.fixed else view[bass.ds(s.v, 1)].rearrange("o p d -> (o p) d")

    @block.sync
    def _(sp):
        for r in range(2):
            sp.dma_start(xr[:, r], xs_v[r]).then_inc(x_loaded[r], 16)

        def step(s):
            if s.at_most(NSLOT - 3):
                sp.wait_ge(tx_ready, s.v + 1)
                sp.nop(nofuse=True)
                sp.dma_start(xr[:, s.par], rows_of(xs_v, s.plus(2))).then_inc(x_loaded[s.par], 16)
            if s.at_least(1):
                d = s.plus(-1)
                sp.wait_ge(y_taken, d.v + 1)
                sp.nop(nofuse=True)
                sp.dma_start(rows_of(yo_v, d), y[:, d.par]).then_inc(y_stored[d.par], 16)

        over_slots(sp, step)
        for r in range(2):
            sp.wait_ge(y_stored[r], (NSLOT + 1 - r) // 2 * 16)
            sp.nop(nofuse=True)

    @block.gpsimd
    def _(pool):
        for e in range(NE):
            if e > 0:
                pool.wait_ge(w_loaded, e * 3 * 16)
            for t, src in ((wg, Wg), (wu, Wu), (wd, Wd)):
                pool.dma_start(t[:, e], src[e].rearrange("(k p) n -> p k n", p=P)).then_inc(w_loaded, 16)

    @block.tensor
    def _(pe):
        def expert(s):
            at = slot_e[0:1, s.off:s.off + 1] if s.fixed else slot_e[0:1, bass.ds(s.v, 1)]
            return pe.value_load(at, min_val=0, max_val=NE - 1)

        def weights(w, e, k):
            return w[:, bass.ds(e, 1), k].rearrange("p o n -> p (o n)")

        def turn_rows(s):
            pe.wait_ge(x_loaded[s.par], (s.half() + 1) * 16)
            if s.at_least(1):
                pe.wait_ge(xt_taken, s.v)
            for k in range(KT):
                mm = nc.tensor.transpose(ps_x[:, k], xr[:, s.par, k * P:(k + 1) * P], ident[:])
            mm.then_inc(tx_ready, 1)

        def gate(s, e):
            pe.wait_ge(w_loaded, e * (3 * 16) + 3 * 16)
            pe.wait_ge(xt_taken, s.v + 1)
            if s.at_least(1):
                pe.wait_ge(sg_ready, s.v)
            for k in range(KT):
                mm = nc.tensor.matmul(ps_g[:], xT[:, s.par, k], weights(wg, e, k), start=k == 0, stop=k == KT - 1)
            mm.then_inc(g_ready, 1)

        def up(s, e):
            if s.at_least(1):
                pe.wait_ge(h_ready, s.v)
            for k in range(KT):
                mm = nc.tensor.matmul(ps_u[:], xT[:, s.par, k], weights(wu, e, k), start=k == 0, stop=k == KT - 1)
            mm.then_inc(u_ready, 1)

        def turn_hidden(s):
            pe.wait_ge(h_ready, s.v + 1)
            if s.at_least(1):
                pe.wait_ge(ht_taken, s.v)
            for k in range(IT):
                mm = nc.tensor.transpose(ps_h[:, k], h[:, s.par, k * P:(k + 1) * P], ident[:])
            mm.then_inc(th_ready, 1)

        def down(s):
            e = expert(s)
            pe.wait_ge(ht_taken, s.v + 1)
            if s.at_least(1):
                pe.wait_ge(y_taken, s.v)
            for k in range(IT):
                mm = nc.tensor.matmul(ps_y[:], hT[:, s.par, k], weights(wd, e, k), start=k == 0, stop=k == IT - 1)
            mm.then_inc(y_ready, 1)

        def step(s):
            if s.at_most(NSLOT - 2):
                turn_rows(s.plus(1))
            if s.at_most(NSLOT - 1):
                e = expert(s)
                gate(s, e)
            if s.at_least(1):
                turn_hidden(s.plus(-1))
            if s.at_most(NSLOT - 1):
                up(s, e)
            if s.at_least(1):
                down(s.plus(-1))

        turn_rows(Batch(0, 0))
        over_slots(pe, step)

    @block.scalar
    def _(act):
        def step(s):
            if s.at_most(NSLOT - 1):
                act.wait_ge(g_ready, s.v + 1)
                if s.at_least(2):
                    act.wait_ge(h_ready, s.v - 1)
                nc.scalar.activation(sg[:, s.par], ps_g[:], ACT.Silu).then_inc(sg_ready, 1)
            if s.at_least(1):
                d = s.plus(-1)
                act.wait_ge(th_ready, d.v + 1)
                if d.at_least(2):
                    act.wait_ge(y_ready, d.v - 1)
                nc.scalar.activation(hT[:, d.par], ps_h[:], ACT.Copy).then_inc(ht_taken, 1)

        over_slots(act, step)

    @block.vector
    def _(dve):
        def take_rows(s):
            dve.wait_ge(tx_ready, s.v + 1)
            if s.at_least(2):
                dve.wait_ge(u_ready, s.v - 1)
            nc.vector.tensor_copy(xT[:, s.par], ps_x[:]).then_inc(xt_taken, 1)

        def step(s):
            if s.at_most(NSLOT - 2):
                take_rows(s.plus(1))
            if s.at_most(NSLOT - 1):
                dve.wait_ge(u_ready, s.v + 1)
                dve.wait_ge(sg_ready, s.v + 1)
                if s.at_least(2):
                    dve.wait_ge(th_ready, s.v - 1)
                nc.vector.tensor_tensor(h[:, s.par], sg[:, s.par], ps_u[:], ALU.mult).then_inc(h_ready, 1)
            if s.at_least(1):
                d = s.plus(-1)
                dve.wait_ge(y_ready, d.v + 1)
                if d.at_least(2):
                    dve.wait_ge(y_stored[d.par], d.half() * 16)
                nc.vector.tensor_copy(y[:, d.par], ps_y[:]).then_inc(y_taken, 1)

        take_rows(Batch(0, 0))
        over_slots(dve, step)


def combine_stage(nc, ctx, sbt, shared_weights, x1_d, yo_d, ys_d, out, ident, mv2, rstd2, pos, wgt):
    def sem(name):
        return ctx.enter_context(nc.semaphore(name))

    BASE = SHARED_FIRST
    ROUNDS = NB // 2
    acc = sbt(ctx, "acc", [P, 2, 2 * TT, D])
    yr = [[sbt(ctx, f"yr{q}{r}", [P, D]) for r in range(2)] for q in range(TT)]
    ix = [sbt(ctx, f"ix{q}", [P, 2], I32) for q in range(TT)]
    acc_loaded = [sem(f"acc_loaded{r}") for r in range(2)]
    stored = [sem(f"stored{r}") for r in range(2)]
    staged = sem("ix_staged")
    gathered = [sem(f"gathered{q}") for q in range(TT)]
    half_done = sem("half_done")
    tile_done = sem("tile_done")
    se = SharedExpert(nc, ctx, sbt, "_2", BASE, NB - BASE, shared_weights, x1_d, ys_d, ident, mv2, rstd2)
    block = ctx.enter_context(nc.Block())
    ys_v = ys_d.rearrange("(r t) p d -> r p t d", t=2 * TT)
    out_v = out.rearrange("b s d -> (b s) d").rearrange("(r t p) d -> r p t d", p=P, t=2 * TT)

    def round_of(view, s):
        return view[s.off] if s.fixed else view[bass.ds(s.v, 1)].rearrange("o p t d -> (o p) t d")

    def rounds(eng, step):
        over_rounds(eng, ROUNDS // 2 - 2, 2, step)

    @block.sync
    def _(sp):
        def load_acc(s):
            if s.at_least(2):
                sp.wait_ge(stored[s.par], s.half() * 16)
                sp.nop(nofuse=True)
                for j in range(2):
                    sp.wait_ge(se.y_stored[j], (s.v - 1 if s.at_most(ROUNDS - 2) else NB - BASE) * 16)
                    sp.nop(nofuse=True)
            sp.dma_start(acc[:, s.par], round_of(ys_v, s)).then_inc(acc_loaded[s.par], 16)

        se.load(sp, Batch(0, 0))
        se.load_weights(sp)
        se.load(sp, Batch(0, 1))
        load_acc(Batch(0, 0))

        def step(s):
            se.store(sp, s.plus(-1))
            if s.at_least(1):
                se.load(sp, s.plus(1))
            if s.at_most(ROUNDS - 3):
                load_acc(s.plus(1))
            if s.fixed and s.off == ROUNDS - 1:
                load_acc(s)
            sp.wait_ge(tile_done, (s.v + 1) * 2 * TT)
            sp.nop(nofuse=True)
            sp.dma_start(round_of(out_v, s), acc[:, s.par]).then_inc(stored[s.par], 16)

        rounds(sp, step)
        for r in range(2):
            sp.wait_ge(stored[r], ROUNDS // 2 * 16)

    @block.tensor
    def _(pe):
        se.transposes(pe, Batch(0, 0))
        pe.wait_ge(se.w_loaded, 3 * 16)
        rounds(pe, lambda s: se.tensor_round(pe, s))

    @block.scalar
    def _(act):
        se.copies(act, Batch(0, 0))
        rounds(act, lambda s: se.scalar_round(act, s))

    @block.gpsimd
    def _(pool):
        def stage(b, q):
            if b.at_least(1):
                pool.wait_ge(tile_done, b.v * TT + q - TT + 1)
            if q > 0 or b.at_least(1):
                pool.wait_ge(staged, b.v * TT + q)
            src = pos[:, b.off * TT + q] if b.fixed else pos[:, bass.ds(b.v * TT + q, 1)].rearrange("p o r -> p (o r)")
            nc.gpsimd.tensor_copy(ix[q][:], src).then_inc(staged, 1)

        def gather(q):
            for r in range(2):
                nc.gpsimd.indirect_dma_start(yr[q][r][:], None, yo_d[:, :],
                                             bass.IndirectOffsetOnAxis(ap=ix[q][:, r:r + 1], axis=0))\
                    .then_inc(gathered[q], 16)

        def step(b):
            for q in range(TT):
                stage(b, q)
                if not (b.fixed and b.off == 0 and q == 0):
                    gather((q - 1) % TT)

        over_rounds(pool, NB // 2 - 1, 0, step)
        pool.wait_ge(staged, NT)
        gather(TT - 1)

    @block.vector
    def _(dve):
        def add_tile(s, c):
            b, q = s.v * 2 + c // TT, c % TT
            dve.wait_ge(gathered[q], b * 32 + 32)
            at = b * TT + q
            k = slice(at, at + 1) if s.fixed else bass.ds(at, 1)
            nc.vector.scalar_tensor_tensor(out=acc[:, s.par, c], in0=yr[q][0][:], scalar=wgt[0][:, k],
                                           in1=acc[:, s.par, c], op0=ALU.mult, op1=ALU.add).then_inc(half_done, 1)
            dve.wait_ge(half_done, at + 1)
            nc.vector.scalar_tensor_tensor(out=acc[:, s.par, c], in0=yr[q][1][:], scalar=wgt[1][:, k],
                                           in1=acc[:, s.par, c], op0=ALU.mult, op1=ALU.add).then_inc(tile_done, 1)

        se.norm(dve, Batch(0, 0))
        se.norm(dve, Batch(0, 1))

        def step(s):
            for i in range(IT):
                se.vector_unit(dve, s, i)
                if i == 0:
                    dve.wait_ge(acc_loaded[s.par], (s.half() + 1) * 16)
                add_tile(s, 2 * i)
                add_tile(s, 2 * i + 1)

        rounds(dve, step)


def kernel(**inputs):
    import numpy as _np
    import concourse.bacc as _bacc
    from concourse import mybir as _mybir
    from concourse.bass_utils import run_bass_kernel_spmd as _run

    ins = ["L0_attn_x", "L0_attn_Wq", "L0_attn_bq", "L0_attn_Wk", "L0_attn_bk", "L0_attn_Wv", "L0_attn_bv",
           "L0_attn_Wo", "L0_attn_bo", "L0_attn_J_attn", "L0_attn_lambda_attn", "L0_ffn_ln_scale", "L0_ffn_ln_bias",
           "L0_ffn_gate_w", "L0_ffn_Wg", "L0_ffn_Wu", "L0_ffn_Wd", "L0_ffn_sWg", "L0_ffn_sWu", "L0_ffn_sWd"]
    turned = {"L0_attn_Wq", "L0_attn_Wk", "L0_attn_Wv", "L0_attn_Wo", "L0_ffn_gate_w"}
    nc = _bacc.Bacc("TRN2", target_bir_lowering=False, num_devices=1)
    arrays, args = {}, []
    for name in ins:
        a = _np.asarray(inputs[name])
        if name in turned:
            a = a.T
        if a.ndim == 0:
            a = a.reshape(1)
        a = _np.ascontiguousarray(a)
        arrays[f"in_{name}_dram"] = a
        args.append(nc.dram_tensor(f"in_{name}_dram", a.shape, _mybir.dt.from_np(a.dtype), kind="ExternalInput").ap())
    args.append(nc.dram_tensor("out_0_dram", (NB, S, D), F32, kind="ExternalOutput").ap())
    build(nc, *args)
    r = _run(nc, [arrays], core_ids=[0])
    return r.results[0]["out_0_dram"]
```

```python
import concourse.bass as bass
from concourse import mybir
from contextlib import ExitStack


F32 = mybir.dt.float32
F32R = mybir.dt.float32r
BF16 = mybir.dt.bfloat16
I32 = mybir.dt.int32
ALU = mybir.AluOpType
ACT = mybir.ActivationFunctionType
AX = mybir.AxisListType

P = 128
NB, S, D = 16, 512, 256
H, HD = 16, 16
KT = D // P
TT = S // P
NT = NB * TT
HG = 4
G = H // HG
PG = P // HD
NE, INTER = 8, 512
IT = INTER // P
EPS = 1e-5
MASK = -1e30
NSLOT = 2 * NT + NE - 1
ZR = 3
EARLY = 4
LEAD = 7
STEPS = G * TT
STACK = 3 * 2 * HD
MROW = STACK
LOADS = 16 * 12
PROLOGUE, TAIL = -1, NB
SHARED_FIRST = 9


class Batch:

    def __init__(self, i, off):
        self.i, self.off = i, off
        self.v = off if isinstance(i, int) and i == 0 else i * 2 + off
        self.par = off % 2
        self.fixed = isinstance(i, int)

    def plus(self, k):
        return Batch(self.i, self.off + k)

    def half(self):
        return self.off // 2 if self.fixed else self.i + self.off // 2

    def at_least(self, n):
        return (not self.fixed) or self.off >= n

    def at_most(self, n):
        return (not self.fixed) or self.off <= n


def over_batches(eng, batch):
    batch(Batch(0, PROLOGUE))
    batch(Batch(0, 0))
    with eng.Fori(0, NB // 2 - 2) as i:
        batch(Batch(i, 1))
        batch(Batch(i, 2))
    for last in (NB - 3, NB - 2, NB - 1, TAIL):
        batch(Batch(0, last))


PIECES = [
    (0, 0, "xt", 0, 1), (0, 1, "xt", 1, 1),
    (1, 0, "ot", 3, -1), (1, 1, "mt", 1, 0),
    (2, 0, "k", 0, 1), (2, 1, "k", 1, 1),
    (3, 0, "q", 0, 1), (3, 1, "q", 1, 1),
    (4, 0, "qj", 0, 1), (4, 1, "qj", 1, 1),
    (5, 0, "ot", 0, 0), (5, 1, "mt", 2, 0),
    (6, 1, "v", 0, 1),
    (7, 1, "v", 1, 1),
    (8, 0, "ont", 0, -1),
    (9, 0, "ot", 1, 0), (9, 1, "mt", 3, 0),
    (10, 0, "ont", 1, -1),
    (11, 0, "out", 0, -1),
    (12, 0, "out", 1, -1),
    (13, 0, "ot", 2, 0), (13, 1, "mt", 0, 1),
    (14, 0, "gt", 0, -1), (14, 1, "gt", 1, -1),
    (15, 1, "lg", 0, -1),
]
PER_BATCH = {"xt": 2, "k": 2, "q": 2, "qj": 2, "v": 2, "mt": G, "ot": G, "ont": 2, "out": 2, "gt": 2, "lg": 1}


def piece_exists(b, rel):
    d = b.plus(rel)
    return d.at_least(0) and d.at_most(NB - 1)


def pieces_at(b, n, place):
    found = []
    for at, (step, pl, kind, j, rel) in enumerate(PIECES):
        if step == n and pl == place and piece_exists(b, rel):
            found.append((kind, j, b.plus(rel), piece_before(b, at)))
    return found


def piece_before(b, at):
    for bb, upto in ((b, at), (b.plus(-1), len(PIECES))):
        if bb.fixed and bb.off < PROLOGUE:
            return None
        for _, _, kind, j, rel in reversed(PIECES[:upto]):
            if piece_exists(bb, rel):
                return kind, j, bb.plus(rel)
    return None


def slot(d, g):
    return HG * (2 * d.par + g if g < 2 else 2 + g)


def build(nc, x, wqT, bq, wkT, bk, wvT, bv, woT, bo, J, lam, lns, lnb, gwT, Wg, Wu, Wd, sWg, sWu, sWd, out):
    x_v = x.rearrange("b (t p) d -> b p t d", p=P)
    k_parts = nc.dram_tensor("k_parts", [2, 2, 2, H, HD, S], F32, kind="Internal").ap()
    q_parts = nc.dram_tensor("q_parts", [2, 2, 2, H, HD, S], F32, kind="Internal").ap()
    x1_d = nc.dram_tensor("x1_d", [NB, P, TT, D], F32, kind="Internal").ap()
    ys_d = nc.dram_tensor("ys_d", [NT, P, D], F32, kind="Internal").ap()
    xs_d = nc.dram_tensor("xs_d", [NSLOT * P, D], F32, kind="Internal").ap()
    yo_d = nc.dram_tensor("yo_d", [NSLOT * P, D], F32, kind="Internal").ap()

    top = ExitStack()
    with top:
        def sbt(ctx, name, shape, dt=F32):
            return ctx.enter_context(nc.sbuf_tensor(name, shape, dt))

        ident = sbt(top, "ident", [P, P])
        ones = sbt(top, "ones", [P, P])
        mv2 = sbt(top, "mv2", [P, NT, 2])
        eps = sbt(top, "eps", [P, 1])
        gws = sbt(top, "gws", [P, KT, NE])
        gwb = sbt(top, "gwb", [P, KT, NE])
        logits = sbt(top, "logits", [P, NT, NE])
        xs_zeroed = top.enter_context(nc.semaphore("xs_zeroed"))

        with ExitStack() as c:
            attention_stage(nc, c, sbt, x_v, wqT, bq, wkT, bk, wvT, bv, woT, bo, J, lam,
                            k_parts, q_parts, x1_d, xs_d, ident, ones, mv2, eps, xs_zeroed,
                            lns, lnb, gwT, gws, gwb, logits)
        with ExitStack() as c:
            moe_stages(nc, c, sbt, gws, gwb, logits, Wg, Wu, Wd, sWg, sWu, sWd, out,
                       x1_d, ys_d, xs_d, yo_d, ident, ones, mv2, eps)


def attention_stage(nc, ctx, sbt, x_v, wqT, bq, wkT, bk, wvT, bv, woT, bo, J, lam,
                    k_parts, q_parts, x1_d, xs_d, ident, ones, mv2, eps, xs_zeroed,
                    lns, lnb, gwT, gws, gwb, logits):
    def sb(name, shape, dt=F32):
        return sbt(ctx, name, shape, dt)

    def sem(name):
        return ctx.enter_context(nc.semaphore(name))

    wq = sb("wq", [P, KT, D])
    wk = sb("wk", [P, KT, D])
    wv = sb("wv", [P, KT, D])
    wo = sb("wo", [P, KT, D])
    bq_c = sb("bq_c", [P, 2])
    bk_c = sb("bk_c", [P, 2])
    bv_b = sb("bv_b", [P, D])
    bo_b = sb("bo_b", [P, D])
    lam_b = sb("lam_b", [P, 1])
    jb = sb("jb", [P, 2, P])
    ident_bf = sb("ident_bf", [P, P], BF16)
    mask_bf = sb("mask_bf", [P, P], BF16)
    mv1 = sb("mv1", [P, NT, 2])
    rstd1 = sb("rstd1", [P, NT])
    st1 = sb("st1", [P, 2, TT, 6])
    zrows = sb("zrows", [P, ZR * D])
    pace_v = sb("pace_v", [1, 1])

    ks = sb("ks", [P, 6 * HG, S], F32R)

    with nc.cleanup_on_exit(), ExitStack() as c1:
        gw = sbt(c1, "gw", [P, KT, NE])
        sc = sbt(c1, "ln_sc", [P, KT])
        bi = sbt(c1, "ln_bi", [P, KT])
        xs1 = sbt(c1, "xs1", [P, EARLY, TT, D])
        s_w = nc.alloc_semaphore("s_w")
        s_j = nc.alloc_semaphore("s_j")
        s_x = [nc.alloc_semaphore(f"s_x{r}") for r in range(EARLY)]
        s_kz = nc.alloc_semaphore("s_kz")
        s_jz = nc.alloc_semaphore("s_jz")
        s_id0 = nc.alloc_semaphore("s_id0")
        s_id = nc.alloc_semaphore("s_id")
        s_st = nc.alloc_semaphore("s_st")
        s_ag = nc.alloc_semaphore("s_ag")
        s_ep = nc.alloc_semaphore("s_ep")
        s_sq = nc.alloc_semaphore("s_sq")
        block = c1.enter_context(nc.Block())

        @block.sync
        def _(sp):
            for r in range(EARLY):
                sp.dma_start(xs1[:, r], x_v[r]).then_inc(s_x[r], 16)
            sp.wait_ge(s_w, 16 * 16)
            sp.wait_ge(s_j, 16 * H)

        @block.scalar
        def _(act):
            for t, src in ((wq, wqT), (wk, wkT), (wv, wvT), (wo, woT)):
                act.dma_start(t[:], src.rearrange("(k p) n -> p k n", p=P)).then_inc(s_w, 16)
            for g in range(2):
                for t, src in ((bq_c, bq), (bk_c, bk)):
                    act.dma_start(t[:, g:g + 1], src[g * P:(g + 1) * P].rearrange("(p o) -> p o", o=1)).then_inc(s_w, 16)
            act.dma_start(bv_b[:], bv.rearrange("(o n) -> o n", o=1).to_broadcast([P, D])).then_inc(s_w, 16)
            act.dma_start(bo_b[:], bo.rearrange("(o n) -> o n", o=1).to_broadcast([P, D])).then_inc(s_w, 16)
            act.dma_start(lam_b[:], lam.rearrange("(o n) -> o n", o=1).to_broadcast([P, 1])).then_inc(s_w, 16)
            act.dma_start(gw[:], gwT.rearrange("(k p) n -> p k n", p=P)).then_inc(s_w, 16)
            for k in range(KT):
                for t, src in ((sc, lns), (bi, lnb)):
                    act.dma_start(t[:, k:k + 1], src[k * P:(k + 1) * P].rearrange("(p o) -> p o", o=1)).then_inc(s_w, 16)
            act.wait_ge(s_jz, 1)
            for h in range(H):
                r = (h % PG) * HD
                act.dma_start(jb[r:r + HD, h // PG, r:r + HD], J[h]).then_inc(s_j, 16)
            act.wait_ge(s_ep, 1)
            act.wait_ge(s_ag, EARLY * TT)
            nc.scalar.activation(rstd1[:, 0:EARLY * TT], mv1[:, 0:EARLY * TT, 1], ACT.Sqrt, bias=eps[:, 0:1]).then_inc(s_sq, 1)

        @block.gpsimd
        def _(pool):
            nc.gpsimd.memset(jb[:], 0.0).then_inc(s_jz, 1)
            nc.gpsimd.memset(zrows[:], 0.0).then_inc(s_id0, 1)
            nc.gpsimd.memset(ident[:], 0.0).then_inc(s_id0, 1)
            nc.gpsimd.memset(ident_bf[:], 0.0).then_inc(s_id0, 1)
            nc.gpsimd.memset(mask_bf[:], 0.0).then_inc(s_id0, 1)
            nc.gpsimd.memset(ones[:], 1.0).then_inc(s_id0, 1)
            pool.wait_ge(s_id0, 5)
            for t in (ident, ident_bf):
                nc.gpsimd.affine_select(out=t[:], in_=t[:], compare_op=ALU.not_equal, fill=1.0, base=0,
                                        pattern=[[-1, P]], channel_multiplier=1).then_inc(s_id, 1)
            nc.gpsimd.affine_select(out=mask_bf[:], in_=mask_bf[:], compare_op=ALU.is_ge, fill=MASK, base=0,
                                    pattern=[[-1, P]], channel_multiplier=1).then_inc(s_id, 1)
            pool.wait_ge(s_id, 3)
            pool.wait_ge(s_jz, 1)
            nc.gpsimd.memset(ks[MROW:P].bitcast(F32), 1.0).then_inc(s_kz, 1)
            pool.wait_ge(s_kz, 1)
            pool.wait_ge(s_w, 16 * 16)
            for k in range(KT):
                nc.gpsimd.tensor_scalar(gws[:, k], gw[:, k], sc[:, k:k + 1], None, ALU.mult)
                nc.gpsimd.tensor_scalar(gwb[:, k], gw[:, k], bi[:, k:k + 1], None, ALU.mult)
            pool.wait_ge(s_j, 16 * H)
            nc.gpsimd.tensor_scalar(jb[:], jb[:], lam_b[:, 0:1], None, ALU.mult).then_inc(s_id, 1)

        @block.vector
        def _(dve):
            nc.vector.memset(eps[:], EPS).then_inc(s_ep, 1)

            for r in range(EARLY):
                dve.wait_ge(s_x[r], 16)
                if r >= 2:
                    dve.wait_ge(s_ag, (r - 1) * TT)
                for t in range(TT):
                    nc.vector.bn_stats(st1[:, r % 2, t], xs1[:, r, t]).then_inc(s_st, 1)
                dve.wait_ge(s_st, (r + 1) * TT)
                for t in range(TT):
                    nc.vector.bn_aggr(mv1[:, r * TT + t], st1[:, r % 2, t]).then_inc(s_ag, 1)
            dve.wait_ge(s_sq, 1)
            nc.vector.reciprocal(rstd1[:, 0:EARLY * TT], rstd1[:, 0:EARLY * TT])

    qs = sb("qs", [P, 6 * HG, S], F32R)
    xn = sb("xn", [P, TT, D])
    xT = sb("xT", [P, KT, S])
    lin = sb("lin", [P, 2, S])
    th = sb("th", [P, 2, S])
    part = {n: sb("part_" + n, [P, 2, S], F32R) for n in ("kh", "kl", "th", "tl")}
    vt = sb("vt", [P, 2, TT, H, 2 * HD])
    probs = sb("probs", [P, 2, HG, S])
    mx = sb("mx", [P, 2, TT, HG])
    nm = sb("nm", [P, TT, P], F32R)
    mT = sb("mT", [P, S], F32R)
    osb = sb("osb", [P, S])
    rec = sb("rec", [P, TT, HG])
    on = sb("on", [P, 2, TT, D])
    onT = sb("onT", [P, KT, S])
    xres = sb("xres", [P, TT, D])
    st2 = sb("st2", [P, TT, 6])
    mvs = sb("mvs", [P, TT, 2])
    pace = sb("pace", [1, 2])

    ps_rows = [ctx.enter_context(nc.psum_tensor(f"ps_rows{r}", [P, S], F32)) for r in range(2)]
    ps_cols = [ctx.enter_context(nc.psum_tensor(f"ps_cols{r}", [P, 2, S], F32)) for r in range(2)]
    ps_o = ctx.enter_context(nc.psum_tensor("ps_o", [P, S], F32))
    ps_m = ctx.enter_context(nc.psum_tensor("ps_m", [P, S], F32))

    rows_ready = sem("rows_ready")
    max_done = sem("max_done")
    nm_ready = sem("nm_ready")
    nmh_ready = sem("nmh_ready")
    mrow_loaded = sem("mrow_loaded")
    cols_ready = sem("cols_ready")
    exp_done = sem("exp_done")
    sel_done = sem("sel_done")
    pv_done = sem("pv_done")
    o_taken = sem("o_taken")
    ready = {k: sem(k + "_ready") for k in PER_BATCH}
    taken = {k: sem(k + "_taken") for k in PER_BATCH}
    x_loaded = sem("x_loaded")
    xn_ready = sem("xn_ready")
    xres_loaded = sem("xres_loaded")
    xres_ready = sem("xres_ready")
    kth_done = sem("kth_done")
    hi_done = sem("hi_done")
    thi_done = sem("thi_done")
    lo_done = sem("lo_done")
    tlo_done = sem("tlo_done")
    lin_out = [sem(f"lin_out{r}") for r in range(2)]
    tan_out = [sem(f"tan_out{r}") for r in range(2)]
    stack01 = [sem(f"stack01_{r}") for r in range(2)]
    stack23 = [sem(f"stack23_{r}") for r in range(2)]
    rec_ready = sem("rec_ready")
    x1_stored = [sem(f"x1_stored{r}") for r in range(2)]
    st2_ready = sem("st2_ready")
    mvs_ready = sem("mvs_ready")
    const_ready = sem("const_ready")
    ring_loaded = [sem(f"ring_loaded{r}") for r in range(4)]
    st1_ready = sem("st1_ready")
    mv1_ready = sem("mv1_ready")
    root1 = sem("root1")
    rstd1_ready = sem("rstd1_ready")

    ring = [probs[:, r // 2, r % 2 * 2:r % 2 * 2 + 2].rearrange("p h s -> p (h s)").rearrange("p (t d) -> p t d", t=TT)
            for r in range(4)]

    def count(kind, j, b):
        return b.v * PER_BATCH[kind] + j + 1

    def unit(b, n):
        m = n + LEAD
        return b.plus(m // STEPS), (m % STEPS) // TT, m % TT

    block = ctx.enter_context(nc.Block())

    @block.tensor
    def _(pe):
        def piece(b, n, place):
            for kind, j, d, before in pieces_at(b, n, place):
                if before:
                    pe.wait_ge(taken[before[0]], count(*before))
                if kind == "xt":
                    pe.wait_ge(xn_ready, d.v + 1)
                    for t in range(TT):
                        mm = nc.tensor.transpose(ps_m[:, t * P:(t + 1) * P], xn[:, t, j * P:(j + 1) * P], ident[:])
                elif kind in ("k", "q"):
                    pe.wait_ge(taken["xt"], count("xt", 1, d))
                    w = wk if kind == "k" else wq
                    for k in range(KT):
                        mm = nc.tensor.matmul(ps_m[:], w[:, k, j * P:(j + 1) * P], xT[:, k], start=k == 0, stop=k == KT - 1)
                elif kind == "qj":
                    pe.wait_ge(kth_done, d.v * 4 + 3 + j)
                    mm = nc.tensor.matmul(ps_m[:], jb[:, j], th[:, j], start=True, stop=True)
                elif kind == "v":
                    for tt in range(2):
                        t = 2 * j + tt
                        for k in range(KT):
                            mm = nc.tensor.matmul(ps_m[:, tt * D:(tt + 1) * D], xT[:, k, t * P:(t + 1) * P], wv[:, k],
                                                  start=k == 0, stop=k == KT - 1)
                elif kind == "mt":
                    pe.wait_ge(nm_ready, d.v * G + j + 1)
                    for t in range(TT):
                        mm = nc.tensor.transpose(ps_m[:, t * P:(t + 1) * P], nm[:, t].bitcast(F32), ident[:])
                elif kind == "ot":
                    pe.wait_ge(o_taken, d.v * G + j + 1)
                    for t in range(TT):
                        mm = nc.tensor.transpose(ps_m[:, t * P:(t + 1) * P], osb[:, t * P:(t + 1) * P], ident[:])
                elif kind == "ont":
                    pe.wait_ge(taken["ot"], count("ot", G - 1, d))
                    for t in range(TT):
                        mm = nc.tensor.transpose(ps_m[:, t * P:(t + 1) * P], on[:, d.par, t, j * P:(j + 1) * P], ident[:])
                elif kind == "out":
                    pe.wait_ge(taken["ont"], count("ont", 1, d))
                    for tt in range(2):
                        t = 2 * j + tt
                        for k in range(KT):
                            mm = nc.tensor.matmul(ps_m[:, tt * D:(tt + 1) * D], onT[:, k, t * P:(t + 1) * P], wo[:, k],
                                                  start=k == 0, stop=k == KT - 1)
                elif kind == "gt":
                    pe.wait_ge(taken["out"], count("out", 1, d))
                    for t in range(TT):
                        mm = nc.tensor.transpose(ps_m[:, t * P:(t + 1) * P], xres[:, t, j * P:(j + 1) * P], ident[:])
                elif kind == "lg":
                    pe.wait_ge(taken["gt"], count("gt", 1, d))
                    for t in range(TT):
                        for k in range(KT):
                            mm = nc.tensor.matmul(ps_m[:, t * NE:(t + 1) * NE], onT[:, k, t * P:(t + 1) * P], gws[:, k],
                                                  start=k == 0, stop=k == KT - 1)
                mm.then_inc(ready[kind], 1)

        def rows(b, n, h):
            d, g, it = unit(b, n)
            if not (d.at_least(0) and d.at_most(NB - 1)):
                return
            first = d.fixed and d.off == 0 and g == 0 and it == 0 and h < 2
            if g != 1 and it == 0 and h == 0:
                if g == 0:
                    pe.wait_ge(stack01[d.par], (d.half() + 1) * LOADS)
                else:
                    pe.wait_ge(stack23[g - 2], (d.v + 1) * LOADS)
            if not first:
                pe.wait_ge(max_done, d.v * (STEPS * HG) + (g * TT + it) * HG + h - 1)
            hh = slot(d, g) + h
            bank = ps_rows[h % 2]
            nc.tensor.matmul(bank[:, 0:(it + 1) * P], qs[0:STACK, hh, it * P:(it + 1) * P],
                             ks[0:STACK, hh, 0:(it + 1) * P], start=True, stop=False)
            nc.tensor.matmul(bank[:, it * P:(it + 1) * P], ident_bf[:], mask_bf[:], start=False, stop=True)\
                .then_inc(rows_ready, 1)

        def cols(b, n, pair):
            g, jt = n // TT, n % TT
            if pair == 0 and jt == 0:
                pe.wait_ge(mrow_loaded, (b.v * G + g + 1) * 16 * HG)
            if not (b.fixed and b.off == 0 and n == 0):
                pe.wait_ge(exp_done, (b.v * STEPS + n) * 2 + pair - 1)
            for e in range(2):
                hh = slot(b, g) + 2 * pair + e
                mm = nc.tensor.matmul(ps_cols[pair][:, e, jt * P:S], ks[0:MROW + 2, hh, jt * P:(jt + 1) * P],
                                      qs[0:MROW + 2, hh, jt * P:S], start=True, stop=True)
            mm.then_inc(cols_ready, 1)

        def pv(b, n):
            g, jt = n // TT, n % TT
            pe.wait_ge(sel_done, b.v * STEPS + n + 1)
            if n == 0:
                pe.wait_ge(taken["v"], count("v", 1, b))
            if jt == 0 and not (b.fixed and b.off == 0 and g == 0):
                pe.wait_ge(o_taken, b.v * G + g)
            for h in range(HG):
                mm = nc.tensor.matmul(ps_o[2 * HD * h:2 * HD * (h + 1), jt * P:S], vt[:, b.par, jt, g * HG + h],
                                      probs[:, n % 2, h, jt * P:S], start=jt == 0, stop=jt == TT - 1)
            mm.then_inc(pv_done, 1)

        def batch(b):
            att = b.at_least(0) and b.at_most(NB - 1)
            for n in range(STEPS):
                if b.fixed and b.off == PROLOGUE and n == 8:
                    pe.wait_ge(const_ready, 2)
                rows(b, n, 0)
                if att:
                    cols(b, n, 0)
                rows(b, n, 1)
                piece(b, n, 0)
                rows(b, n, 2)
                if att:
                    cols(b, n, 1)
                rows(b, n, 3)
                if n > 0 and att:
                    pv(b, n - 1)
                if n == 0 and b.at_least(1):
                    pv(b.plus(-1), STEPS - 1)
                piece(b, n, 1)

        over_batches(pe, batch)

    @block.scalar
    def _(act):
        def piece(b, n, place):
            for kind, j, d, _ in pieces_at(b, n, place):
                if kind == "xt":
                    act.wait_ge(ready[kind], count(kind, j, d))
                    nc.scalar.activation(xT[:, j], ps_m[:], ACT.Copy).then_inc(taken[kind], 1)
                elif kind in ("k", "q"):
                    c = 0 if kind == "k" else 2
                    act.wait_ge(taken[kind], count(kind, j, d))
                    if kind == "k":
                        if d.at_least(1):
                            act.wait_ge(ready["qj"], d.v * 2 + j - 1)
                    else:
                        act.wait_ge(tlo_done, d.v * 2 + 1 + j)
                    nc.scalar.activation(th[:, j], lin[:, j], ACT.Tanh, scale=1.0 if kind == "k" else 4.0)\
                        .then_inc(kth_done, 1)
                    if kind == "q" or d.at_least(1):
                        act.wait_ge(lin_out[j], (d.v * 2 + c // 2) * 32)
                    nc.scalar.activation(part["kh"][:, j], lin[:, j], ACT.Copy).then_inc(hi_done, 1)
                    if kind == "k":
                        if d.at_least(1):
                            act.wait_ge(tan_out[j], d.v * 64)
                        act.wait_ge(kth_done, d.v * 4 + j + 1)
                        nc.scalar.activation(part["th"][:, j], th[:, j], ACT.Copy).then_inc(thi_done, 1)
                elif kind == "qj":
                    act.wait_ge(ready[kind], count(kind, j, d))
                    act.wait_ge(tan_out[j], d.v * 64 + 32)
                    nc.scalar.activation(part["th"][:, j], ps_m[:], ACT.Copy).then_inc(thi_done, 1)
                elif kind == "mt":
                    act.wait_ge(ready[kind], count(kind, j, d))
                    if j > 0 or d.at_least(1):
                        act.wait_ge(mrow_loaded, (d.v * G + j) * 16 * HG)
                    nc.scalar.activation(mT[0:2 * HG], ps_m[0:2 * HG], ACT.Copy).then_inc(taken[kind], 1)
                elif kind in ("ont", "gt"):
                    act.wait_ge(ready[kind], count(kind, j, d))
                    nc.scalar.activation(onT[:, j], ps_m[:], ACT.Copy).then_inc(taken[kind], 1)

        def exps(b, n, pair):
            g, jt = n // TT, n % TT
            act.wait_ge(cols_ready, (b.v * STEPS + n) * 2 + pair + 1)
            if pair == 0 and not (b.fixed and b.off == 0 and n < 2):
                act.wait_ge(pv_done, b.v * STEPS + n - 1)
            nc.scalar.activation(probs[:, n % 2, 2 * pair:2 * pair + 2, jt * P:S], ps_cols[pair][:, :, jt * P:S],
                                 ACT.Exp).then_inc(exp_done, 1)

        def o_copy(b, g):
            act.wait_ge(pv_done, b.v * STEPS + (g + 1) * TT)
            if g > 0 or b.at_least(1):
                act.wait_ge(ready["ot"], b.v * G + g)
            nc.scalar.activation(osb[:], ps_o[:], ACT.Copy).then_inc(o_taken, 1)

        def batch(b):
            att = b.at_least(0) and b.at_most(NB - 1)
            for n in range(STEPS):
                if b.fixed and b.off == PROLOGUE and n == 14:
                    act.wait_ge(mv1_ready, NB - EARLY)
                    nc.scalar.activation(rstd1[:, EARLY * TT:], mv1[:, EARLY * TT:, 1], ACT.Sqrt, bias=eps[:, 0:1]).then_inc(root1, 1)
                if att:
                    exps(b, n, 0)
                piece(b, n, 0)
                if att:
                    exps(b, n, 1)
                if n % TT == 0:
                    if n > 0 and att:
                        o_copy(b, n // TT - 1)
                    if n == 0 and b.at_least(1):
                        o_copy(b.plus(-1), G - 1)
                piece(b, n, 1)

        over_batches(act, batch)

    @block.vector
    def _(dve):
        def layer_norm(d):
            dve.wait_ge(x_loaded, (d.v + 1) * 16)
            for t in range(TT):
                if d.fixed:
                    m, r = mv1[:, d.off * TT + t, 0:1], rstd1[:, d.off * TT + t:d.off * TT + t + 1]
                else:
                    m = mv1[:, bass.ds(d.v * TT + t, 1), 0]
                    r = rstd1[:, bass.ds(d.v * TT + t, 1)]
                ts = nc.vector.tensor_scalar(xn[:, t], xn[:, t], m, r, ALU.subtract, ALU.mult)
            ts.then_inc(xn_ready, 1)

        def maximum(b, n, h):
            d, g, it = unit(b, n)
            if not (d.at_least(0) and d.at_most(NB - 1)):
                return
            gb = g % 2
            dve.wait_ge(rows_ready, d.v * (STEPS * HG) + (g * TT + it) * HG + h + 1)
            nc.vector.tensor_reduce(mx[:, gb, it, h:h + 1], ps_rows[h % 2][:, 0:(it + 1) * P], AX.X, ALU.max)\
                .then_inc(max_done, 1)
            if it == TT - 1 and h == HG - 1:
                dve.wait_ge(max_done, d.v * (STEPS * HG) + (g + 1) * TT * HG)
                if g > 0 or d.at_least(1):
                    dve.wait_ge(ready["mt"], d.v * G + g)
                pair = nm[:, :, 0:2 * HG].rearrange("p t (h two) -> p t h two", two=2)
                nc.vector.tensor_scalar(pair[:, :, :, 0], mx[:, gb], -1.0, None, ALU.mult).then_inc(nmh_ready, 1)
                dve.wait_ge(nmh_ready, d.v * G + g + 1)
                nc.vector.scalar_tensor_tensor(out=pair[:, :, :, 1], in0=mx[:, gb], scalar=-1.0,
                                               in1=pair[:, :, :, 0].bitcast(F32), op0=ALU.mult, op1=ALU.subtract)\
                    .then_inc(nm_ready, 1)

        def piece(b, n, place):
            for kind, j, d, _ in pieces_at(b, n, place):
                if kind in ("xt", "mt", "ont", "gt"):
                    continue
                dve.wait_ge(ready[kind], count(kind, j, d))
                if kind == "k":
                    if d.at_least(1):
                        dve.wait_ge(lo_done, d.v * 4 - 1 + j)
                    nc.vector.tensor_scalar(lin[:, j], ps_m[:], bk_c[:, j:j + 1], None, ALU.add).then_inc(taken[kind], 1)
                elif kind == "q":
                    dve.wait_ge(lo_done, d.v * 4 + 1 + j)
                    nc.vector.tensor_scalar(lin[:, j], ps_m[:], bq_c[:, j:j + 1], 0.25, ALU.add, ALU.mult)\
                        .then_inc(taken[kind], 1)
                elif kind == "qj":
                    dve.wait_ge(thi_done, d.v * 4 + 3 + j)
                    dve.wait_ge(tan_out[j], d.v * 64 + 32)
                    nc.vector.tensor_tensor(part["tl"][:, j], ps_m[:], part["th"][:, j].bitcast(F32), ALU.subtract)\
                        .then_inc(taken[kind], 1)
                elif kind == "v":
                    for tt in range(2):
                        a = nc.vector.tensor_tensor(
                            vt[:, d.par, 2 * j + tt, :, 0:HD],
                            ps_m[:, tt * D:(tt + 1) * D].rearrange("p (h e) -> p h e", h=H),
                            bv_b[:].rearrange("p (h e) -> p h e", h=H), ALU.add)
                    a.then_inc(taken[kind], 1)
                elif kind == "ot":
                    pso = ps_m[:].rearrange("p (t h e) -> p t h e", t=TT, h=HG)
                    nc.vector.reciprocal(rec[:], pso[:, :, :, HD]).then_inc(rec_ready, 1)
                    dve.wait_ge(rec_ready, d.v * G + j + 1)
                    nc.vector.tensor_tensor(
                        on[:, d.par, :, j * HG * HD:(j + 1) * HG * HD].rearrange("p t (h e) -> p t h e", h=HG),
                        pso[:, :, :, 0:HD], rec[:].unsqueeze(3).to_broadcast([P, TT, HG, HD]), ALU.mult)\
                        .then_inc(taken[kind], 1)
                elif kind == "lg":
                    at = d.v * TT
                    nc.vector.tensor_copy(logits[:, at:at + TT] if d.fixed else logits[:, bass.ds(at, TT)],
                                          ps_m[:, 0:TT * NE].rearrange("p (t e) -> p t e", t=TT)).then_inc(taken[kind], 1)
                elif kind == "out":
                    dve.wait_ge(xres_ready, d.v + 1)
                    x1 = xres[:, 2 * j:2 * j + 2]
                    nc.vector.tensor_tensor(x1, ps_m[:].rearrange("p (t e) -> p t e", t=2), x1, ALU.add)\
                        .then_inc(taken[kind], 1)

        def statistics(d, t):
            if t == 0 or t == 2:
                dve.wait_ge(taken["out"], count("out", t // 2, d))
            nc.vector.bn_stats(st2[:, t], xres[:, t]).then_inc(st2_ready, 1)
            if t == TT - 1:
                dve.wait_ge(st2_ready, (d.v + 1) * TT)
                nc.vector.tensor_copy(pace_v[:], eps[0:1])
                for k in range(TT):
                    s_ = nc.vector.bn_aggr(mvs[:, k], st2[:, k])
                s_.then_inc(mvs_ready, 1)
                dve.wait_ge(mvs_ready, d.v + 1)
                at = d.v * TT
                nc.vector.tensor_copy(mv2[:, at:at + TT] if d.fixed else mv2[:, bass.ds(at, TT)], mvs[:])

        def statistics1(k):
            dve.wait_ge(ring_loaded[k % 4], (k // 4 + 1) * 16)
            if k >= 2:
                dve.wait_ge(mv1_ready, k - 1)
            for t in range(TT):
                nc.vector.bn_stats(st1[:, k % 2, t], ring[k % 4][:, t]).then_inc(st1_ready, 1)
            dve.wait_ge(st1_ready, (k + 1) * TT)
            for t in range(TT):
                a = nc.vector.bn_aggr(mv1[:, (EARLY + k) * TT + t], st1[:, k % 2, t])
            a.then_inc(mv1_ready, 1)

        def batch(b):
            for n in range(STEPS):
                if b.fixed and b.off == PROLOGUE and n < NB - EARLY:
                    statistics1(n)
                if b.fixed and b.off == 0 and n == 0:
                    dve.wait_ge(root1, 1)
                    nc.vector.reciprocal(rstd1[:, EARLY * TT:], rstd1[:, EARLY * TT:]).then_inc(rstd1_ready, 1)
                    dve.wait_ge(rstd1_ready, 1)
                maximum(b, n, 0)
                maximum(b, n, 1)
                piece(b, n, 0)
                maximum(b, n, 2)
                maximum(b, n, 3)
                piece(b, n, 1)
                if 11 <= n < 11 + TT and piece_exists(b, -1):
                    statistics(b.plus(-1), n - 11)
                if n == 9 and b.plus(2).at_most(NB - 1):
                    layer_norm(b.plus(2))

        layer_norm(Batch(0, 0))
        nc.vector.memset(nm[:].bitcast(F32), 0.0).then_inc(const_ready, 1)
        nc.vector.memset(vt[:, :, :, :, HD:2 * HD], 1.0).then_inc(const_ready, 1)
        over_batches(dve, batch)

    @block.gpsimd
    def _(pool):
        def piece(b, n, place):
            for kind, j, d, _ in pieces_at(b, n, place):
                if kind in ("k", "q"):
                    c = 0 if kind == "k" else 2
                    pool.wait_ge(hi_done, d.v * 4 + c + j + 1)
                    if kind == "q" or d.at_least(1):
                        pool.wait_ge(lin_out[j], (d.v * 2 + c // 2) * 32)
                    nc.gpsimd.tensor_tensor(part["kl"][:, j], lin[:, j], part["kh"][:, j].bitcast(F32), ALU.subtract)\
                        .then_inc(lo_done, 1)
                    if kind == "k":
                        pool.wait_ge(thi_done, d.v * 4 + j + 1)
                        if d.at_least(1):
                            pool.wait_ge(tan_out[j], d.v * 64)
                        nc.gpsimd.tensor_tensor(part["tl"][:, j], th[:, j], part["th"][:, j].bitcast(F32), ALU.subtract)\
                            .then_inc(tlo_done, 1)

        def select(b, n):
            jt = n % TT
            pool.wait_ge(exp_done, (b.v * STEPS + n) * 2 + 2)
            nc.gpsimd.tensor_tensor(pace[:, n % 2:n % 2 + 1], eps[0:1], eps[0:1], ALU.add)
            blk = probs[:, n % 2, :, jt * P:(jt + 1) * P]
            nc.gpsimd.affine_select(out=blk, in_=blk, compare_op=ALU.is_ge, fill=0.0, base=0,
                                    pattern=[[0, HG], [1, P]], channel_multiplier=-1).then_inc(sel_done, 1)

        def batch(b):
            att = b.at_least(0) and b.at_most(NB - 1)
            for n in range(STEPS):
                piece(b, n, 0)
                if att:
                    select(b, n)
                piece(b, n, 1)
                if n == 6 and piece_exists(b, -1):
                    d = b.plus(-1)
                    pool.wait_ge(xres_loaded, (d.v + 1) * 16)
                    nc.gpsimd.tensor_tensor(xres[:], xres[:], bo_b[:].unsqueeze(1).to_broadcast([P, TT, D]), ALU.add)\
                        .then_inc(xres_ready, 1)

        over_batches(pool, batch)

    @block.sync
    def _(sp):
        assert NSLOT == (NB - 1) * ZR * ZR
        xs_z = xs_d.rearrange("(a p s) d -> a p (s d)", p=P, s=ZR)

        def store(d, kind, j, row, done, tile, out_sem):
            dram = k_parts if kind == "k" else q_parts
            sp.wait_ge(*done)
            sp.nop(nofuse=True)
            sp.dma_start(dram[d.par, row[0], row[1], j * PG:(j + 1) * PG].rearrange("h r t -> (h r) t"), part[tile][:, j].bitcast(F32))\
                .then_inc(out_sem[j], 16)

        def store_parts(d, kind, j):
            if kind == "k" and j == 0 and d.at_least(2):
                sp.wait_ge(stack23[1], (d.v - 1) * LOADS)
                sp.nop(nofuse=True)
            if kind in ("k", "q"):
                n = d.v * 4 + (0 if kind == "k" else 2) + j + 1
                store(d, kind, j, (0, 0), (hi_done, n), "kh", lin_out)
                store(d, kind, j, (1, 0), (lo_done, n), "kl", lin_out)
            if kind in ("k", "qj"):
                n = d.v * 4 + (0 if kind == "k" else 2) + j + 1
                store(d, kind, j, (0, 1), (thi_done, n), "th", tan_out)
                store(d, kind, j, (1, 1), (tlo_done, d.v * 2 + j + 1) if kind == "k" else (taken["qj"], count("qj", j, d)),
                      "tl", tan_out)

        def load_stack(d, g, groups, stack, dram, pair, done, sides=(0, 1)):
            for a, part_no in enumerate(pair):
                for c in sides:
                    r = (2 * a + c) * HD
                    sp.dma_start(stack[r:r + HD, slot(d, g):slot(d, g) + HG * groups].bitcast(F32),
                                 dram[d.par, part_no, c, HG * g:HG * (g + groups)].rearrange("h r t -> r h t"))\
                        .then_inc(done, 16)

        KEY_PARTS, QUERY_PARTS = (0, 1, 0), (0, 0, 1)

        def load_keys01(d):
            for j in range(2):
                sp.wait_ge(lin_out[j], d.v * 64 + 32)
                sp.nop(nofuse=True)
                sp.wait_ge(tan_out[j], d.v * 64 + 32)
                sp.nop(nofuse=True)
            if d.at_least(2):
                sp.wait_ge(cols_ready, (d.v - 1) * STEPS * 2)
                sp.nop(nofuse=True)
            load_stack(d, 0, 2, ks, k_parts, KEY_PARTS, stack01[d.par])

        def load_queries01(d, side):
            for j in range(2):
                sp.wait_ge((lin_out, tan_out)[side][j], (d.v + 1) * 64)
                sp.nop(nofuse=True)
            load_stack(d, 0, 2, qs, q_parts, QUERY_PARTS, stack01[d.par], (side,))

        def load_group(d, g):
            if d.at_least(1):
                sp.wait_ge(cols_ready, ((d.v - 1) * STEPS + (g + 1) * TT) * 2)
                sp.nop(nofuse=True)
            load_stack(d, g, 1, ks, k_parts, KEY_PARTS, stack23[g - 2])
            load_stack(d, g, 1, qs, q_parts, QUERY_PARTS, stack23[g - 2])

        def max_rows(d, g):
            sp.wait_ge(taken["mt"], d.v * G + g + 1)
            sp.nop(nofuse=True)
            for h in range(HG):
                sp.dma_start(qs[MROW:MROW + 2, slot(d, g) + h].bitcast(F32), mT[2 * h:2 * h + 2, :].bitcast(F32)).then_inc(mrow_loaded, 16)

        def x_of(view, d):
            return view[d.off] if d.fixed else view[bass.ds(d.v, 1)].rearrange("o p t e -> (o p) t e")

        def batch(b):
            for n in range(STEPS):
                if b.fixed and b.off == PROLOGUE and n < NB - EARLY - 4:
                    sp.wait_ge(st1_ready, (n + 1) * TT)
                    sp.dma_start(ring[n % 4], x_v[EARLY + 4 + n]).then_inc(ring_loaded[n % 4], 16)
                if n == 3 and b.plus(2).at_most(NB - 1):
                    sp.wait_ge(ready["xt"], (b.v + 2) * 2)
                    sp.nop(nofuse=True)
                    sp.dma_start(xn[:], x_of(x_v, b.plus(2))).then_inc(x_loaded, 16)
                if n == 0 and b.at_least(0) and b.at_most(NB - 1):
                    load_group(b, 3)
                for place in range(2):
                    for kind, j, d, _ in pieces_at(b, n, place):
                        if kind in ("k", "q", "qj"):
                            store_parts(d, kind, j)
                            if (kind, j) == ("q", 1):
                                load_keys01(d)
                            if (kind, j) == ("qj", 1):
                                load_queries01(d, 0)
                                load_queries01(d, 1)
                        elif kind == "mt":
                            max_rows(d, j)
                        elif kind == "out":
                            sp.wait_ge(taken["out"], count("out", j, d))
                            sp.nop(nofuse=True)
                            sp.dma_start(x_of(x1_d, d)[:, 2 * j:2 * j + 2], xres[:, 2 * j:2 * j + 2]).then_inc(x1_stored[j], 16)
                if n == 12 and b.plus(1).at_most(NB - 1):
                    load_group(b.plus(1), 2)
                if n in (9, 10, 11) and b.at_least(0) and b.at_most(NB - 2):
                    at = b.v * ZR + n - 9
                    dest = xs_z[at] if b.fixed else xs_z[bass.ds(at, 1)].rearrange("o p n -> (o p) n")
                    sp.dma_start(dest, zrows[:]).then_inc(xs_zeroed, 16)
                if n == 15 and b.at_least(0) and b.at_most(NB - 1):
                    if b.at_least(1):
                        sp.wait_ge(x1_stored[0], b.v * 16)
                        sp.nop(nofuse=True)
                        sp.wait_ge(x1_stored[1], b.v * 16)
                        sp.nop(nofuse=True)
                        sp.wait_ge(st2_ready, b.v * TT)
                        sp.nop(nofuse=True)
                        sp.wait_ge(ready["gt"], b.v * 2)
                        sp.nop(nofuse=True)
                    sp.dma_start(xres[:], x_of(x_v, b)).then_inc(xres_loaded, 16)

        sp.dma_start(xn[:], x_of(x_v, Batch(0, 0))).then_inc(x_loaded, 16)
        for q in range(4):
            sp.dma_start(ring[q], x_v[EARLY + q]).then_inc(ring_loaded[q], 16)
        over_batches(sp, batch)
        for j in range(2):
            sp.wait_ge(x1_stored[j], NB * 16)
        sp.wait_ge(xs_zeroed, NSLOT // ZR * 16)


def moe_stages(nc, ctx, sbt, gws, gwb, logits, Wg, Wu, Wd, sWg, sWu, sWd, out,
               x1_d, ys_d, xs_d, yo_d, ident, ones, mv2, eps):
    pos = sbt(ctx, "pos", [P, NT, 2], I32)
    wgt = [sbt(ctx, f"wgt{r}", [P, NT]) for r in range(2)]
    slot_e = sbt(ctx, "slot_e", [1, NSLOT], I32)
    rstd2 = sbt(ctx, "rstd2", [P, NT])
    shared_weights = (sWg, sWu, sWd)

    with ExitStack() as c:
        xall = sbt(c, "xall", [P, NT, D])
        with nc.cleanup_on_exit(), ExitStack() as c1:
            route_stage(nc, c1, sbt, x1_d, xall, ones, mv2, eps, rstd2, logits, gws, gwb, pos, wgt, slot_e)
        with ExitStack() as c1:
            scatter_stage(nc, c1, sbt, shared_weights, x1_d, xall, ys_d, xs_d, ident, mv2, rstd2, pos)
    with ExitStack() as c:
        expert_stage(nc, c, sbt, Wg, Wu, Wd, xs_d, yo_d, ident, slot_e)
    with ExitStack() as c:
        combine_stage(nc, c, sbt, shared_weights, x1_d, yo_d, ys_d, out, ident, mv2, rstd2, pos, wgt)


PART_PAIRS = ((0, 0), (0, 1), (1, 0))


class SharedExpert:

    def __init__(self, nc, ctx, sbt, tag, base, count, weights, x1_d, ys_d, ident, mv2, rstd2):
        def sb(name, shape, dt=F32):
            return sbt(ctx, name + tag, shape, dt)

        def sem(name):
            return ctx.enter_context(nc.semaphore(name + tag))

        self.nc, self.base, self.count, self.weights = nc, base, count, weights
        self.x1_d, self.ys_d, self.ident, self.mv2, self.rstd2 = x1_d, ys_d, ident, mv2, rstd2
        self.w_in = sb("sw_in", [P, 3, KT * INTER])
        self.wg = sb("swg", [P, 2, KT, INTER], F32R)
        self.wu = sb("swu", [P, 2, KT, INTER], F32R)
        self.wd = sb("swd", [P, 2, IT, D], F32R)
        self.x1 = sb("x1s", [P, 2, TT, D])
        self.x2 = sb("x2n", [P, 2, TT, D])
        self.x2T = sb("x2T", [P, 2, 2, KT, S], F32R)
        self.sg = sb("sg", [P, 2, S])
        self.h = sb("h", [P, 2, S])
        self.hT = sb("hT", [P, 2, 2, IT, S], F32R)
        self.ysb = sb("ysb", [P, 2, 2, 2, D])
        self.xin = sb("xin", [P, TT, D])
        self.ps_t = [ctx.enter_context(nc.psum_tensor(f"ps_t{r}" + tag, [P, S], F32)) for r in range(2)]
        self.ps_g = [ctx.enter_context(nc.psum_tensor(f"ps_g{r}" + tag, [P, S], F32)) for r in range(2)]
        self.ps_u = [ctx.enter_context(nc.psum_tensor(f"ps_u{r}" + tag, [P, S], F32)) for r in range(2)]
        self.ps_y = [ctx.enter_context(nc.psum_tensor(f"ps_y{r}" + tag, [P, 2, D], F32)) for r in range(2)]
        self.w_loaded = sem("w_loaded")
        self.w_hi = sem("w_hi")
        self.w_lo = sem("w_lo")
        self.x1_loaded = [sem(f"x1_loaded{r}") for r in range(2)]
        self.xin_loaded = sem("xin_loaded")
        self.x2_ready = sem("x2_ready")
        self.xt_ready = sem("xt_ready")
        self.xt_hi = sem("xt_hi")
        self.xt_lo = sem("xt_lo")
        self.g_ready = sem("g_ready")
        self.u_ready = sem("u_ready")
        self.sg_ready = sem("sg_ready")
        self.h_ready = sem("h_ready")
        self.h_hi = sem("h_hi")
        self.h_lo = sem("h_lo")
        self.y_ready = sem("y_ready")
        self.y_taken = sem("y_taken")
        self.y_stored = [[sem(f"y_stored{r}{j}") for j in range(2)] for r in range(2)]

    def has(self, s):
        return s.at_least(0) and s.at_most(self.count - 1)

    def batch_of(self, view, s):
        return view[self.base + s.off] if s.fixed else view[bass.ds(s.v + self.base, 1)].rearrange("o p t d -> (o p) t d")

    def load_weights(self, eng):
        for m, (k, src) in enumerate(zip((KT, KT, IT), self.weights)):
            eng.dma_start(self.w_in[:, m].rearrange("p (k n) -> p k n", k=k), src.rearrange("(k p) n -> p k n", p=P))\
                .then_inc(self.w_loaded, 16)

    def load(self, eng, s):
        if not self.has(s):
            return
        if s.at_least(2):
            eng.wait_ge(self.y_taken, (s.v - 1) * 2)
            eng.nop(nofuse=True)
        eng.dma_start(self.x1[:, s.par], self.batch_of(self.x1_d, s)).then_inc(self.x1_loaded[s.par], 16)

    def load_in(self, eng, s):
        if not self.has(s):
            return
        if s.at_least(1):
            eng.wait_ge(self.x2_ready, s.v)
            eng.nop(nofuse=True)
        eng.dma_start(self.xin[:], self.batch_of(self.x1_d, s)).then_inc(self.xin_loaded, 16)

    def store(self, eng, s):
        if not self.has(s):
            return
        ys_v = self.ys_d.rearrange("(c t) p d -> c p t d", t=TT)
        for j in range(2):
            eng.wait_ge(self.y_taken, s.v * 2 + j + 1)
            eng.nop(nofuse=True)
            eng.dma_start(self.batch_of(ys_v, s)[:, 2 * j:2 * j + 2], self.ysb[:, s.par, j]).then_inc(self.y_stored[s.par][j], 16)

    def split_weights_hi(self, act):
        act.wait_ge(self.w_loaded, 3 * 16)
        for m, w in enumerate((self.wg, self.wu, self.wd)):
            self.nc.scalar.activation(w[:, 0].rearrange("p k n -> p (k n)"), self.w_in[:, m], ACT.Copy).then_inc(self.w_hi, 1)

    def split_weights_lo(self, dve):
        for m, w in enumerate((self.wg, self.wu, self.wd)):
            dve.wait_ge(self.w_hi, m + 1)
            hi, lo = (w[:, c].rearrange("p k n -> p (k n)") for c in range(2))
            self.nc.vector.tensor_tensor(lo, self.w_in[:, m], hi.bitcast(F32), ALU.subtract).then_inc(self.w_lo, 1)

    def transposes(self, pe, s):
        if not self.has(s):
            return
        nc = self.nc
        pe.wait_ge(self.x2_ready, s.v + 1)
        for k in range(KT):
            if s.at_least(1):
                pe.wait_ge(self.xt_lo, (s.v - 1) * KT + k + 1)
            for t in range(TT):
                mm = nc.tensor.transpose(self.ps_t[k][:, t * P:(t + 1) * P], self.x2[:, s.par, t, k * P:(k + 1) * P], self.ident[:])
            mm.then_inc(self.xt_ready, 1)

    def gate_up(self, pe, s, i):
        nc = self.nc
        if i == 0:
            pe.wait_ge(self.xt_lo, (s.v + 1) * KT)
        for w, bank, freed, done in ((self.wg, self.ps_g, self.sg_ready, self.g_ready),
                                     (self.wu, self.ps_u, self.h_ready, self.u_ready)):
            if i >= 2 or s.at_least(1):
                pe.wait_ge(freed, s.v * IT + i - 1)
            for at, (wp, xp) in enumerate(PART_PAIRS):
                for k in range(KT):
                    mm = nc.tensor.matmul(bank[i % 2][:], w[:, wp, k, i * P:(i + 1) * P], self.x2T[:, s.par, xp, k],
                                          start=at == 0 and k == 0, stop=at == 2 and k == KT - 1)
            mm.then_inc(done, 1)

    def down(self, pe, s):
        nc = self.nc
        pe.wait_ge(self.h_lo, s.v * IT + IT)
        for j in range(2):
            if s.at_least(1):
                pe.wait_ge(self.y_taken, s.v * 2 + j - 1)
            for tt in range(2):
                t = 2 * j + tt
                for at, (hp, wp) in enumerate(PART_PAIRS):
                    for i in range(IT):
                        mm = nc.tensor.matmul(self.ps_y[j][:, tt], self.hT[:, s.par, hp, i, t * P:(t + 1) * P], self.wd[:, wp, i],
                                              start=at == 0 and i == 0, stop=at == 2 and i == IT - 1)
            mm.then_inc(self.y_ready, 1)

    def tensor_round(self, pe, s):
        if self.has(s):
            self.gate_up(pe, s, 0)
        if self.has(s.plus(-1)):
            self.down(pe, s.plus(-1))
        if self.has(s):
            for i in range(1, IT):
                self.gate_up(pe, s, i)
                if i == 2:
                    self.transposes(pe, s.plus(1))

    def copies(self, act, s):
        if not self.has(s):
            return
        for k in range(KT):
            act.wait_ge(self.xt_ready, s.v * KT + k + 1)
            if s.at_least(2):
                act.wait_ge(self.u_ready, (s.v - 1) * IT)
            self.nc.scalar.activation(self.x2T[:, s.par, 0, k], self.ps_t[k][:], ACT.Copy).then_inc(self.xt_hi, 1)

    def scalar_round(self, act, s):
        if not self.has(s):
            return
        for i in range(IT):
            act.wait_ge(self.g_ready, s.v * IT + i + 1)
            if i >= 2 or s.at_least(1):
                act.wait_ge(self.h_ready, s.v * IT + i - 1)
            self.nc.scalar.activation(self.sg[:, i % 2], self.ps_g[i % 2][:], ACT.Silu).then_inc(self.sg_ready, 1)
            if i:
                self.upper(act, s, i - 1)
            if i == 2:
                self.copies(act, s.plus(1))
        self.upper(act, s, IT - 1)

    def upper(self, act, s, i):
        act.wait_ge(self.h_ready, s.v * IT + i + 1)
        if s.at_least(2):
            act.wait_ge(self.y_ready, (s.v - 1) * 2)
        self.nc.scalar.activation(self.hT[:, s.par, 0, i], self.h[:, i % 2], ACT.Copy).then_inc(self.h_hi, 1)

    def norm(self, dve, s):
        if not self.has(s):
            return
        dve.wait_ge(self.xin_loaded, (s.v + 1) * 16)
        if s.at_least(2):
            dve.wait_ge(self.xt_ready, (s.v - 1) * KT)
        for t in range(TT):
            at = (s.v + self.base) * TT + t
            if s.fixed:
                m, rs = self.mv2[:, at, 0:1], self.rstd2[:, at:at + 1]
            else:
                m, rs = self.mv2[:, bass.ds(at, 1), 0], self.rstd2[:, bass.ds(at, 1)]
            a = self.nc.vector.tensor_scalar(self.x2[:, s.par, t], self.xin[:, t], m, rs, ALU.subtract, ALU.mult)
        a.then_inc(self.x2_ready, 1)

    def product(self, dve, s, i):
        dve.wait_ge(self.u_ready, s.v * IT + i + 1)
        dve.wait_ge(self.sg_ready, s.v * IT + i + 1)
        if i >= 2 or s.at_least(1):
            dve.wait_ge(self.h_lo, s.v * IT + i - 1)
        self.nc.vector.tensor_tensor(self.h[:, i % 2], self.sg[:, i % 2], self.ps_u[i % 2][:], ALU.mult)\
            .then_inc(self.h_ready, 1)

    def lower(self, dve, s, i):
        dve.wait_ge(self.h_hi, s.v * IT + i + 1)
        self.nc.vector.tensor_tensor(self.hT[:, s.par, 1, i], self.h[:, i % 2], self.hT[:, s.par, 0, i].bitcast(F32), ALU.subtract)\
            .then_inc(self.h_lo, 1)

    def lower_rows(self, dve, s):
        if not self.has(s):
            return
        for k in range(KT):
            dve.wait_ge(self.xt_hi, s.v * KT + k + 1)
            self.nc.vector.tensor_tensor(self.x2T[:, s.par, 1, k], self.ps_t[k][:], self.x2T[:, s.par, 0, k].bitcast(F32),
                                         ALU.subtract).then_inc(self.xt_lo, 1)

    def outputs(self, dve, s):
        dve.wait_ge(self.x1_loaded[s.par], (s.half() + 1) * 16)
        for j in range(2):
            dve.wait_ge(self.y_ready, s.v * 2 + j + 1)
            if s.at_least(2):
                dve.wait_ge(self.y_stored[s.par][j], s.half() * 16)
            self.nc.vector.tensor_tensor(self.ysb[:, s.par, j], self.ps_y[j][:], self.x1[:, s.par, 2 * j:2 * j + 2], ALU.add)\
                .then_inc(self.y_taken, 1)

    def vector_unit(self, dve, s, i):
        if self.has(s):
            self.product(dve, s, i)
        if i and self.has(s):
            self.lower(dve, s, i - 1)
        if i == 0 and self.has(s.plus(-1)):
            self.outputs(dve, s.plus(-1))
        if i == 2 and self.has(s):
            self.lower_rows(dve, s.plus(1))
        if i == 1 and s.at_least(1):
            self.norm(dve, s.plus(1))


def over_rounds(eng, pairs, tail, step):
    step(Batch(0, 0))
    step(Batch(0, 1))
    with eng.Fori(0, pairs) as i:
        step(Batch(i, 2))
        step(Batch(i, 3))
    for s in range(2 + 2 * pairs, 2 + 2 * pairs + tail):
        step(Batch(0, s))


def route_stage(nc, ctx, sbt, x1_d, xall, ones, mv2, eps, rstd2, logits, gws, gwb, pos, wgt, slot_e):
    def sb(name, shape, dt=F32):
        return sbt(ctx, name, shape, dt)

    def sem(name):
        return nc.alloc_semaphore(name)

    rr = sb("rr", [P, NT])
    v3 = sb("v3", [P, NT])
    lower = sb("lower", [P, P])
    sgb = sb("sgb", [P, 2, NE])
    a = sb("ra", [P, NT, NE])
    b = sb("rb", [P, NT, NE])
    prob = sb("prob", [P, NT, NE])
    oh = [sb(f"oh{r}", [P, NT, NE]) for r in range(2)]
    rank = sb("rank", [P, NT, NE])
    m1 = sb("m1", [P, NT])
    m2 = sb("m2", [P, NT])
    cc = sb("cc", [P, NT])
    desc = sb("desc", [P, NE])
    one64 = sb("one64", [P, NT])
    tot = sb("tot", [P, NE])
    toti = sb("toti", [P, NE], I32)
    incl = sb("incl", [P, NE])
    base = sb("base", [P, NE])
    start = sb("start", [1, NSLOT])
    cmp_ = sb("cmp_", [1, NSLOT, NE])
    cnt = sb("cnt", [1, NSLOT])
    ps_s = ctx.enter_context(nc.psum_tensor("ps_s", [P, 2, NE], F32))
    ps_r = ctx.enter_context(nc.psum_tensor("ps_r", [P, NT, NE], F32))
    ps_n = ctx.enter_context(nc.psum_tensor("ps_n", [P, NT, NE], F32))

    filled = sem("filled")
    lower_ready = sem("lower_ready")
    iotas = sem("iotas")
    sums_ready = sem("sums_ready")
    chosen = sem("chosen")
    ranked = sem("ranked")
    chain = sem("chain")
    root = sem("root")
    v3_ready = sem("v3_ready")
    exp_in = sem("exp_in")
    exp_out = sem("exp_out")
    pos_ready = sem("pos_ready")
    x_loaded = sem("xa_loaded")
    block = ctx.enter_context(nc.Block())

    @block.tensor
    def _(pe):
        for c, w in enumerate((gws, gwb)):
            for k in range(KT):
                mm = nc.tensor.matmul(ps_s[:, c], ones[:], w[:, k], start=k == 0, stop=k == KT - 1)
        mm.then_inc(sums_ready, 1)
        pe.wait_ge(chosen, 1)
        pe.wait_ge(lower_ready, 1)
        nc.tensor.matmul(ps_r[:].rearrange("p t e -> p (t e)"), lower[:], rank[:].rearrange("p t e -> p (t e)"), start=True, stop=True)
        nc.tensor.matmul(ps_n[:].rearrange("p t e -> p (t e)"), ones[:], rank[:].rearrange("p t e -> p (t e)"), start=True, stop=True)\
            .then_inc(ranked, 1)

    @block.scalar
    def _(act):
        nc.scalar.activation(rstd2[:], mv2[:, :, 1], ACT.Sqrt, bias=eps[:, 0:1]).then_inc(root, 1)
        act.wait_ge(v3_ready, 1)
        nc.scalar.activation(rr[:], v3[:], ACT.Sqrt, bias=eps[:, 0:1]).then_inc(root, 1)
        act.wait_ge(exp_in, 1)
        nc.scalar.activation(prob[:], a[:], ACT.Exp).then_inc(exp_out, 1)

    @block.gpsimd
    def _(pool):
        nc.gpsimd.memset(lower[:], 1.0).then_inc(filled, 1)
        pool.wait_ge(filled, 1)
        nc.gpsimd.affine_select(out=lower[:], in_=lower[:], compare_op=ALU.is_gt, fill=0.0, base=0,
                                pattern=[[1, P]], channel_multiplier=-1).then_inc(lower_ready, 1)
        nc.gpsimd.iota(desc[:], pattern=[[-1, NE]], base=NE, channel_multiplier=0,
                       allow_small_or_imprecise_dtypes=True).then_inc(iotas, 1)
        nc.gpsimd.iota(start[:], pattern=[[P, NSLOT]], base=0, channel_multiplier=0,
                       allow_small_or_imprecise_dtypes=True).then_inc(iotas, 1)

    @block.sync
    def _(sp):
        x1_v = x1_d.rearrange("b p t d -> p b t d")
        n = NB // 4
        for c in range(4):
            sp.dma_start(xall[:, c * n * TT:(c + 1) * n * TT].rearrange("p (b t) d -> p b t d", t=TT), x1_v[:, c * n:(c + 1) * n])\
                .then_inc(x_loaded, 16)
        sp.wait_ge(x_loaded, 4 * 16)

    @block.vector
    def _(dve):
        n = [0]

        def then(ins):
            n[0] += 1
            ins.then_inc(chain, 1)
            dve.wait_ge(chain, n[0])

        def over_e(ap):
            return ap.unsqueeze(2).to_broadcast([P, NT, NE])

        def over_t(ap):
            return ap.unsqueeze(1).to_broadcast([P, NT, NE])

        def tt(o, x, y, op):
            return nc.vector.tensor_tensor(o, x, y, op)

        dve.wait_ge(root, 1)
        then(nc.vector.reciprocal(rstd2[:], rstd2[:]))
        then(tt(v3[:], mv2[:, :, 1], rstd2[:], ALU.mult))
        tt(v3[:], v3[:], rstd2[:], ALU.mult).then_inc(v3_ready, 1)
        dve.wait_ge(root, 2)
        then(nc.vector.reciprocal(rr[:], rr[:]))
        then(tt(rr[:], rr[:], rstd2[:], ALU.mult))
        dve.wait_ge(sums_ready, 1)
        then(nc.vector.tensor_copy(sgb[:], ps_s[:]))
        then(nc.vector.memset(one64[:], 1.0))
        then(nc.vector.tensor_copy(m1[:], mv2[:, :, 0]))
        then(tt(a[:], over_e(m1[:]), over_t(sgb[:, 0]), ALU.mult))
        then(tt(a[:], logits[:], a[:], ALU.subtract))
        then(tt(a[:], a[:], over_e(rr[:]), ALU.mult))
        then(tt(a[:], a[:], over_t(sgb[:, 1]), ALU.add))
        then(nc.vector.tensor_reduce(m1[:], a[:], AX.X, ALU.max))
        tt(a[:], a[:], over_e(m1[:]), ALU.subtract).then_inc(exp_in, 1)
        dve.wait_ge(exp_out, 1)
        then(nc.vector.tensor_reduce(m1[:], prob[:], AX.X, ALU.add))
        then(nc.vector.reciprocal(m1[:], m1[:]))
        then(tt(prob[:], prob[:], over_e(m1[:]), ALU.mult))
        dve.wait_ge(iotas, 2)

        def choose(p, best, onehot):
            then(nc.vector.tensor_reduce(best[:], p[:], AX.X, ALU.max))
            then(tt(a[:], p[:], over_e(best[:]), ALU.is_equal))
            then(tt(a[:], a[:], over_t(desc[:]), ALU.mult))
            then(nc.vector.tensor_reduce(cc[:], a[:], AX.X, ALU.max))
            then(tt(onehot[:], over_t(desc[:]), over_e(cc[:]), ALU.is_equal))

        choose(prob, m1, oh[0])
        then(nc.vector.scalar_tensor_tensor(out=b[:], in0=oh[0][:], scalar=-2.0, in1=prob[:], op0=ALU.mult, op1=ALU.add))
        choose(b, m2, oh[1])
        then(tt(cc[:], m1[:], m2[:], ALU.add))
        then(nc.vector.tensor_scalar(cc[:], cc[:], EPS, None, ALU.add))
        then(nc.vector.reciprocal(cc[:], cc[:]))
        then(tt(wgt[0][:], m1[:], cc[:], ALU.mult))
        then(tt(wgt[1][:], m2[:], cc[:], ALU.mult))
        tt(rank[:], oh[0][:], oh[1][:], ALU.add).then_inc(chosen, 1)
        dve.wait_ge(ranked, 1)
        then(nc.vector.tensor_copy(b[:], ps_n[:]))
        for e in range(NE):
            s_ = nc.vector.tensor_tensor_scan(a[:, :, e], one64[:], b[:, :, e], 0.0, ALU.mult, ALU.add)
        then(s_)
        then(nc.vector.tensor_copy(tot[:], a[:, NT - 1]))
        then(tt(a[:], a[:], b[:], ALU.subtract))
        then(tt(rank[:], a[:], ps_r[:], ALU.add))
        then(nc.vector.tensor_scalar(toti[:], tot[:], float(P - 1), None, ALU.add))
        then(nc.vector.tensor_scalar(toti[:], toti[:], 7, None, ALU.arith_shift_right))
        then(nc.vector.tensor_copy(tot[:], toti[:]))
        then(nc.vector.tensor_scalar(tot[:], tot[:], float(P), None, ALU.mult))
        then(nc.vector.tensor_tensor_scan(incl[:], one64[:, 0:NE], tot[:], 0.0, ALU.mult, ALU.add))
        then(tt(base[:], incl[:], tot[:], ALU.subtract))
        then(tt(rank[:], rank[:], over_t(base[:]), ALU.add))
        for r in range(2):
            then(tt(a[:], rank[:], oh[r][:], ALU.mult))
            then(nc.vector.tensor_reduce(cc[:], a[:], AX.X, ALU.add))
            nc.vector.tensor_copy(pos[:, :, r], cc[:]).then_inc(pos_ready, 1)
            dve.wait_ge(pos_ready, r + 1)
        then(tt(cmp_[:], start[:].unsqueeze(2).to_broadcast([1, NSLOT, NE]),
                incl[0:1].unsqueeze(1).to_broadcast([1, NSLOT, NE]), ALU.is_ge))
        then(nc.vector.tensor_reduce(cnt[:], cmp_[:], AX.X, ALU.add))
        then(nc.vector.tensor_scalar(slot_e[:], cnt[:], float(NE - 1), None, ALU.min))


def scatter_stage(nc, ctx, sbt, shared_weights, x1_d, xall, ys_d, xs_d, ident, mv2, rstd2, pos):
    FIRST, RING = SHARED_FIRST, 2 * TT
    idx = [sbt(ctx, f"idx{q}", [P, 2], I32) for q in range(RING)]
    row = [sbt(ctx, f"row{q}", [P, D]) for q in range(RING)]
    staged = ctx.enter_context(nc.semaphore("staged"))
    normed = ctx.enter_context(nc.semaphore("normed"))
    scattered = [ctx.enter_context(nc.semaphore(f"scattered{q}")) for q in range(RING)]
    se = SharedExpert(nc, ctx, sbt, "_1", 0, FIRST, shared_weights, x1_d, ys_d, ident, mv2, rstd2)
    block = ctx.enter_context(nc.Block())

    def rounds(eng, step):
        pairs = (FIRST - 4) // 2
        over_rounds(eng, pairs, FIRST - 1 - 2 * pairs, step)

    @block.sync
    def _(sp):
        se.load_in(sp, Batch(0, 0))
        se.load_weights(sp)
        se.load_in(sp, Batch(0, 1))
        se.load(sp, Batch(0, 0))
        se.load(sp, Batch(0, 1))
        se.load_in(sp, Batch(0, 2))

        def step(s):
            se.store(sp, s.plus(-1))
            if s.at_least(1):
                se.load(sp, s.plus(1))
                if s.at_most(FIRST - 3):
                    se.load_in(sp, s.plus(2))

        rounds(sp, step)
        for r in range(2):
            for j in range(2):
                sp.wait_ge(se.y_stored[r][j], (FIRST + 1 - r) // 2 * 16)

    @block.tensor
    def _(pe):
        se.transposes(pe, Batch(0, 0))
        pe.wait_ge(se.w_lo, 3)
        rounds(pe, lambda s: se.tensor_round(pe, s))

    @block.scalar
    def _(act):
        se.split_weights_hi(act)
        se.copies(act, Batch(0, 0))
        rounds(act, lambda s: se.scalar_round(act, s))

    @block.vector
    def _(dve):
        se.norm(dve, Batch(0, 0))
        se.split_weights_lo(dve)
        se.lower_rows(dve, Batch(0, 0))
        se.norm(dve, Batch(0, 1))

        def norm_tile(s, c):
            at = s.v * 2 * TT + c
            k = slice(at, at + 1) if s.fixed else bass.ds(at, 1)
            tile = xall[:, at] if s.fixed else xall[:, k].rearrange("p o e -> p (o e)")
            mean = mv2[:, at, 0:1] if s.fixed else mv2[:, k, 0]
            if s.at_least(1) or c >= RING:
                dve.wait_ge(scattered[c % RING], (s.v * 2 * TT // RING + c // RING if s.fixed else s.v * (2 * TT // RING) + c // RING) * 32)
            nc.vector.tensor_scalar(row[c % RING][:], tile, mean, rstd2[:, k], ALU.subtract, ALU.mult).then_inc(normed, 1)

        def step(s):
            for i in range(IT):
                if s.at_most(NB // 2 - 1):
                    norm_tile(s, 2 * i)
                    norm_tile(s, 2 * i + 1)
                se.vector_unit(dve, s, i)
            if se.has(s):
                se.lower(dve, s, IT - 1)

        rounds(dve, step)

    @block.gpsimd
    def _(pool):
        def stage(t, q, n):
            if n is not None:
                pool.wait_ge(scattered[q], n * 32)
            if n is not None or q > 0:
                pool.wait_ge(normed, t)
                pool.wait_ge(staged, t)
            one = pos[:, t] if isinstance(t, int) else pos[:, bass.ds(t, 1)].rearrange("p o e -> p (o e)")
            nc.gpsimd.tensor_copy(idx[q][:], one).then_inc(staged, 1)

        def scatter(q):
            for r in range(2):
                nc.gpsimd.indirect_dma_start(xs_d[:, :], bass.IndirectOffsetOnAxis(ap=idx[q][:, r:r + 1], axis=0),
                                             row[q][:], None).then_inc(scattered[q], 16)

        stage(0, 0, None)
        for q in range(1, RING):
            stage(q, q, None)
            scatter(q - 1)
        with pool.Fori(1, NT // RING) as i:
            for q in range(RING):
                stage(i * RING + q, q, i)
                scatter((q - 1) % RING)
        pool.wait_ge(normed, NT)
        pool.wait_ge(staged, NT)
        scatter(RING - 1)
        for q in range(RING):
            pool.wait_ge(scattered[q], NT // RING * 32)


def expert_stage(nc, ctx, sbt, Wg, Wu, Wd, xs_d, yo_d, ident, slot_e):
    def sb(name, shape, dt=F32):
        return sbt(ctx, name, shape, dt)

    def sem(name):
        return ctx.enter_context(nc.semaphore(name))

    GU = KT * INTER
    w_hi = sb("w_hi", [P, NE, 3, GU], F32R)
    w_lo = sb("w_lo", [P, NE, 3, GU], BF16)
    w_in = sb("w_in", [P, 3, GU])
    xr = sb("xr", [P, 2, D])
    x_hi = sb("x_hi", [P, 2, KT, P], F32R)
    x_lo = sb("x_lo", [P, 2, KT, P], F32R)
    x_bf = sb("x_bf", [P, 2, KT, P], BF16)
    sg = sb("sg_e", [P, 2, INTER])
    h = sb("h_e", [P, 2, INTER])
    h_hi = sb("h_hi", [P, 2, IT, P], F32R)
    h_lo = sb("h_lo", [P, 2, IT, P], F32R)
    h_bf = sb("h_bf", [P, 2, IT, P], BF16)
    y = sb("y_e", [P, 2, D])
    ps_x = ctx.enter_context(nc.psum_tensor("ps_x", [P, KT, P], F32))
    ps_g = ctx.enter_context(nc.psum_tensor("ps_ge", [P, INTER], F32))
    ps_u = ctx.enter_context(nc.psum_tensor("ps_ue", [P, INTER], F32))
    ps_h = ctx.enter_context(nc.psum_tensor("ps_h", [P, IT, P], F32))
    ps_y = [ctx.enter_context(nc.psum_tensor(f"ps_ye{r}", [P, D], F32)) for r in range(2)]

    PARTS = 6
    w_loaded = sem("we_loaded")
    w_ready = sem("we_ready")
    w0_hi = sem("w0_hi")
    p_hi = sem("p_hi")
    x_loaded = [sem(f"xe_loaded{r}") for r in range(2)]
    tx_ready = sem("tx_ready")
    xh_ready = sem("xh_ready")
    xb_ready = sem("xb_ready")
    xl_ready = sem("xl_ready")
    g_ready = sem("ge_ready")
    sg_ready = sem("sge_ready")
    u_ready = sem("ue_ready")
    h_ready = sem("he_ready")
    th_ready = sem("th_ready")
    hh_ready = sem("hh_ready")
    hb_ready = sem("hb_ready")
    hl_ready = sem("hl_ready")
    y_ready = sem("ye_ready")
    y_taken = sem("ye_taken")
    y_stored = [sem(f"ye_stored{r}") for r in range(2)]
    block = ctx.enter_context(nc.Block())

    xs_v = xs_d.rearrange("(s p) d -> s p d", p=P)
    yo_v = yo_d.rearrange("(s p) d -> s p d", p=P)

    def over_slots(eng, step):
        for s in range(3):
            step(Batch(0, s))
        with eng.Fori(0, (NSLOT - 5) // 2) as i:
            step(Batch(i, 3))
            step(Batch(i, 4))
        for s in range(NSLOT - 2, NSLOT + 2):
            step(Batch(0, s))

    def exists(s):
        return s.at_least(0) and s.at_most(NSLOT - 1)

    def rows_of(view, s):
        return view[s.off] if s.fixed else view[bass.ds(s.v, 1)].rearrange("o p d -> (o p) d")

    @block.sync
    def _(sp):
        for r in range(2):
            sp.dma_start(xr[:, r], xs_v[r]).then_inc(x_loaded[r], 16)

        def step(s):
            if exists(s) and s.at_most(NSLOT - 3):
                sp.wait_ge(tx_ready, s.v + 1)
                sp.nop(nofuse=True)
                sp.dma_start(xr[:, s.par], rows_of(xs_v, s.plus(2))).then_inc(x_loaded[s.par], 16)
            if exists(s.plus(-2)):
                d = s.plus(-2)
                sp.wait_ge(y_taken, d.v + 1)
                sp.nop(nofuse=True)
                sp.dma_start(rows_of(yo_v, d), y[:, d.par]).then_inc(y_stored[d.par], 16)

        over_slots(sp, step)
        for r in range(2):
            sp.wait_ge(y_stored[r], (NSLOT + 1 - r) // 2 * 16)

    @block.gpsimd
    def _(pool):
        def load(e):
            for m, src in enumerate((Wg, Wu, Wd)):
                pool.dma_start(w_in[:, m].rearrange("p (k n) -> p k n", k=KT if m < 2 else IT),
                               src[e].rearrange("(k p) n -> p k n", p=P)).then_inc(w_loaded, 16)

        load(0)
        for e in range(1, NE):
            pool.wait_ge(w_ready, e * PARTS)
            load(e)
            pool.wait_ge(w_loaded, (e + 1) * 3 * 16)
            for m in range(3):
                nc.gpsimd.tensor_copy(w_hi[:, e, m], w_in[:, m]).then_inc(p_hi, 1)
            pool.wait_ge(p_hi, e * 3)
            for m in range(3):
                nc.gpsimd.tensor_tensor(w_lo[:, e, m], w_in[:, m], w_hi[:, e, m].bitcast(F32), ALU.subtract)\
                    .then_inc(w_ready, 2)

    @block.tensor
    def _(pe):
        def expert(s):
            at = slot_e[0:1, s.off:s.off + 1] if s.fixed else slot_e[0:1, bass.ds(s.v, 1)]
            return pe.value_load(at, min_val=0, max_val=NE - 1)

        def product(bank, n, hi, lo, bf, m, e, ready, count):
            width = GU // n
            w = [t[:, bass.ds(e, 1), m].rearrange("p o n -> p (o n)") for t in (w_hi, w_lo)]
            for at, (part, side) in enumerate(((hi, 0), (bf, 1), (lo, 0))):
                if ready:
                    pe.wait_ge(ready[at], count)
                for k in range(n):
                    mm = nc.tensor.matmul(bank, part[:, k], w[side][:, k * width:(k + 1) * width],
                                          start=at == 0 and k == 0, stop=at == 2 and k == n - 1)
            return mm

        def turn_rows(s):
            pe.wait_ge(x_loaded[s.par], (s.half() + 1) * 16)
            if s.at_least(1):
                for taken_by in (xh_ready, xl_ready):
                    pe.wait_ge(taken_by, s.v)
            for k in range(KT):
                mm = nc.tensor.transpose(ps_x[:, k], xr[:, s.par, k * P:(k + 1) * P], ident[:])
            mm.then_inc(tx_ready, 1)

        def gate(s, e):
            pe.wait_ge(w_ready, e * PARTS + PARTS)
            if s.at_least(1):
                pe.wait_ge(sg_ready, s.v)
            product(ps_g[:], KT, x_hi[:, s.par], x_lo[:, s.par], x_bf[:, s.par], 0, e,
                    (xh_ready, xb_ready, xl_ready), s.v + 1).then_inc(g_ready, 1)

        def up(s, e):
            if s.at_least(1):
                pe.wait_ge(h_ready, s.v)
            product(ps_u[:], KT, x_hi[:, s.par], x_lo[:, s.par], x_bf[:, s.par], 1, e, None, 0).then_inc(u_ready, 1)

        def turn_hidden(s):
            pe.wait_ge(h_ready, s.v + 1)
            if s.at_least(1):
                for taken_by in (hh_ready, hl_ready):
                    pe.wait_ge(taken_by, s.v)
            for k in range(IT):
                mm = nc.tensor.transpose(ps_h[:, k], h[:, s.par, k * P:(k + 1) * P], ident[:])
            mm.then_inc(th_ready, 1)

        def down(s, e):
            if s.at_least(2):
                pe.wait_ge(y_taken, s.v - 1)
            product(ps_y[s.par][:], IT, h_hi[:, s.par], h_lo[:, s.par], h_bf[:, s.par], 2, e,
                    (hh_ready, hb_ready, hl_ready), s.v + 1).then_inc(y_ready, 1)

        def step(s):
            if exists(s):
                e = expert(s)
                gate(s, e)
            if exists(s.plus(-2)):
                e_down = expert(s.plus(-2))
            if exists(s.plus(-1)):
                turn_hidden(s.plus(-1))
            if exists(s.plus(-2)):
                down(s.plus(-2), e_down)
            if s.at_most(NSLOT - 2):
                turn_rows(s.plus(1))
            if exists(s):
                up(s, e)

        turn_rows(Batch(0, 0))
        over_slots(pe, step)

    @block.scalar
    def _(act):
        def take_rows(s):
            act.wait_ge(tx_ready, s.v + 1)
            if s.at_least(2):
                act.wait_ge(u_ready, s.v - 1)
            nc.scalar.activation(x_hi[:, s.par], ps_x[:], ACT.Copy).then_inc(xh_ready, 1)
            act.wait_ge(xh_ready, s.v + 1)
            nc.scalar.activation(x_bf[:, s.par], x_hi[:, s.par].bitcast(F32), ACT.Copy).then_inc(xb_ready, 1)

        def step(s):
            if exists(s):
                act.wait_ge(g_ready, s.v + 1)
                if s.at_least(2):
                    act.wait_ge(h_ready, s.v - 1)
                nc.scalar.activation(sg[:, s.par], ps_g[:], ACT.Silu).then_inc(sg_ready, 1)
            if exists(s.plus(-1)):
                d = s.plus(-1)
                act.wait_ge(th_ready, d.v + 1)
                if d.at_least(2):
                    act.wait_ge(y_ready, d.v - 1)
                nc.scalar.activation(h_hi[:, d.par], ps_h[:], ACT.Copy).then_inc(hh_ready, 1)
                act.wait_ge(hh_ready, d.v + 1)
                nc.scalar.activation(h_bf[:, d.par], h_hi[:, d.par].bitcast(F32), ACT.Copy).then_inc(hb_ready, 1)
            if s.at_most(NSLOT - 2):
                take_rows(s.plus(1))

        act.wait_ge(w_loaded, 3 * 16)
        for m in range(3):
            nc.scalar.activation(w_hi[:, 0, m], w_in[:, m], ACT.Copy).then_inc(w0_hi, 1)
        take_rows(Batch(0, 0))
        over_slots(act, step)

    @block.vector
    def _(dve):
        def take_rows(s):
            dve.wait_ge(xh_ready, s.v + 1)
            if s.at_least(2):
                dve.wait_ge(u_ready, s.v - 1)
            nc.vector.tensor_tensor(x_lo[:, s.par], ps_x[:], x_hi[:, s.par].bitcast(F32), ALU.subtract).then_inc(xl_ready, 1)

        def step(s):
            if exists(s.plus(-1)):
                d = s.plus(-1)
                dve.wait_ge(hh_ready, d.v + 1)
                if d.at_least(2):
                    dve.wait_ge(y_ready, d.v - 1)
                nc.vector.tensor_tensor(h_lo[:, d.par], ps_h[:], h_hi[:, d.par].bitcast(F32), ALU.subtract).then_inc(hl_ready, 1)
            if exists(s.plus(-2)):
                d = s.plus(-2)
                dve.wait_ge(y_ready, d.v + 1)
                if d.at_least(2):
                    dve.wait_ge(y_stored[d.par], d.half() * 16)
                nc.vector.tensor_copy(y[:, d.par], ps_y[d.par][:]).then_inc(y_taken, 1)
            if s.at_most(NSLOT - 2):
                take_rows(s.plus(1))
            if exists(s):
                dve.wait_ge(u_ready, s.v + 1)
                dve.wait_ge(sg_ready, s.v + 1)
                if s.at_least(2):
                    dve.wait_ge(th_ready, s.v - 1)
                nc.vector.tensor_tensor(h[:, s.par], sg[:, s.par], ps_u[:], ALU.mult).then_inc(h_ready, 1)

        for m in range(3):
            dve.wait_ge(w0_hi, m + 1)
            nc.vector.tensor_tensor(w_lo[:, 0, m], w_in[:, m], w_hi[:, 0, m].bitcast(F32), ALU.subtract).then_inc(w_ready, 2)
        take_rows(Batch(0, 0))
        over_slots(dve, step)


def combine_stage(nc, ctx, sbt, shared_weights, x1_d, yo_d, ys_d, out, ident, mv2, rstd2, pos, wgt):
    def sem(name):
        return ctx.enter_context(nc.semaphore(name))

    BASE = SHARED_FIRST
    ROUNDS = NB // 2
    acc = sbt(ctx, "acc", [P, 2, 2 * TT, D])
    yr = [[sbt(ctx, f"yr{q}{r}", [P, D]) for r in range(2)] for q in range(2 * TT)]
    ix = [sbt(ctx, f"ix{q}", [P, 2], I32) for q in range(2 * TT)]
    acc_loaded = [sem(f"acc_loaded{r}") for r in range(2)]
    stored = [sem(f"stored{r}") for r in range(2)]
    staged = sem("ix_staged")
    gathered = [sem(f"gathered{q}") for q in range(2 * TT)]
    half_done = sem("half_done")
    tile_done = sem("tile_done")
    se = SharedExpert(nc, ctx, sbt, "_2", BASE, NB - BASE, shared_weights, x1_d, ys_d, ident, mv2, rstd2)
    block = ctx.enter_context(nc.Block())
    ys_v = ys_d.rearrange("(r t) p d -> r p t d", t=2 * TT)
    out_v = out.rearrange("b s d -> (b s) d").rearrange("(r t p) d -> r p t d", p=P, t=2 * TT)

    def round_of(view, s):
        return view[s.off] if s.fixed else view[bass.ds(s.v, 1)].rearrange("o p t d -> (o p) t d")

    def rounds(eng, step):
        over_rounds(eng, (NB - BASE - 4) // 2, ROUNDS - 2 - (NB - BASE - 4) // 2 * 2, step)

    @block.sync
    def _(sp):
        def load_acc(s):
            if s.at_least(2):
                sp.wait_ge(stored[s.par], s.half() * 16)
                sp.nop(nofuse=True)
                last = s.fixed and s.off == ROUNDS - 1
                for r in range(2):
                    stored_r = (NB - BASE + 1 - r) // 2 if last else s.half() - (1 if r > s.par else 0)
                    if last or not s.fixed or stored_r > 0:
                        for j in range(2):
                            sp.wait_ge(se.y_stored[r][j], stored_r * 16)
                            sp.nop(nofuse=True)
            sp.dma_start(acc[:, s.par], round_of(ys_v, s)).then_inc(acc_loaded[s.par], 16)

        se.load_in(sp, Batch(0, 0))
        se.load_weights(sp)
        se.load_in(sp, Batch(0, 1))
        se.load(sp, Batch(0, 0))
        se.load(sp, Batch(0, 1))
        se.load_in(sp, Batch(0, 2))
        load_acc(Batch(0, 0))

        def step(s):
            se.store(sp, s.plus(-1))
            if s.at_least(1):
                se.load(sp, s.plus(1))
                if s.at_most(NB - BASE - 3):
                    se.load_in(sp, s.plus(2))
            if s.at_most(ROUNDS - 3):
                load_acc(s.plus(1))
            if s.fixed and s.off == ROUNDS - 1:
                load_acc(s)
            sp.wait_ge(tile_done, (s.v + 1) * 2 * TT)
            sp.nop(nofuse=True)
            sp.dma_start(round_of(out_v, s), acc[:, s.par]).then_inc(stored[s.par], 16)

        rounds(sp, step)
        for r in range(2):
            sp.wait_ge(stored[r], ROUNDS // 2 * 16)

    @block.tensor
    def _(pe):
        se.transposes(pe, Batch(0, 0))
        pe.wait_ge(se.w_lo, 3)
        rounds(pe, lambda s: se.tensor_round(pe, s))

    @block.scalar
    def _(act):
        se.split_weights_hi(act)
        se.copies(act, Batch(0, 0))
        rounds(act, lambda s: se.scalar_round(act, s))

    @block.gpsimd
    def _(pool):
        def stage(s, c):
            if s.at_least(1):
                pool.wait_ge(tile_done, (s.v - 1) * (2 * TT) + c + 1)
            if c > 0 or s.at_least(1):
                pool.wait_ge(staged, s.v * (2 * TT) + c)
            at = s.v * (2 * TT) + c
            src = pos[:, at] if s.fixed else pos[:, bass.ds(at, 1)].rearrange("p o r -> p (o r)")
            nc.gpsimd.tensor_copy(ix[c][:], src).then_inc(staged, 1)

        def gather(c):
            for r in range(2):
                nc.gpsimd.indirect_dma_start(yr[c][r][:], None, yo_d[:, :],
                                             bass.IndirectOffsetOnAxis(ap=ix[c][:, r:r + 1], axis=0))\
                    .then_inc(gathered[c], 16)

        def step(s):
            for c in range(2 * TT):
                stage(s, c)
                if not (s.fixed and s.off == 0 and c == 0):
                    gather((c - 1) % (2 * TT))

        over_rounds(pool, ROUNDS // 2 - 1, 0, step)
        pool.wait_ge(staged, NT)
        gather(2 * TT - 1)

    @block.vector
    def _(dve):
        def add_tile(s, c):
            dve.wait_ge(gathered[c], s.v * 32 + 32)
            at = s.v * (2 * TT) + c
            k = slice(at, at + 1) if s.fixed else bass.ds(at, 1)
            nc.vector.scalar_tensor_tensor(out=acc[:, s.par, c], in0=yr[c][0][:], scalar=wgt[0][:, k],
                                           in1=acc[:, s.par, c], op0=ALU.mult, op1=ALU.add).then_inc(half_done, 1)
            dve.wait_ge(half_done, at + 1)
            nc.vector.scalar_tensor_tensor(out=acc[:, s.par, c], in0=yr[c][1][:], scalar=wgt[1][:, k],
                                           in1=acc[:, s.par, c], op0=ALU.mult, op1=ALU.add).then_inc(tile_done, 1)

        se.norm(dve, Batch(0, 0))
        se.split_weights_lo(dve)
        se.lower_rows(dve, Batch(0, 0))
        se.norm(dve, Batch(0, 1))

        def step(s):
            for i in range(IT):
                se.vector_unit(dve, s, i)
                if i == 0:
                    dve.wait_ge(acc_loaded[s.par], (s.half() + 1) * 16)
                if i == IT - 1 and se.has(s):
                    se.lower(dve, s, i)
                add_tile(s, 2 * i)
                add_tile(s, 2 * i + 1)

        rounds(dve, step)


def kernel(**inputs):
    import numpy as _np
    import concourse.bacc as _bacc
    from concourse import mybir as _mybir
    from concourse.bass_utils import run_bass_kernel_spmd as _run

    ins = ["L0_attn_x", "L0_attn_Wq", "L0_attn_bq", "L0_attn_Wk", "L0_attn_bk", "L0_attn_Wv", "L0_attn_bv",
           "L0_attn_Wo", "L0_attn_bo", "L0_attn_J_attn", "L0_attn_lambda_attn", "L0_ffn_ln_scale", "L0_ffn_ln_bias",
           "L0_ffn_gate_w", "L0_ffn_Wg", "L0_ffn_Wu", "L0_ffn_Wd", "L0_ffn_sWg", "L0_ffn_sWu", "L0_ffn_sWd"]
    turned = {"L0_attn_Wq", "L0_attn_Wk", "L0_attn_Wv", "L0_attn_Wo", "L0_ffn_gate_w"}
    nc = _bacc.Bacc("TRN2", target_bir_lowering=False, num_devices=1)
    arrays, args = {}, []
    for name in ins:
        a = _np.asarray(inputs[name])
        if name in turned:
            a = a.T
        if a.ndim == 0:
            a = a.reshape(1)
        a = _np.ascontiguousarray(a)
        arrays[f"in_{name}_dram"] = a
        args.append(nc.dram_tensor(f"in_{name}_dram", a.shape, _mybir.dt.from_np(a.dtype), kind="ExternalInput").ap())
    args.append(nc.dram_tensor("out_0_dram", (NB, S, D), F32, kind="ExternalOutput").ap())
    build(nc, *args)
    r = _run(nc, [arrays], core_ids=[0])
    return r.results[0]["out_0_dram"]
```
